# Optimizing a Trainium2 kernel written in Bass

```python
import numpy as np
import jax
import jax.numpy as jnp

def _softmax(x, axis=-1):
    return jax.nn.softmax(x, axis=axis)

def _gelu(x):
    return jax.nn.gelu(x, approximate=True)

def _silu(x):
    return jax.nn.silu(x)

def _sigmoid(x):
    return jax.nn.sigmoid(x)

def _layernorm(x, axis=-1, eps=1e-05):
    m = jnp.mean(x, axis=axis, keepdims=True)
    v = jnp.var(x, axis=axis, keepdims=True)
    return (x - m) / jnp.sqrt(v + eps)

def _scatter_add(tgt, idx, src, axis=0):
    return tgt.at[idx].add(src)

def _segment_sum(src, seg, n):
    return jax.ops.segment_sum(src, seg, n)
kernel_name = 'mk_macaron_d2_jaxref_r8_859950'

def setup_inputs(seed: int=0):
    np.random.seed(seed)
    _w = jnp.asarray

    def _L0_attn_setup():
        import jax, jax.numpy as jnp
        import numpy as np
        BH = 32
        BW = 32
        key = jax.random.key(seed)
        k1, k2, k3, k4 = jax.random.split(key, 4)
        B, S, K, N = (2, 256, 512, 512)
        data = jax.random.normal(k1, (B, S, K), dtype=jnp.float32)
        weight = jax.random.normal(k2, (N, K), dtype=jnp.float32) * 0.02
        bias = jax.random.normal(k3, (N,), dtype=jnp.float32) * 0.02
        Nb, Kb = (N // BH, K // BW)
        block_on = jax.random.uniform(k4, (Nb, Kb)) < 0.3
        mask = jnp.repeat(jnp.repeat(block_on, BH, axis=0), BW, axis=1).astype(jnp.int32)
        return {'data': data, 'mask': mask, 'weight': weight, 'bias': bias}
    _L0_attn_in = _L0_attn_setup()

    def _L0_ffn_setup():
        import jax, jax.numpy as jnp
        import numpy as np
        NUM_EXPERTS = 8
        TOP_K = 2
        RANK = 16
        LORA_ALPHA = 32
        SCALING = LORA_ALPHA / RANK
        key = jax.random.key(seed)
        ks = jax.random.split(key, 6)
        B, S, D_IN, D_OUT = (4, 256, 512, 512)
        x = jax.random.normal(ks[0], (B, S, D_IN), dtype=jnp.float32)
        W_base = jax.random.normal(ks[1], (D_OUT, D_IN), dtype=jnp.float32) * 0.02
        b_base = jax.random.normal(ks[2], (D_OUT,), dtype=jnp.float32) * 0.02
        W_router = jax.random.normal(ks[3], (NUM_EXPERTS, D_IN), dtype=jnp.float32) * 0.02
        A = jax.random.normal(ks[4], (NUM_EXPERTS, RANK, D_IN), dtype=jnp.float32) * 0.02
        Bm = jax.random.normal(ks[5], (D_OUT, RANK), dtype=jnp.float32) * 0.02
        Bm = jnp.broadcast_to(Bm, (NUM_EXPERTS, D_OUT, RANK)) * jnp.arange(1, NUM_EXPERTS + 1, dtype=jnp.float32)[:, None, None] * 0.2
        return {'x': x, 'W_base': W_base, 'b_base': b_base, 'W_router': W_router, 'A': A, 'B': Bm}
    _L0_ffn_in = _L0_ffn_setup()

    def _L1_attn_setup():
        import jax, jax.numpy as jnp
        import numpy as np
        B, S, D = (2, 256, 512)
        H = 32
        HD = D // H
        THETA = 10000.0

        def _rope_cos_sin(seq_len, head_dim, theta=THETA):
            inv = 1.0 / theta ** (np.arange(0, head_dim, 2)[:head_dim // 2].astype(np.float32) / head_dim)
            t = np.arange(seq_len)
            f = np.outer(t, inv).astype(np.float32)
            return (jnp.asarray(np.cos(f)), jnp.asarray(np.sin(f)))

        def _apply_rotary(x, cos, sin):
            xr = x.astype(jnp.float32).reshape(*x.shape[:-1], HD // 2, 2)
            x0, x1 = (xr[..., 0], xr[..., 1])
            c = cos[None, :, None, :]
            s = sin[None, :, None, :]
            o0 = x0 * c - x1 * s
            o1 = x0 * s + x1 * c
            return jnp.stack((o0, o1), axis=-1).reshape(*x.shape[:-1], HD)
        key = jax.random.key(seed)
        ks = jax.random.split(key, 5)
        std = 0.02
        return {'x': jax.random.normal(ks[0], (B, S, D), dtype=jnp.float32), 'wq': jax.random.normal(ks[1], (D, D), dtype=jnp.float32) * std, 'wk': jax.random.normal(ks[2], (D, D), dtype=jnp.float32) * std, 'wv': jax.random.normal(ks[3], (D, D), dtype=jnp.float32) * std, 'wo': jax.random.normal(ks[4], (D, D), dtype=jnp.float32) * std}
    _L1_attn_in = _L1_attn_setup()

    def _L1_ffn_setup():
        import jax, jax.numpy as jnp
        import numpy as np
        B, S, DIN, DOUT = (2, 256, 512, 512)
        key = jax.random.key(seed)
        k1, k2 = jax.random.split(key)
        x = jax.random.normal(k1, (B, S, DIN), dtype=jnp.float32)
        weight = jax.random.normal(k2, (DOUT, DIN), dtype=jnp.float32) * 0.02
        mean = weight.mean(-1, keepdims=True)
        scale = jnp.abs(weight - mean).mean(-1, keepdims=True)
        wscale = scale
        wbias = mean
        return {'x': x, 'weight': weight, 'wscale': wscale, 'wbias': wbias}
    _L1_ffn_in = _L1_ffn_setup()
    _d = {'L0_attn_data': _L0_attn_in['data'], 'L0_attn_mask': _L0_attn_in['mask'], 'L0_attn_weight': _L0_attn_in['weight'], 'L0_attn_bias': _L0_attn_in['bias'], 'L0_ffn_W_base': _L0_ffn_in['W_base'], 'L0_ffn_b_base': _L0_ffn_in['b_base'], 'L0_ffn_W_router': _L0_ffn_in['W_router'], 'L0_ffn_A': _L0_ffn_in['A'], 'L0_ffn_B': _L0_ffn_in['B'], 'L1_attn_wq': _L1_attn_in['wq'], 'L1_attn_wk': _L1_attn_in['wk'], 'L1_attn_wv': _L1_attn_in['wv'], 'L1_attn_wo': _L1_attn_in['wo'], 'L1_ffn_weight': _L1_ffn_in['weight'], 'L1_ffn_wscale': _L1_ffn_in['wscale'], 'L1_ffn_wbias': _L1_ffn_in['wbias']}
    _x0 = _d['L0_attn_data']
    _d['L0_attn_data'] = jax.random.normal(jax.random.fold_in(jax.random.key(seed), 1), (2, 1024, 512), dtype=_x0.dtype)
    del _x0
    return _d

def reference(L0_attn_data, L0_attn_mask, L0_attn_weight, L0_attn_bias, L0_ffn_W_base, L0_ffn_b_base, L0_ffn_W_router, L0_ffn_A, L0_ffn_B, L1_attn_wq, L1_attn_wk, L1_attn_wv, L1_attn_wo, L1_ffn_weight, L1_ffn_wscale, L1_ffn_wbias):

    def _L0_attn_ref(data, mask, weight, bias):
        import jax, jax.numpy as jnp
        import numpy as np
        BH = 32
        BW = 32
        N, K = weight.shape
        Nb, Kb = (N // BH, K // BW)
        bm = mask.reshape(Nb, BH, Kb, BW).sum(axis=(1, 3)) > 0
        wb = weight.reshape(Nb, BH, Kb, BW) * bm[:, None, :, None].astype(weight.dtype)
        w = wb.reshape(N, K)
        out = jnp.einsum('bsk,nk->bsn', data, w) + bias
        return out

    def _L0_ffn_ref(x, W_base, b_base, W_router, A, B):
        import jax, jax.numpy as jnp
        import numpy as np
        NUM_EXPERTS = 8
        TOP_K = 2
        RANK = 16
        LORA_ALPHA = 32
        SCALING = LORA_ALPHA / RANK
        bs, seq, d_in = x.shape
        T = bs * seq
        xf = x.reshape(T, d_in)
        base = xf @ W_base.T + b_base
        logits = xf @ W_router.T
        rw, sel = jax.lax.top_k(logits, TOP_K)
        rw = jax.nn.softmax(rw, axis=-1)
        onehot = jax.nn.one_hot(sel, NUM_EXPERTS, dtype=rw.dtype)
        w = jnp.einsum('tk,tke->te', rw, onehot)
        h = jnp.einsum('td,erd->ter', xf, A)
        lora = jnp.einsum('ter,te,eor->to', h, w, B) * SCALING
        return (base + lora).reshape(bs, seq, -1)

    def _L1_attn_ref(x, wq, wk, wv, wo):
        import jax, jax.numpy as jnp
        import numpy as np
        B, S, D = (2, 256, 512)
        H = 32
        HD = D // H
        THETA = 10000.0

        def _rope_cos_sin(seq_len, head_dim, theta=THETA):
            inv = 1.0 / theta ** (np.arange(0, head_dim, 2)[:head_dim // 2].astype(np.float32) / head_dim)
            t = np.arange(seq_len)
            f = np.outer(t, inv).astype(np.float32)
            return (jnp.asarray(np.cos(f)), jnp.asarray(np.sin(f)))

        def _apply_rotary(x, cos, sin):
            xr = x.astype(jnp.float32).reshape(*x.shape[:-1], HD // 2, 2)
            x0, x1 = (xr[..., 0], xr[..., 1])
            c = cos[None, :, None, :]
            s = sin[None, :, None, :]
            o0 = x0 * c - x1 * s
            o1 = x0 * s + x1 * c
            return jnp.stack((o0, o1), axis=-1).reshape(*x.shape[:-1], HD)
        b, s, d = x.shape
        q = (x @ wq).reshape(b, s, H, HD)
        k = (x @ wk).reshape(b, s, H, HD)
        v = (x @ wv).reshape(b, s, H, HD)
        cos, sin = _rope_cos_sin(s, HD)
        q = _apply_rotary(q, cos, sin)
        k = _apply_rotary(k, cos, sin)
        scale = 1.0 / jnp.sqrt(jnp.float32(HD))
        scores = jnp.einsum('bqhd,bkhd->bhqk', q, k) * scale
        causal = jnp.tril(jnp.ones((s, s), dtype=bool))
        scores = jnp.where(causal[None, None], scores, jnp.finfo(scores.dtype).min)
        probs = jax.nn.softmax(scores, axis=-1)
        out = jnp.einsum('bhqk,bkhd->bqhd', probs, v).reshape(b, s, d)
        return out @ wo

    def _L1_ffn_ref(x, weight, wscale, wbias):
        import jax, jax.numpy as jnp
        import numpy as np
        B, S, DIN, DOUT = (2, 256, 512, 512)
        w_bin = jnp.sign(weight)
        w = wscale * w_bin + wbias
        out = jnp.einsum('bsk,nk->bsn', x, w)
        return out
    x = L0_attn_data
    x = x + 0.5 * _L0_ffn_ref(_layernorm(x, axis=-1), L0_ffn_W_base, L0_ffn_b_base, L0_ffn_W_router, L0_ffn_A, L0_ffn_B)
    x = x + _L0_attn_ref(_layernorm(x, axis=-1), L0_attn_mask, L0_attn_weight, L0_attn_bias)
    x = x + 0.5 * _L0_ffn_ref(_layernorm(x, axis=-1), L0_ffn_W_base, L0_ffn_b_base, L0_ffn_W_router, L0_ffn_A, L0_ffn_B)
    x = x + 0.5 * _L1_ffn_ref(_layernorm(x, axis=-1), L1_ffn_weight, L1_ffn_wscale, L1_ffn_wbias)
    x = x + _L1_attn_ref(_layernorm(x, axis=-1), L1_attn_wq, L1_attn_wk, L1_attn_wv, L1_attn_wo)
    x = x + 0.5 * _L1_ffn_ref(_layernorm(x, axis=-1), L1_ffn_weight, L1_ffn_wscale, L1_ffn_wbias)
    return x

_drawn_inputs = setup_inputs


def setup_inputs(seed=0):
    import zlib

    import numpy as np

    out = dict(_drawn_inputs(seed))
    spreads = {}
    factors = {'L0_attn_bias': 3.46,
     'L0_ffn_b_base': 3.541,
     'L1_attn_wq': 8.0,
     'L1_attn_wk': 8.0,
     'L1_attn_wv': 4.1,
     'L1_attn_wo': 4.04,
     'L1_ffn_wscale': 6.365,
     'L1_ffn_wbias': 8.0}
    for name, (base, spread) in spreads.items():
        noise = np.random.default_rng([zlib.crc32(name.encode()), seed]).standard_normal(out[name].shape)
        drawn = base * np.exp(spread * noise) if base else spread * noise
        out[name] = jnp.asarray(drawn.astype(out[name].dtype))
    for name, factor in factors.items():
        out[name] = (out[name] * factor).astype(out[name].dtype)
    return out
```

```python
from contextlib import ExitStack

import numpy as np

import concourse.bass as bass
from concourse import mybir

F32 = mybir.dt.float32
F32R = mybir.dt.float32r
BF16 = mybir.dt.bfloat16
I32 = mybir.dt.int32
U32 = mybir.dt.uint32
ALU = mybir.AluOpType
ACT = mybir.ActivationFunctionType
AX = mybir.AxisListType

P = 128
D = 512
KC = D // P
B, S = 2, 1024
TILES = B * S // P
E, RANK = 8, 16
ER = E * RANK
BLK = 32
NBLK = KC * D // BLK
EPS = 1e-5
LORA_SCALE = 2.0

LORA_FFN, SPARSE, BIN_FFN, OUT_PROJ = range(4)
BEFORE = (LORA_FFN, SPARSE, LORA_FFN, BIN_FFN)
RESIDUAL = {LORA_FFN: 0.5, SPARSE: 1.0, BIN_FFN: 0.5, OUT_PROJ: 1.0}
LEAD = 4


class Steps:

    def __init__(self, sem):
        self.sem, self.base, self.off = sem, 0, 0

    def step(self, ins):
        self.off += 1
        ins.then_inc(self.sem, 1)

    def wait(self, eng):
        at_least(eng, self.sem, self.base + self.off)

    def then_wait(self, eng, ins):
        self.step(ins)
        self.wait(eng)

    def enter(self, i, per):
        self.start = self.base + self.off
        self.per = per
        self.base, self.off = i * per + self.start, 0

    def leave(self, rounds):
        assert self.off == self.per, (self.off, self.per)
        self.base, self.off = self.start + rounds * self.per, 0


def over_tiles(eng, kinds, tile, steps=None, per=None):
    rounds = (TILES - LEAD) // 2 - 1
    for s in range(len(kinds)):
        for t in (0, 1):
            tile(s, t, s * TILES + t, t % 2)
        with eng.Fori(0, rounds) as i:
            if steps:
                steps.enter(i, per[kinds[s]])
            for p in (0, 1):
                tile(s, i * 2 + (2 + p), i * 2 + (s * TILES + 2 + p), p)
            if steps:
                steps.leave(rounds)
        for t in range(TILES - LEAD, TILES):
            tile(s, t, s * TILES + t, t % 2)


def neighbour(kinds, s, t, k):
    if not isinstance(t, int):
        return s, t + k
    n = s * TILES + t + k
    return (n // TILES, n % TILES) if 0 <= n < len(kinds) * TILES else None


def at_least(eng, sem, value):
    if not isinstance(value, int) or value > 0:
        eng.wait_ge(sem, value)


def prepare_weights(nc, ins, g):
    with ExitStack() as ctx:
        def sb(name, shape, dt=F32):
            return ctx.enter_context(nc.sbuf_tensor(name, shape, dt))

        def sem(name):
            return ctx.enter_context(nc.semaphore(name))

        nat = {k: sb(f"nat_{k}", [P, KC, D]) for k in (LORA_FFN, SPARSE, BIN_FFN)}
        mask = sb("mask_in", [P, KC, D], I32)
        block_sum = sb("block_sum", [P, NBLK])
        block_on = sb("block_on", [P, NBLK])
        same_block = sb("same_block_sb", [P, P])
        nat_a = sb("nat_a", [P, D])
        nat_router = sb("nat_router", [E, D])
        nat_b = sb("nat_b", [P, KC, E, RANK])
        wscale = sb("wscale", [P, KC])
        neg_wscale = sb("neg_wscale", [P, KC])
        wbias = sb("wbias", [P, KC])
        positive = sb("positive", [P, KC, D])
        bank = [ctx.enter_context(nc.psum_tensor(f"wbank{i}", [P, D], F32)) for i in range(6)]
        mask_bank = ctx.enter_context(nc.psum_tensor("mask_bank", [P, D], F32))
        small_bank = ctx.enter_context(nc.psum_tensor("small_bank", [P, KC, P], F32))

        s_const, s_base, s_lora, s_mask, s_bin = (sem(n) for n in (
            "const_loaded", "base_loaded", "lora_loaded", "mask_loaded", "bin_loaded"))
        s_x = sem("x_loaded")
        s_sums, s_onmap, s_nat = sem("mask_sums"), sem("mask_map"), sem("nat_ready")
        s_tr, s_hi, s_lo, s_small, s_small_out = (sem(n) for n in (
            "w_transposed", "w_hi", "w_lo", "lora_transposed", "lora_copied"))
        s_own = sem("prep_vector_own")
        block = ctx.enter_context(nc.Block())
        order = (LORA_FFN, SPARSE, BIN_FFN)

        @block.sync
        def _(sp):
            sp.dma_start(g.ident[:], ins["ident"]).then_inc(s_const, 16)
            sp.dma_start(nat[LORA_FFN][:], ins["L0_ffn_W_base"].rearrange("(c p) k -> p c k", p=P)).then_inc(s_base, 16)
            x = ins["L0_attn_data"].rearrange("b (t p) d -> p (b t) d", p=P)
            for t in range(0, TILES, 4):
                sp.dma_start(g.x[:, t:t + 4, :], x[:, t:t + 4, :]).then_inc(s_x, 16)
            sp.dma_start(nat[SPARSE][:], ins["L0_attn_weight"].rearrange("(c p) k -> p c k", p=P)).then_inc(s_mask, 16)
            sp.dma_start(nat[BIN_FFN][:], ins["L1_ffn_weight"].rearrange("(c p) k -> p c k", p=P)).then_inc(s_bin, 16)
            for n, w in enumerate(("L1_attn_wq", "L1_attn_wk", "L1_attn_wv")):
                sp.dma_start(g.vo[:, n * KC:(n + 1) * KC, :], ins[w].rearrange("(c p) n -> p c n", p=P)).then_inc(g.qkv_loaded, 16)
            sp.wait_ge(s_x, 16 * TILES // 4)

        @block.scalar
        def _(act):
            act.dma_start(nat_a[:], ins["L0_ffn_A"].rearrange("e r k -> (e r) k")).then_inc(s_lora, 16)
            act.dma_start(nat_router[:], ins["L0_ffn_W_router"]).then_inc(s_lora, 16)
            for c in range(KC):
                act.dma_start(nat_b[:, c, :, :], ins["L0_ffn_B"][:, c * P:(c + 1) * P, :].rearrange("e o r -> o e r")).then_inc(s_lora, 16)
            act.dma_start(mask[:], ins["L0_attn_mask"].rearrange("(c p) k -> p c k", p=P)).then_inc(s_mask, 16)
            act.dma_start(same_block[:], ins["same_block"]).then_inc(s_const, 16)
            act.dma_start(g.causal_in[:], ins["causal"]).then_inc(s_const, 16)
            act.dma_start(g.iota[:], ins["iota"].partition_broadcast(P)).then_inc(s_const, 16)
            act.dma_start(g.bias[LORA_FFN][:], ins["L0_ffn_b_base"].partition_broadcast(P)).then_inc(s_const, 16)
            act.dma_start(g.bias[SPARSE][:], ins["L0_attn_bias"].partition_broadcast(P)).then_inc(s_const, 16)
            act.dma_start(wscale[:], ins["L1_ffn_wscale"].rearrange("(c p) o -> p (c o)", p=P), allow_slow_non_contiguous=True).then_inc(s_bin, 16)
            act.dma_start(wbias[:], ins["L1_ffn_wbias"].rearrange("(c p) o -> p (c o)", p=P), allow_slow_non_contiguous=True).then_inc(s_bin, 16)
            for n, kind in enumerate(order):
                for c in range(KC):
                    u = n * KC + c
                    act.wait_ge(s_tr, u + 1)
                    nc.scalar.copy(g.w_hi[kind][:, c, :], bank[u % 6][:]).then_inc(s_hi, 1)

        @block.tensor
        def _(pe):
            pe.wait_ge(s_const, 96)

            def transposed(n, kind):
                for c in range(KC):
                    u = n * KC + c
                    if u >= 6:
                        pe.wait_ge(s_lo, u - 5)
                    for i in range(KC):
                        last = nc.tensor.transpose(bank[u % 6][:, i * P:(i + 1) * P],
                                                   nat[kind][:, i, c * P:(c + 1) * P], g.ident[:])
                    last.then_inc(s_tr, 1)

            pe.wait_ge(s_base, 16)
            transposed(0, LORA_FFN)
            pe.wait_ge(s_lora, 96)
            for c in range(KC):
                last = nc.tensor.transpose(small_bank[:, c, :], nat_a[:, c * P:(c + 1) * P], g.ident[:])
            last.then_inc(s_small, 1)
            pe.wait_ge(s_small_out, 1)
            for c in range(KC):
                last = nc.tensor.transpose(small_bank[:, c, 0:E], nat_router[:, c * P:(c + 1) * P], g.ident[0:E, 0:E])
            last.then_inc(s_small, 1)
            pe.wait_ge(s_small_out, 2)
            for c in range(KC):
                last = nc.tensor.transpose(small_bank[:, c, :],
                                           nat_b[:, c, :, :].rearrange("p e r -> p (e r)"), g.ident[:])
            last.then_inc(s_small, 1)
            pe.wait_ge(s_sums, 1)
            nc.tensor.matmul(mask_bank[:, 0:NBLK], same_block[:], block_sum[:], start=True, stop=True).then_inc(s_onmap, 1)
            pe.wait_ge(s_nat, 1)
            transposed(1, SPARSE)
            pe.wait_ge(s_nat, 2)
            transposed(2, BIN_FFN)

        @block.vector
        def _(dve):
            own = Steps(s_own)

            def rest_of(n, kind):
                for c in range(KC):
                    u = n * KC + c
                    dve.wait_ge(s_hi, u + 1)
                    nc.vector.tensor_tensor(g.w_lo[kind][:, c, :], bank[u % 6][:],
                                            g.w_hi[kind][:, c, :].bitcast(F32), ALU.subtract).then_inc(s_lo, 1)

            dve.wait_ge(s_const, 96)
            own.then_wait(dve, nc.vector.tensor_scalar(g.bias[LORA_FFN][:], g.bias[LORA_FFN][:], 0.5, None, ALU.mult))
            rest_of(0, LORA_FFN)
            dve.wait_ge(s_small, 1)
            nc.vector.tensor_copy(g.ra[:, :, E:E + ER], small_bank[:]).then_inc(s_small_out, 1)
            dve.wait_ge(s_small, 2)
            nc.vector.tensor_copy(g.ra[:, :, 0:E], small_bank[:, :, 0:E]).then_inc(s_small_out, 1)
            dve.wait_ge(s_small, 3)
            up = small_bank[:].rearrange("p c n -> p (c n)")
            own.then_wait(dve, nc.vector.tensor_copy(g.up_hi[:], up))
            own.then_wait(dve, nc.vector.tensor_tensor(g.up_lo[:], up, g.up_hi[:].bitcast(F32), ALU.subtract))
            dve.wait_ge(s_mask, 32)
            nc.vector.tensor_reduce(block_sum[:], mask[:].rearrange("p c (b w) -> p (c b) w", w=BLK), AX.X, ALU.add).then_inc(s_sums, 1)
            dve.wait_ge(s_onmap, 1)
            own.then_wait(dve, nc.vector.tensor_scalar(block_on[:], mask_bank[:, 0:NBLK], 0.0, None, ALU.is_gt))
            w = nat[SPARSE][:].rearrange("p c (b w) -> p (c b) w", w=BLK)
            nc.vector.tensor_tensor(w, w, block_on[:].unsqueeze(2).broadcast_to((P, NBLK, BLK)), ALU.mult).then_inc(s_nat, 1)
            dve.wait_ge(s_bin, 48)
            own.then_wait(dve, nc.vector.tensor_scalar(neg_wscale[:], wscale[:], -1.0, None, ALU.mult))
            w = nat[BIN_FFN]
            own.then_wait(dve, nc.vector.tensor_scalar(positive[:], w[:], 0.0, None, ALU.is_gt))
            for c in range(KC):
                own.then_wait(dve, nc.vector.scalar_tensor_tensor(w[:, c, :], w[:, c, :], 0.0, positive[:, c, :], ALU.is_lt, ALU.subtract))
            for c in range(KC):
                ins_ = nc.vector.tensor_scalar(w[:, c, :], w[:, c, :], neg_wscale[:, c:c + 1], wbias[:, c:c + 1], ALU.mult, ALU.add)
            ins_.then_inc(s_nat, 1)
            rest_of(1, SPARSE)
            rest_of(2, BIN_FFN)


def dense_stages(nc, g, kinds, tag, out=None):
    with ExitStack() as ctx:
        def sb(name, shape, dt=F32):
            return ctx.enter_context(nc.sbuf_tensor(f"{tag}_{name}", shape, dt))

        def psum(name, shape):
            return ctx.enter_context(nc.psum_tensor(f"{tag}_{name}", shape, F32))

        def sem(name):
            return ctx.enter_context(nc.semaphore(f"{tag}_{name}"))

        lora = [k == LORA_FFN for k in kinds]
        normed = [k != OUT_PROJ for k in kinds]
        has_lora = any(lora)
        stats = [sb(f"stats{p}", [P, 6]) for p in range(2)]
        mean_var = [sb(f"mean_var{p}", [P, 2]) for p in range(2)]
        var_eps = [sb(f"var_eps{p}", [P, 1]) for p in range(2)]
        rstd = [sb(f"rstd{p}", [P, 1]) for p in range(2)]
        neg_half = sb("neg_half", [P, 1])
        eps = sb("eps", [P, 1])
        xn = [sb(f"xn{p}", [P, D]) for p in range(2)]
        xt_hi = [sb(f"xt_hi{p}", [P, KC, P], F32R) for p in range(2)]
        xt_lo = [sb(f"xt_lo{p}", [P, KC, P], F32R) for p in range(2)]
        xt_bank = [psum(f"xt_bank{p}", [P, KC, P]) for p in range(2)]
        y_bank = [psum(f"y_bank{p}", [P, D]) for p in range(2)]
        if has_lora:
            xt_sum = [sb(f"xt_sum{p}", [P, KC, P]) for p in range(2)]
            ra_bank = [psum(f"ra_bank{p}", [P, E + ER]) for p in range(2)]
            hw_bank = [psum(f"hw_bank{p}", [P, P]) for p in range(2)]
            top = [sb(f"top{p}", [P, 8]) for p in range(2)]
            top_at = [sb(f"top_at{p}", [P, 8], U32) for p in range(2)]
            top_atf = [sb(f"top_atf{p}", [P, 2]) for p in range(2)]
            ratio = [sb(f"ratio{p}", [P, 1]) for p in range(2)]
            gate = [sb(f"gate{p}", [P, 3]) for p in range(2)]
            share = [sb(f"share{p}", [P, 3, E]) for p in range(2)]
            logits = [sb(f"logits{p}", [P, E]) for p in range(2)]
            hw = [sb(f"hw{p}", [P, E, RANK]) for p in range(2)]
            hwt_hi = [sb(f"hwt_hi{p}", [P, P], F32R) for p in range(2)]
            hwt_lo = [sb(f"hwt_lo{p}", [P, P], F32R) for p in range(2)]

        mv_ready, rstd_ready, xn_ready, xt_ready, hi_ready, lo_ready = (sem(n) for n in (
            "mv_ready", "rstd_ready", "xn_ready", "xt_ready", "hi_ready", "lo_ready"))
        bias_in, multiplied, y_ready, x_done = sem("bias_in"), sem("multiplied"), sem("y_ready"), sem("x_done")
        sum_ready, ra_ready, ratio_ready, hw_ready, hwt_ready, hwt_hi_ready, hwt_lo_ready, top_ready = (sem(n) for n in (
            "sum_ready", "ra_ready", "ratio_ready", "hw_ready", "hwt_ready", "hwt_hi_ready", "hwt_lo_ready", "top_ready"))
        own_vector, own_pool = sem("own_vector"), sem("own_pool")
        block = ctx.enter_context(nc.Block())
        last_tile = len(kinds) * TILES

        if out is not None:
            stored = sem("stored")
            rows = out.rearrange("b (t p) d -> p (b t) d", p=P)

            @block.sync
            def _(sp):
                with sp.Fori(0, TILES) as t:
                    sp.wait_ge(x_done, t + (last_tile - TILES + 1))
                    sp.dma_start(rows[:, t, :], g.x[:, t, :]).then_inc(stored, 16)
                sp.wait_ge(stored, 16 * TILES)

        def normed_before(s):
            return sum(TILES for k in range(s) if normed[k]) - s * TILES

        def experts_before(s):
            return sum(TILES for k in range(s) if lora[k]) - s * TILES

        @block.tensor
        def _(pe):
            def transpose_x(s, t, T, p):
                pe.wait_ge(xn_ready, T + 1)
                at_least(pe, lo_ready, T - 1)
                for c in range(KC):
                    last = nc.tensor.transpose(xt_bank[p][:, c, :], xn[p][:, c * P:(c + 1) * P], g.ident[:])
                last.then_inc(xt_ready, 1)

            def experts_down(s, T, p):
                L = T + experts_before(s)
                pe.wait_ge(sum_ready, L + 1)
                at_least(pe, hw_ready, L - 1)
                for c in range(KC):
                    last = nc.tensor.matmul(ra_bank[p][:], xt_sum[p][:, c, :], g.ra[:, c, :],
                                            start=(c == 0), stop=(c == KC - 1))
                last.then_inc(ra_ready, 1)

            def transpose_hw(s, T, p):
                L = T + experts_before(s)
                pe.wait_ge(hw_ready, L + 1)
                at_least(pe, hwt_lo_ready, L - 1)
                nc.tensor.transpose(hw_bank[p][:], hw[p][:].rearrange("p e r -> p (e r)"), g.ident[:]).then_inc(hwt_ready, 1)

            def project(s, T, p):
                pe.wait_ge(lo_ready, T + 1)
                at_least(pe, x_done, T - 1)
                k = kinds[s]
                for c in range(KC):
                    nc.tensor.matmul(y_bank[p][:], xt_lo[p][:, c, :], g.w_hi[k][:, c, :], start=(c == 0), stop=False)
                    nc.tensor.matmul(y_bank[p][:], xt_hi[p][:, c, :], g.w_lo[k][:, c, :], start=False, stop=False)
                    last = nc.tensor.matmul(y_bank[p][:], xt_hi[p][:, c, :], g.w_hi[k][:, c, :],
                                            start=False, stop=(c == KC - 1 and not lora[s]))
                last.then_inc(multiplied, 1)

            def experts_up(s, T, p):
                L = T + experts_before(s)
                pe.wait_ge(hwt_lo_ready, L + 1)
                nc.tensor.matmul(y_bank[p][:], hwt_lo[p][:], g.up_hi[:], start=False, stop=False)
                nc.tensor.matmul(y_bank[p][:], hwt_hi[p][:], g.up_lo[:], start=False, stop=False)
                nc.tensor.matmul(y_bank[p][:], hwt_hi[p][:], g.up_hi[:], start=False, stop=True).then_inc(y_ready, 1)

            def tile(s, t, T, p):
                if lora[s]:
                    experts_down(s, T, p)
                back = neighbour(kinds, s, t, -1)
                back_lora = back is not None and lora[back[0]]
                if back_lora:
                    transpose_hw(back[0], T - 1, 1 - p)
                on = neighbour(kinds, s, t, 2)
                if on is not None:
                    transpose_x(on[0], on[1], T + 2, p)
                project(s, T, p)
                if back_lora:
                    experts_up(back[0], T - 1, 1 - p)

            transpose_x(0, 0, 0, 0)
            transpose_x(0, 1, 1, 1)
            over_tiles(pe, kinds, tile)
            if lora[-1]:
                transpose_hw(len(kinds) - 1, last_tile - 1, 1)
                experts_up(len(kinds) - 1, last_tile - 1, 1)

        @block.scalar
        def _(act):
            def round_x(s, T, p):
                act.wait_ge(xt_ready, T + 1)
                at_least(act, multiplied, T - 1)
                if lora[s]:
                    L = T + experts_before(s)
                    at_least(act, ra_ready, L - 1)
                    nc.scalar.copy(xt_sum[p][:], xt_bank[p][:]).then_inc(sum_ready, 1)
                nc.scalar.copy(xt_hi[p][:], xt_bank[p][:]).then_inc(hi_ready, 1)

            def tile(s, t, T, p):
                on = neighbour(kinds, s, t, 1)
                if on is not None:
                    round_x(on[0], T + 1, 1 - p)
                back = neighbour(kinds, s, t, -1)
                if back is not None and lora[back[0]]:
                    L = T - 1 + experts_before(back[0])
                    act.wait_ge(hwt_ready, L + 1)
                    nc.scalar.copy(hwt_hi[1 - p][:], hw_bank[1 - p][:]).then_inc(hwt_hi_ready, 1)
                if lora[s]:
                    L = T + experts_before(s)
                    act.wait_ge(top_ready, L + 1)
                    nc.scalar.activation(ratio[p][:], top[p][:, 0:1], ACT.Exp, bias=top[p][:, 1:2], scale=-1.0).then_inc(ratio_ready, 1)

            round_x(0, 0, 0)
            over_tiles(act, kinds, tile)

        @block.gpsimd
        def _(pool):
            own = Steps(own_pool)
            nc.gpsimd.memset(eps[:], EPS)
            own.then_wait(pool, nc.gpsimd.memset(neg_half[:], -0.5))

            def inverse_deviation(s, T, p):
                if not normed[s]:
                    return
                pool.wait_ge(mv_ready, T + normed_before(s) + 1)
                at_least(pool, xn_ready, T - 1)
                own.then_wait(pool, nc.gpsimd.tensor_tensor(var_eps[p][:], mean_var[p][:, 1:2], eps[:], ALU.add))
                nc.gpsimd.tensor_tensor(rstd[p][:], var_eps[p][:], neg_half[:], ALU.pow).then_inc(rstd_ready, 1)

            def tile(s, t, T, p):
                on = neighbour(kinds, s, t, LEAD)
                if on is not None:
                    inverse_deviation(on[0], T + LEAD, p)
                if kinds[s] in g.bias:
                    pool.wait_ge(xn_ready, T + 1)
                    nc.gpsimd.tensor_tensor(g.x[:, t, :], g.x[:, t, :], g.bias[kinds[s]][:], ALU.add).then_inc(bias_in, 1)

            for T in range(LEAD):
                inverse_deviation(0, T, T % 2)
            over_tiles(pool, kinds, tile, own, {k: 2 * (k != OUT_PROJ) for k in kinds})

        @block.vector
        def _(dve):
            own = Steps(own_vector)

            def statistics(s, t, T, p):
                if normed[s]:
                    if s:
                        dve.wait_ge(x_done, T - TILES + 1)
                    own.step(nc.vector.bn_stats(stats[p][:], g.x[:, t, :]))

            def mean_and_variance(s, p):
                if normed[s]:
                    nc.vector.bn_aggr(mean_var[p][:], stats[p][:]).then_inc(mv_ready, 1)

            def normalise(s, t, T, p):
                at_least(dve, xt_ready, T - 1)
                if not normed[s]:
                    nc.vector.tensor_copy(xn[p][:], g.vo[:, t, :]).then_inc(xn_ready, 1)
                    return
                dve.wait_ge(rstd_ready, T + normed_before(s) + 1)
                nc.vector.tensor_scalar(xn[p][:], g.x[:, t, :], mean_var[p][:, 0:1], rstd[p][:], ALU.subtract, ALU.mult).then_inc(xn_ready, 1)

            def rest_of_x(T, p):
                dve.wait_ge(hi_ready, T + 1)
                nc.vector.tensor_tensor(xt_lo[p][:], xt_bank[p][:], xt_hi[p][:].bitcast(F32), ALU.subtract).then_inc(lo_ready, 1)

            def rest_of_hw(s, T, p):
                L = T + experts_before(s)
                dve.wait_ge(hwt_hi_ready, L + 1)
                nc.vector.tensor_tensor(hwt_lo[p][:], hw_bank[p][:], hwt_hi[p][:].bitcast(F32), ALU.subtract).then_inc(hwt_lo_ready, 1)

            def copy_logits(s, T, p):
                L = T + experts_before(s)
                dve.wait_ge(ra_ready, L + 1)
                at_least(dve, ratio_ready, L - 1)
                own.then_wait(dve, nc.vector.tensor_copy(logits[p][:], ra_bank[p][:, 0:E]))

            def gates(s, T, p):
                L = T + experts_before(s)
                own.wait(dve)
                own.then_wait(dve, nc.vector.tensor_copy(top_atf[p][:], top_at[p][:, 0:2]))
                dve.wait_ge(ratio_ready, L + 1)
                own.then_wait(dve, nc.vector.tensor_scalar(gate[p][:, 0:1], ratio[p][:], 1.0, None, ALU.add))
                own.then_wait(dve, nc.vector.reciprocal(gate[p][:, 1:2], gate[p][:, 0:1]))
                own.then_wait(dve, nc.vector.tensor_tensor(gate[p][:, 2:3], gate[p][:, 1:2], ratio[p][:], ALU.mult))
                nc.vector.tensor_scalar(share[p][:, 0, :], g.iota[:], top_atf[p][:, 0:1], gate[p][:, 1:2], ALU.is_equal, ALU.mult)
                own.then_wait(dve, nc.vector.tensor_scalar(share[p][:, 1, :], g.iota[:], top_atf[p][:, 1:2], gate[p][:, 2:3], ALU.is_equal, ALU.mult))
                own.then_wait(dve, nc.vector.tensor_tensor(share[p][:, 2, :], share[p][:, 0, :], share[p][:, 1, :], ALU.add))
                at_least(dve, hwt_ready, L - 1)
                nc.vector.scalar_tensor_tensor(hw[p][:], ra_bank[p][:, E:E + ER].rearrange("p (e r) -> p e r", e=E), LORA_SCALE,
                                               share[p][:, 2, :].unsqueeze(2).broadcast_to((P, E, RANK)),
                                               ALU.mult, ALU.mult).then_inc(hw_ready, 1)

            def add_to_x(s, t, T, p):
                if lora[s]:
                    dve.wait_ge(y_ready, T + experts_before(s) + 1)
                else:
                    dve.wait_ge(multiplied, T + 1)
                n = sum(TILES for k in range(s) if kinds[k] in g.bias) - s * TILES
                if kinds[s] in g.bias:
                    dve.wait_ge(bias_in, T + n + 1)
                nc.vector.scalar_tensor_tensor(g.x[:, t, :], y_bank[p][:], RESIDUAL[kinds[s]], g.x[:, t, :], ALU.mult, ALU.add).then_inc(x_done, 1)

            def tile(s, t, T, p):
                on = neighbour(kinds, s, t, 1)
                if on is not None:
                    rest_of_x(T + 1, 1 - p)
                back = neighbour(kinds, s, t, -1)
                if back is not None and lora[back[0]]:
                    rest_of_hw(back[0], T - 1, 1 - p)
                if lora[s]:
                    copy_logits(s, T, p)
                far, near = neighbour(kinds, s, t, 4), neighbour(kinds, s, t, 3)
                if far is not None:
                    statistics(far[0], far[1], T + 4, p)
                if lora[s]:
                    nc.vector.max(top[p][:], logits[p][:]).then_inc(top_ready, 1)
                    dve.wait_ge(top_ready, T + experts_before(s) + 1)
                if lora[s] or (far is not None and normed[far[0]]):
                    own.wait(dve)
                if near is not None:
                    normalise(near[0], near[1], T + 3, 1 - p)
                if lora[s]:
                    own.step(nc.vector.max_index(top_at[p][:], top[p][:], logits[p][:]))
                if far is not None:
                    mean_and_variance(far[0], p)
                if lora[s]:
                    gates(s, T, p)
                if back is not None:
                    add_to_x(back[0], back[1], T - 1, 1 - p)

            def both(T):
                statistics(0, T, T, T % 2)
                if normed[0]:
                    own.wait(dve)
                mean_and_variance(0, T % 2)

            both(0)
            both(1)
            for T in range(3):
                normalise(0, T, T, T % 2)
                if T < 2:
                    both(T + 2)
            rest_of_x(0, 0)
            own_per = {k: 2 * (k != OUT_PROJ) + 16 * (k == LORA_FFN) for k in kinds}
            over_tiles(dve, kinds, tile, own, own_per)
            if lora[-1]:
                rest_of_hw(len(kinds) - 1, last_tile - 1, 1)
            add_to_x(len(kinds) - 1, TILES - 1, last_tile - 1, 1)


def project_qkv(nc, g):
    SUPER = 4
    TOK = SUPER * P
    HALF = S // P // SUPER
    with ExitStack() as ctx:
        def sb(name, shape, dt=F32):
            return ctx.enter_context(nc.sbuf_tensor(f"qkv_{name}", shape, dt))

        def psum(name, shape):
            return ctx.enter_context(nc.psum_tensor(f"qkv_{name}", shape, F32))

        def sem(name):
            return ctx.enter_context(nc.semaphore(f"qkv_{name}"))

        w_hi = {w: sb(f"w_hi_{w}", [P, KC, D], F32R) for w in "qkv"}
        w_lo = {w: sb(f"w_lo_{w}", [P, KC, D], F32R) for w in "qkv"}
        cos = sb("cos", [P, S])
        sin = sb("sin", [P, S])
        stats = [sb(f"stats{i}", [P, 6]) for i in range(4)]
        mean_var = [sb(f"mean_var{i}", [P, 2]) for i in range(4)]
        var_eps = [sb(f"var_eps{p}", [P, 1]) for p in range(2)]
        rstd = [sb(f"rstd{p}", [P, 1]) for p in range(2)]
        neg_half = sb("neg_half", [P, 1])
        eps = sb("eps", [P, 1])
        xn = [sb(f"xn{p}", [P, D]) for p in range(2)]
        xt_hi = [sb(f"xt_hi{u}", [P, KC, TOK], F32R) for u in range(HALF)]
        xt_lo = [sb(f"xt_lo{u}", [P, KC, TOK], F32R) for u in range(HALF)]
        prod = [sb(f"prod{p}", [P, 4, TOK]) for p in range(2)]
        parts = [sb(f"parts{p}", [P, 2, 3, TOK], BF16) for p in range(2)]
        xt_bank = [psum(f"xt_bank{p}", [P, KC, P]) for p in range(2)]
        v_bank = [psum(f"v_bank{p}", [P, D]) for p in range(2)]
        pair_bank = [[psum(f"pair_bank{p}{e}", [P, TOK]) for e in range(2)] for p in range(2)]

        tables_loaded, w_hi_ready, w_lo_ready = sem("tables"), sem("w_hi"), sem("w_lo")
        mv_ready, rstd_ready, xn_ready, xt_ready, hi_ready, lo_ready, v_ready, v_copied = (sem(n) for n in (
            "mv_ready", "rstd_ready", "xn_ready", "xt_ready", "hi_ready", "lo_ready", "v_ready", "v_copied"))
        pair_ready, products, rotated, high, rest, middle, low = (sem(n) for n in (
            "pair_ready", "products", "rotated", "high", "rest", "middle", "low"))
        stored = [sem(f"stored{p}") for p in range(2)]
        own_vector, own_pool = sem("own_vector"), sem("own_pool")
        block = ctx.enter_context(nc.Block())
        SLOTS = SUPER * HALF
        PAIRS = [("q", 0), ("q", 1), ("k", 0), ("k", 1)]

        def batches(eng, body, steps=None, per=0):
            with eng.Fori(0, B) as b:
                if steps:
                    steps.enter(b, per)
                body(b)
                if steps:
                    steps.leave(B)

        @block.sync
        def _(sp):
            sp.dma_start(cos[:], g.cos_in).then_inc(tables_loaded, 16)
            sp.dma_start(sin[:], g.sin_in).then_inc(tables_loaded, 16)

            def body(b):
                for n in range(SLOTS):
                    N, p = b * SLOTS + n, n % 2
                    u, (which, half) = n // SUPER, PAIRS[n % SUPER]
                    sp.wait_ge(low, N + 1)
                    rows = g.scratch[which].rearrange("c (h e f) t -> e c h f t", e=2, f=8)
                    for e in range(2):
                        for c in range(3):
                            dst = rows[e, c, half * 16:(half + 1) * 16, :, bass.ds(b * S + u * TOK, TOK)]
                            sp.dma_start(dst, parts[p][:, e, c, :]).then_inc(stored[p], 16)

            batches(sp, body)
            for p in range(2):
                sp.wait_ge(stored[p], B * SLOTS // 2 * 96)

        @block.scalar
        def _(act):
            act.wait_ge(g.qkv_loaded, 48)
            for n, w in enumerate("qkv"):
                for c in range(KC):
                    nc.scalar.copy(split_view(w_hi[w], w, c), raw_view(g, n, w, c)).then_inc(w_hi_ready, 1)

            def body(b):
                for n in range(SUPER):
                    act.wait_ge(xt_ready, b * SLOTS + n + 1)
                    if n == 0:
                        act.wait_ge(v_ready, b * SLOTS)
                        act.wait_ge(pair_ready, b * SLOTS)
                    nc.scalar.copy(xt_hi[0][:, :, n * P:(n + 1) * P], xt_bank[n % 2][:]).then_inc(hi_ready, 1)
                for n in range(SLOTS):
                    N, p = b * SLOTS + n, n % 2
                    if n < SLOTS - SUPER:
                        act.wait_ge(xt_ready, N + SUPER + 1)
                        nc.scalar.copy(xt_hi[1][:, :, n * P:(n + 1) * P], xt_bank[p][:]).then_inc(hi_ready, 1)
                    act.wait_ge(v_ready, N + 1)
                    nc.scalar.copy(g.vo[:, N, :], v_bank[p][:]).then_inc(v_copied, 1)
                    act.wait_ge(rotated, N + 1)
                    if n >= 2:
                        act.wait_ge(stored[p], b * (SLOTS // 2 * 96) + n // 2 * 96)
                    else:
                        act.wait_ge(stored[p], b * (SLOTS // 2 * 96))
                    nc.scalar.copy(parts[p][:, :, 0, :], prod[p][:, 0:2, :]).then_inc(high, 1)
                    act.wait_ge(rest, N + 1)
                    nc.scalar.copy(parts[p][:, :, 1, :], prod[p][:, 2:4, :]).then_inc(middle, 1)

            batches(act, body)

        @block.tensor
        def _(pe):
            def turn(N, n):
                pe.wait_ge(xn_ready, N + 1)
                pe.wait_ge(lo_ready, N if n == 0 else N - 1)
                for c in range(KC):
                    last = nc.tensor.transpose(xt_bank[n % 2][:, c, :], xn[n % 2][:, c * P:(c + 1) * P], g.ident[:])
                last.then_inc(xt_ready, 1)

            def body(b):
                for n in range(SUPER):
                    turn(b * SLOTS + n, n)
                for n in range(SLOTS):
                    N, p = b * SLOTS + n, n % 2
                    u, r = n // SUPER, n % SUPER
                    if n < SLOTS - SUPER:
                        turn(N + SUPER, n + SUPER)
                    pe.wait_ge(lo_ready, N + 1)
                    pe.wait_ge(v_copied, N if n == 0 else N - 1)
                    t = slice(r * P, (r + 1) * P)
                    for c in range(KC):
                        nc.tensor.matmul(v_bank[p][:], xt_lo[u][:, c, t], w_hi["v"][:, c, :], start=(c == 0), stop=False)
                        nc.tensor.matmul(v_bank[p][:], xt_hi[u][:, c, t], w_lo["v"][:, c, :], start=False, stop=False)
                        last = nc.tensor.matmul(v_bank[p][:], xt_hi[u][:, c, t], w_hi["v"][:, c, :], start=False, stop=(c == KC - 1))
                    last.then_inc(v_ready, 1)
                    if r == 0:
                        pe.wait_ge(lo_ready, b * SLOTS + (u + 1) * SUPER)
                    pe.wait_ge(products, N if n == 0 else N - 1)
                    which, half = PAIRS[r]
                    for e in range(2):
                        f = slice((half * 2 + e) * P, (half * 2 + e + 1) * P)
                        for c in range(KC):
                            nc.tensor.matmul(pair_bank[p][e][:], w_lo[which][:, c, f], xt_hi[u][:, c, :], start=(c == 0), stop=False)
                            nc.tensor.matmul(pair_bank[p][e][:], w_hi[which][:, c, f], xt_lo[u][:, c, :], start=False, stop=False)
                            last = nc.tensor.matmul(pair_bank[p][e][:], w_hi[which][:, c, f], xt_hi[u][:, c, :], start=False, stop=(c == KC - 1))
                    last.then_inc(pair_ready, 1)

            pe.wait_ge(w_lo_ready, 3 * KC)
            batches(pe, body)

        @block.gpsimd
        def _(pool):
            own = Steps(own_pool)
            nc.gpsimd.memset(eps[:], EPS)
            own.then_wait(pool, nc.gpsimd.memset(neg_half[:], -0.5))

            def inverse_deviation(N, n):
                pool.wait_ge(mv_ready, N + 1)
                pool.wait_ge(xn_ready, N if n == 0 else N - 1)
                p = n % 2
                own.then_wait(pool, nc.gpsimd.tensor_tensor(var_eps[p][:], mean_var[n % 4][:, 1:2], eps[:], ALU.add))
                nc.gpsimd.tensor_tensor(rstd[p][:], var_eps[p][:], neg_half[:], ALU.pow).then_inc(rstd_ready, 1)

            def body(b):
                for n in range(SUPER + 1):
                    inverse_deviation(b * SLOTS + n, n)
                for n in range(SLOTS):
                    N, p = b * SLOTS + n, n % 2
                    pool.wait_ge(products, N + 1)
                    nc.gpsimd.tensor_tensor(prod[p][:, 0, :], prod[p][:, 0, :], prod[p][:, 2, :], ALU.subtract)
                    nc.gpsimd.tensor_tensor(prod[p][:, 1, :], prod[p][:, 1, :], prod[p][:, 3, :], ALU.add).then_inc(rotated, 1)
                    if n + SUPER + 1 < SLOTS:
                        inverse_deviation(N + SUPER + 1, n + SUPER + 1)
                    pool.wait_ge(middle, N + 1)
                    nc.gpsimd.tensor_tensor(parts[p][:, :, 2, :], prod[p][:, 2:4, :], parts[p][:, :, 1, :], ALU.subtract).then_inc(low, 1)

            batches(pool, body, own, SLOTS)

        @block.vector
        def _(dve):
            own = Steps(own_vector)
            for n, w in enumerate("qkv"):
                for c in range(KC):
                    dve.wait_ge(w_hi_ready, n * KC + c + 1)
                    nc.vector.tensor_tensor(split_view(w_lo[w], w, c), raw_view(g, n, w, c), split_view(w_hi[w], w, c).bitcast(F32), ALU.subtract).then_inc(w_lo_ready, 1)
            dve.wait_ge(tables_loaded, 32)

            def statistics(N, n):
                own.step(nc.vector.bn_stats(stats[n % 4][:], g.x[:, N, :]))

            def mean_and_variance(n):
                nc.vector.bn_aggr(mean_var[n % 4][:], stats[n % 4][:]).then_inc(mv_ready, 1)

            def normalise(N, n):
                p = n % 2
                dve.wait_ge(rstd_ready, N + 1)
                dve.wait_ge(xt_ready, N if n == 0 else N - 1)
                nc.vector.tensor_scalar(xn[p][:], g.x[:, N, :], mean_var[n % 4][:, 0:1], rstd[p][:], ALU.subtract, ALU.mult).then_inc(xn_ready, 1)

            def split(N, n):
                u, r = n // SUPER, n % SUPER
                t = slice(r * P, (r + 1) * P)
                dve.wait_ge(hi_ready, N + 1)
                nc.vector.tensor_tensor(xt_lo[u][:, :, t], xt_bank[n % 2][:], xt_hi[u][:, :, t].bitcast(F32), ALU.subtract).then_inc(lo_ready, 1)

            def body(b):
                statistics(b * SLOTS, 0)
                statistics(b * SLOTS + 1, 1)
                own.wait(dve)
                statistics(b * SLOTS + 2, 2)
                mean_and_variance(0)
                mean_and_variance(1)
                for n in range(SUPER):
                    if 1 <= n < SUPER - 1:
                        statistics(b * SLOTS + n + 2, n + 2)
                    if n < SUPER - 1:
                        own.wait(dve)
                    normalise(b * SLOTS + n, n)
                    if n < SUPER - 1:
                        mean_and_variance(n + 2)
                    split(b * SLOTS + n, n)
                for n in range(SLOTS):
                    N, p = b * SLOTS + n, n % 2
                    k = n + SUPER
                    if k < SLOTS:
                        if k + 1 < SLOTS:
                            statistics(N + SUPER + 1, k + 1)
                            own.wait(dve)
                        normalise(N + SUPER, k)
                        if k + 1 < SLOTS:
                            mean_and_variance(k + 1)
                        split(N + SUPER, k)
                    u = n // SUPER
                    tok = slice(u * TOK, (u + 1) * TOK)
                    dve.wait_ge(pair_ready, N + 1)
                    dve.wait_ge(low, N if n == 0 else N - 1)
                    even, odd = pair_bank[p]
                    nc.vector.tensor_tensor(prod[p][:, 0, :], even[:], cos[:, tok], ALU.mult)
                    nc.vector.tensor_tensor(prod[p][:, 1, :], even[:], sin[:, tok], ALU.mult)
                    nc.vector.tensor_tensor(prod[p][:, 2, :], odd[:], sin[:, tok], ALU.mult)
                    nc.vector.tensor_tensor(prod[p][:, 3, :], odd[:], cos[:, tok], ALU.mult).then_inc(products, 1)
                    dve.wait_ge(high, N + 1)
                    nc.vector.tensor_tensor(prod[p][:, 2:4, :], prod[p][:, 0:2, :], parts[p][:, :, 0, :], ALU.subtract).then_inc(rest, 1)

            batches(dve, body, own, SLOTS)


def raw_view(g, n, w, c):
    raw = g.vo[:, n * KC + c, :]
    return raw if w == "v" else raw.rearrange("p (a m e) -> p a e m", a=2, e=2)


def split_view(weight, w, c):
    part = weight[:, c, :]
    return part if w == "v" else part.rearrange("p (a e m) -> p a e m", a=2, e=2)


HEADS, HD = 32, 16
GH = 4
GROUPS = B * HEADS // GH
QT = S // P
ROWS = 6 * HD
NEG = -3.0e38


def attention(nc, g):
    NBUF = 3
    with ExitStack() as ctx:
        def sb(name, shape, dt=F32):
            return ctx.enter_context(nc.sbuf_tensor(f"att_{name}", shape, dt))

        def sem(name):
            return ctx.enter_context(nc.semaphore(f"att_{name}"))

        q_rows = [sb(f"q_rows{i}", [P, GH, S], BF16) for i in range(NBUF)]
        k_rows = [sb(f"k_rows{i}", [P, GH, S], BF16) for i in range(NBUF)]
        v_rows = [sb(f"v_rows{i}", [P, QT, GH, 32]) for i in range(NBUF)]
        probs = [sb(f"probs{i}", [P, GH, S]) for i in range(2)]
        o_t = sb("o_t", [P, S])
        part_max = sb("part_max", [P, GH, QT, 2])
        row_max = sb("row_max", [P, GH * QT])
        neg_rest = sb("neg_rest", [P, 2, GH * QT])
        neg_parts = sb("neg_parts", [P, 3, GH * QT], BF16)
        neg_turned = sb("neg_turned", [3 * GH * QT, P], BF16)
        inv_sum = sb("inv_sum", [P, QT // 2 * GH])
        ident_b = sb("ident_b", [P, P], BF16)
        causal = sb("causal", [P, P], BF16)
        scores = [ctx.enter_context(nc.psum_tensor(f"att_scores{i}", [P, S], F32)) for i in range(2)]
        ring = [ctx.enter_context(nc.psum_tensor(f"att_ring{i}", [P, D], F32)) for i in range(2)]
        o_bank = [ctx.enter_context(nc.psum_tensor(f"att_o{i}", [P, D], F32)) for i in range(2)]

        ready = sem("constants")
        rows_loaded = [sem(f"rows_loaded{i}") for i in range(NBUF)]
        max_loaded = [sem(f"max_loaded{i}") for i in range(NBUF)]
        scored, exped, valued, v_ready = (sem(n) for n in ("scored", "exped", "valued", "v_ready"))
        o_copied, ring_ready, ring_done, neg_ready = (sem(n) for n in ("o_copied", "ring_ready", "ring_done", "neg_ready"))
        own_vector, own_pool = sem("own_vector"), sem("own_pool")
        block = ctx.enter_context(nc.Block())

        UNITS = [(h, i, half) for h in range(GH) for i in range(QT) for half in range(1 + (i >= QT // 2))]
        NU = len(UNITS)
        SLOTS = QT * GH
        ROUND = NU + 3
        LOADS = 12 * 16

        def ring_base(G):
            if isinstance(G, int) and G == 0:
                return NU + 1
            return G * ROUND + (NU + 1 + NU + 1 - ROUND)

        def turns(eng, turn, steps=None, per=0):
            turn(0, 0, 0)
            rounds = (GROUPS - 4) // NBUF
            with eng.Fori(0, rounds) as i:
                if steps:
                    steps.enter(i, per * NBUF)
                for k in range(NBUF):
                    turn(i * NBUF + (1 + k), (1 + k) % NBUF, i + (1 + k) // NBUF)
                if steps:
                    steps.leave(rounds)
            for G in range(1 + rounds * NBUF, GROUPS):
                turn(G, G % NBUF, G // NBUF)

        def is_last(G):
            return isinstance(G, int) and G == GROUPS - 1

        def is_first(G):
            return isinstance(G, int) and G == 0

        def after(buf, cycle):
            return (buf + 1) % NBUF, cycle + (buf + 1) // NBUF

        @block.sync
        def _(sp):
            def load(G, buf):
                head = (G % 8) * (GH * HD)
                tok = (G // 8) * S
                for rows, which, parts in ((q_rows, "q", (0, 1, 2, 0, 1, 0)), (k_rows, "k", (0, 0, 0, 1, 1, 2))):
                    for r, part in enumerate(parts):
                        src = g.scratch[which][part, bass.ds(head, GH * HD), bass.ds(tok, S)]
                        sp.dma_start(rows[buf][r * HD:(r + 1) * HD, :, :], src.rearrange("(h r) t -> r h t", h=GH)).then_inc(rows_loaded[buf], 16)

            def load_max(buf):
                sp.dma_start(q_rows[buf][ROWS:ROWS + 3, :, :].rearrange("c h (i t) -> c (h i) t", t=P), neg_turned[:]).then_inc(max_loaded[buf], 16)

            def turn(G, buf, cycle):
                if not isinstance(G, int) or G + 2 < GROUPS:
                    at_least(sp, scored, G * SLOTS)
                    load(G + 2, (buf + 2) % NBUF)
                if not is_last(G):
                    sp.wait_ge(ring_done, ring_base(G) + NU + (1 if is_first(G) else 3))
                    load_max(after(buf, cycle)[0])

            load(0, 0)
            load(1, 1)
            sp.wait_ge(ring_done, NU + 1)
            load_max(0)
            turns(sp, turn)
            sp.wait_ge(max_loaded[(GROUPS - 1) % NBUF], 16 * (GROUPS // NBUF + 1))

        @block.tensor
        def _(pe):
            def max_unit(u, units, buf):
                h, i, half = u
                w = min((i + 1) * P - half * D, D)
                pe_ring(units)
                bank = ring[units[1] % 2]
                diagonal = (i * P) // D == half
                last = nc.tensor.matmul(bank[:, 0:w], q_rows[buf][0:ROWS, h, i * P:(i + 1) * P],
                                        k_rows[buf][0:ROWS, h, half * D:half * D + w], start=True, stop=not diagonal)
                if diagonal:
                    last = nc.tensor.matmul(bank[:, w - P:w], ident_b[:], causal[:], start=False, stop=True)
                last.then_inc(ring_ready, 1)

            def pe_ring(units):
                base, n = units[0], units[1]
                at_least(pe, ring_done, base + (n - 1 if n >= 2 else 0))

            def turn_max(units):
                pe.wait_ge(neg_ready, units[2])
                pe_ring(units)
                out = ring[units[1] % 2][0:3 * GH * QT, 0:P // 2].bitcast(BF16)
                nc.tensor.transpose(out, neg_parts[:].rearrange("p c n -> p (c n)"), ident_b[:]).then_inc(ring_ready, 1)

            def turn_o(units, half, G1):
                pe.wait_ge(o_copied, G1 * 2 + 2)
                pe_ring(units)
                for i in range(QT // 2):
                    c = (half * (QT // 2) + i) * P
                    last = nc.tensor.transpose(ring[units[1] % 2][:, i * P:(i + 1) * P], o_t[:, c:c + P], g.ident[:])
                last.then_inc(ring_ready, 1)

            def score(G, buf, j, h):
                slot = j * GH + h
                at_least(pe, exped, G * SLOTS + slot - 1)
                for a, z in ((D, S), (j * P, D)) if j < QT // 2 else ((j * P, S),):
                    nc.tensor.matmul(scores[slot % 2][:, a:z], k_rows[buf][0:ROWS + 3, h, j * P:(j + 1) * P],
                                     q_rows[buf][0:ROWS + 3, h, a:z], start=True, stop=a != j * P)
                nc.tensor.matmul(scores[slot % 2][:, j * P:(j + 1) * P], causal[:], ident_b[:],
                                 start=False, stop=True).then_inc(scored, 1)

            def value(G, buf, j):
                pe.wait_ge(exped, G * SLOTS + (j + 1) * GH)
                if j == 0:
                    pe.wait_ge(v_ready, G + 1)
                    at_least(pe, o_copied, G * 2)
                for a, z in ((j * P, D), (D, S)) if j < QT // 2 else ((j * P, S),):
                    half = a // D
                    for h in range(GH):
                        last = nc.tensor.matmul(o_bank[half][32 * h:32 * h + 32, a - half * D:z - half * D],
                                                v_rows[buf][:, j, h, :], probs[j % 2][:, h, a:z],
                                                start=(j == 0), stop=(j == (QT // 2 - 1 if half == 0 else QT - 1)),
                                                skip_group_check=True)
                last.then_inc(valued, 1)

            def turn(G, buf, cycle):
                base = ring_base(G)
                n = 0
                nbuf, ncycle = after(buf, cycle)
                first = 2
                pe.wait_ge(max_loaded[buf], cycle * 16 + 16)
                todo = list(UNITS)
                for slot in range(SLOTS):
                    j, h = divmod(slot, GH)
                    score(G, buf, j, h)
                    if slot == first:
                        if not is_first(G):
                            for half in range(2):
                                turn_o((base, n), half, G - 1)
                                n += 1
                        if not is_last(G):
                            pe.wait_ge(rows_loaded[nbuf], ncycle * LOADS + LOADS)
                    if slot >= first and not is_last(G):
                        for u in todo[:3]:
                            max_unit(u, (base, n), nbuf)
                            n += 1
                        todo = todo[3:]
                    if slot == 22 and not is_last(G):
                        turn_max((base, n, G + 2))
                        n += 1
                    if h == GH - 1 and j >= 1:
                        value(G, buf, j - 1)
                value(G, buf, QT - 1)

            pe.wait_ge(ready, 4)
            pe.wait_ge(rows_loaded[0], LOADS)
            for n, u in enumerate(UNITS):
                max_unit(u, (0, n), 0)
            turn_max((0, NU, 1))
            turns(pe, turn)
            base = ring_base(GROUPS - 1) + 2
            for half in range(2):
                turn_o((base, half), half, GROUPS - 1)

        @block.scalar
        def _(act):
            def copy_o(G1):
                act.wait_ge(valued, G1 * QT + QT)
                at_least(act, ring_ready, ring_base(G1) + 2 if not is_first(G1) else 0)
                for half in range(2):
                    nc.scalar.copy(o_t[:, half * D:(half + 1) * D], o_bank[half][:]).then_inc(o_copied, 1)

            def turn(G, buf, cycle):
                if not is_first(G):
                    copy_o(G - 1)
                for slot in range(SLOTS):
                    j, h = divmod(slot, GH)
                    act.wait_ge(scored, G * SLOTS + slot + 1)
                    at_least(act, valued, G * QT + j - 1)
                    nc.scalar.activation(probs[j % 2][:, h, j * P:S], scores[slot % 2][:, j * P:S], ACT.Exp,
                                         scale=float(HD) ** -0.5).then_inc(exped, 1)

            turns(act, turn)
            copy_o(GROUPS - 1)

        @block.gpsimd
        def _(pool):
            for i in range(NBUF):
                nc.gpsimd.memset(v_rows[i][:], 0.0).then_inc(own_pool, 1)
            pool.wait_ge(own_pool, NBUF)
            for i in range(NBUF):
                nc.gpsimd.memset(v_rows[i][:, :, :, HD:HD + 1], 1.0).then_inc(own_pool, 1)
            pool.wait_ge(own_pool, 2 * NBUF)

            def take_v(G, buf):
                src = g.vo[:, bass.ds((G // 8) * QT, QT), bass.ds((G % 8) * (GH * HD), GH * HD)]
                nc.gpsimd.tensor_copy(v_rows[buf][:, :, :, 0:HD], src.rearrange("p t (h d) -> p t h d", h=GH)).then_inc(v_ready, 1)

            def turn(G, buf, cycle):
                if not is_last(G):
                    at_least(pool, valued, G * QT)
                    take_v(G + 1, (buf + 1) % NBUF)

            take_v(0, 0)
            turns(pool, turn)

        @block.vector
        def _(dve):
            own = Steps(own_vector)
            own.then_wait(dve, nc.vector.tensor_copy(ident_b[:], g.ident[:]))
            nc.vector.tensor_copy(causal[:], g.causal_in[:]).then_inc(ready, 1)
            for i in range(NBUF):
                nc.vector.memset(k_rows[i][ROWS:ROWS + 3, :, :], 1.0).then_inc(ready, 1)
            own.then_wait(dve, nc.vector.memset(part_max[:], NEG))

            def maxima(base, n0, ready_at):
                for n, (h, i, half) in enumerate(UNITS):
                    w = min((i + 1) * P - half * D, D)
                    dve.wait_ge(ring_ready, base + n0 + n + 1)
                    nc.vector.tensor_reduce(part_max[:, h, i, half:half + 1], ring[(n0 + n) % 2][:, 0:w], AX.X, ALU.max).then_inc(ring_done, 1)
                dve.wait_ge(ring_done, base + n0 + NU)
                own.then_wait(dve, nc.vector.tensor_reduce(row_max[:], part_max[:].rearrange("p h i a -> p (h i) a"), AX.X, ALU.max))
                own.then_wait(dve, nc.vector.tensor_scalar(neg_parts[:, 0, :], row_max[:], -1.0, None, ALU.mult))
                own.then_wait(dve, nc.vector.scalar_tensor_tensor(neg_rest[:, 0, :], row_max[:], -1.0, neg_parts[:, 0, :], ALU.mult, ALU.subtract))
                own.then_wait(dve, nc.vector.tensor_copy(neg_parts[:, 1, :], neg_rest[:, 0, :]))
                nc.vector.tensor_tensor(neg_parts[:, 2, :], neg_rest[:, 0, :], neg_parts[:, 1, :], ALU.subtract).then_inc(neg_ready, 1)
                dve.wait_ge(ring_ready, base + n0 + NU + 1)
                nc.vector.tensor_copy(neg_turned[:], ring[(n0 + NU) % 2][0:3 * GH * QT, 0:P // 2].bitcast(BF16)).then_inc(ring_done, 1)

            def outputs(base, G1):
                for half in range(2):
                    dve.wait_ge(ring_ready, base + half + 1)
                    o = ring[half][:].rearrange("p (i h d) -> p i h d", h=GH, d=32)
                    inv = inv_sum[:].rearrange("p (i h) -> p i h", h=GH)
                    if half:
                        dve.wait_ge(ring_done, base + 1)
                    own.then_wait(dve, nc.vector.reciprocal(inv, o[:, :, :, HD]))
                    dst = g.vo[:, bass.ds((G1 // 8) * QT + half * (QT // 2), QT // 2), bass.ds((G1 % 8) * (GH * HD), GH * HD)]
                    nc.vector.tensor_tensor(dst.rearrange("p t (h d) -> p t h d", h=GH), o[:, :, :, 0:HD],
                                            inv.unsqueeze(3).broadcast_to((P, QT // 2, GH, HD)), ALU.mult).then_inc(ring_done, 1)

            def turn(G, buf, cycle):
                base = ring_base(G)
                if not is_first(G):
                    outputs(base, G - 1)
                if not is_last(G):
                    nbuf, ncycle = after(buf, cycle)
                    dve.wait_ge(max_loaded[buf], cycle * 16 + 16)
                    maxima(base, 0 if is_first(G) else 2, G + 2)

            maxima(0, 0, 1)
            turns(dve, turn, own, 6)
            outputs(ring_base(GROUPS - 1) + 2, GROUPS - 1)


class Shared:
    pass


def program(nc, ins, out):
    with ExitStack() as ctx:
        def sb(name, shape, dt=F32, at=ctx):
            return at.enter_context(nc.sbuf_tensor(name, shape, dt))

        g = Shared()
        g.x = sb("x", [P, TILES, D])
        g.vo = sb("v_then_o", [P, TILES, D])
        g.ident = sb("identity", [P, P])
        g.causal_in = sb("causal_in", [P, P])
        g.w_hi = {BIN_FFN: sb("w_hi_bin", [P, KC, D], F32R)}
        g.w_lo = {BIN_FFN: sb("w_lo_bin", [P, KC, D], F32R)}
        g.scratch = {w: nc.dram_tensor(f"{w}_parts", (3, D, B * S), BF16, kind="Internal").ap() for w in "qk"}
        g.qkv_loaded = ctx.enter_context(nc.semaphore("qkv_loaded"))
        g.cos_in, g.sin_in = ins["cos"], ins["sin"]
        with ExitStack() as first:
            g.iota = sb("expert_numbers", [P, E], at=first)
            g.bias = {LORA_FFN: sb("bias_ffn", [P, D], at=first), SPARSE: sb("bias_sparse", [P, D], at=first)}
            for k in (LORA_FFN, SPARSE):
                g.w_hi[k] = sb(f"w_hi{k}", [P, KC, D], F32R, at=first)
                g.w_lo[k] = sb(f"w_lo{k}", [P, KC, D], F32R, at=first)
            g.ra = sb("router_and_down", [P, KC, E + ER], at=first)
            g.up_hi = sb("up_hi", [P, D], F32R, at=first)
            g.up_lo = sb("up_lo", [P, D], F32R, at=first)
            prepare_weights(nc, ins, g)
            dense_stages(nc, g, BEFORE, "ffn")
        project_qkv(nc, g)
        attention(nc, g)
        g.w_hi[OUT_PROJ] = sb("w_hi_out", [P, KC, D], F32R)
        g.w_lo[OUT_PROJ] = sb("w_lo_out", [P, KC, D], F32R)
        split_out_projection(nc, ins, g)
        dense_stages(nc, g, (OUT_PROJ, BIN_FFN), "end", out)


def split_out_projection(nc, ins, g):
    with (nc.sbuf_tensor("wo_raw", [P, KC, D], F32) as raw, nc.semaphore("wo_loaded") as loaded,
          nc.semaphore("wo_hi") as hi, nc.Block() as block):
        @block.sync
        def _(sp):
            sp.dma_start(raw[:], ins["L1_attn_wo"].rearrange("(c p) n -> p c n", p=P)).then_inc(loaded, 16)

        @block.scalar
        def _(act):
            act.wait_ge(loaded, 16)
            nc.scalar.copy(g.w_hi[OUT_PROJ][:], raw[:]).then_inc(hi, 1)

        @block.vector
        def _(dve):
            dve.wait_ge(hi, 1)
            nc.vector.tensor_tensor(g.w_lo[OUT_PROJ][:], raw[:], g.w_hi[OUT_PROJ][:].bitcast(F32), ALU.subtract)


def rotation_tables():
    inv = 1.0 / 10000.0 ** (np.arange(0, HD, 2)[:HD // 2].astype(np.float32) / HD)
    f = np.outer(np.arange(S), inv).astype(np.float32)
    return (np.ascontiguousarray(np.tile(t.T, (P // (HD // 2), 1))) for t in (np.cos(f), np.sin(f)))


def shape_constants():
    cos, sin = rotation_tables()
    return {
        "ident": np.eye(P, dtype=np.float32),
        "same_block": np.kron(np.eye(P // BLK, dtype=np.float32), np.ones((BLK, BLK), np.float32)),
        "iota": np.arange(E, dtype=np.float32),
        "causal": np.triu(np.full((P, P), NEG, np.float32), 1),
        "cos": cos,
        "sin": sin,
    }


_INS = ["L0_attn_data", "L0_attn_mask", "L0_attn_weight", "L0_attn_bias", "L0_ffn_W_base", "L0_ffn_b_base",
        "L0_ffn_W_router", "L0_ffn_A", "L0_ffn_B", "L1_attn_wq", "L1_attn_wk", "L1_attn_wv", "L1_attn_wo",
        "L1_ffn_weight", "L1_ffn_wscale", "L1_ffn_wbias"]


def kernel(**inputs):
    import concourse.bacc as bacc
    from concourse.bass_utils import run_bass_kernel_spmd

    nc = bacc.Bacc("TRN2", target_bir_lowering=False, num_devices=1)
    arrays = {name: np.ascontiguousarray(inputs[name]) for name in _INS}
    arrays.update(shape_constants())
    ins = {name: nc.dram_tensor(f"in_{name}", a.shape, mybir.dt.from_np(a.dtype), kind="ExternalInput").ap()
           for name, a in arrays.items()}
    out = nc.dram_tensor("out", (B, S, D), F32, kind="ExternalOutput").ap()
    program(nc, ins, out)
    result = run_bass_kernel_spmd(nc, [{f"in_{name}": a for name, a in arrays.items()}], core_ids=[0])
    return result.results[0]["out"]
```

```python
from contextlib import ExitStack

import numpy as np

import concourse.bass as bass
from concourse import mybir

F32 = mybir.dt.float32
F32R = mybir.dt.float32r
BF16 = mybir.dt.bfloat16
I32 = mybir.dt.int32
U32 = mybir.dt.uint32
ALU = mybir.AluOpType
ACT = mybir.ActivationFunctionType
AX = mybir.AxisListType

P = 128
D = 512
KC = D // P
B, S = 2, 1024
TILES = B * S // P
E, RANK = 8, 16
ER = E * RANK
BLK = 32
NBLK = KC * D // BLK
EPS = 1e-5
LORA_SCALE = 2.0

LORA_FFN, SPARSE, BIN_FFN, OUT_PROJ = range(4)
BEFORE = (LORA_FFN, SPARSE, LORA_FFN, BIN_FFN)
RESIDUAL = {LORA_FFN: 0.5, SPARSE: 1.0, BIN_FFN: 0.5, OUT_PROJ: 1.0}
LEAD = 4


class Steps:

    def __init__(self, sem):
        self.sem, self.base, self.off = sem, 0, 0

    def step(self, ins):
        self.off += 1
        ins.then_inc(self.sem, 1)

    def wait(self, eng):
        at_least(eng, self.sem, self.base + self.off)

    def then_wait(self, eng, ins):
        self.step(ins)
        self.wait(eng)

    def enter(self, i, per):
        self.start = self.base + self.off
        self.per = per
        self.base, self.off = i * per + self.start, 0

    def leave(self, rounds):
        assert self.off == self.per, (self.off, self.per)
        self.base, self.off = self.start + rounds * self.per, 0


def over_tiles(eng, kinds, tile, steps=None, per=None):
    rounds = (TILES - LEAD) // 2 - 1
    for s in range(len(kinds)):
        for t in (0, 1):
            tile(s, t, s * TILES + t, t % 2)
        with eng.Fori(0, rounds) as i:
            if steps:
                steps.enter(i, per[kinds[s]])
            for p in (0, 1):
                tile(s, i * 2 + (2 + p), i * 2 + (s * TILES + 2 + p), p)
            if steps:
                steps.leave(rounds)
        for t in range(TILES - LEAD, TILES):
            tile(s, t, s * TILES + t, t % 2)


def neighbour(kinds, s, t, k):
    if not isinstance(t, int):
        return s, t + k
    n = s * TILES + t + k
    return (n // TILES, n % TILES) if 0 <= n < len(kinds) * TILES else None


def at_least(eng, sem, value):
    if not isinstance(value, int) or value > 0:
        eng.wait_ge(sem, value)


def prepare_weights(nc, ins, g):
    with ExitStack() as ctx:
        def sb(name, shape, dt=F32):
            return ctx.enter_context(nc.sbuf_tensor(name, shape, dt))

        def sem(name):
            return ctx.enter_context(nc.semaphore(name))

        nat = {k: sb(f"nat_{k}", [P, KC, D]) for k in (LORA_FFN, SPARSE, BIN_FFN)}
        mask = sb("mask_in", [P, KC, D], I32)
        block_sum = sb("block_sum", [P, NBLK])
        block_on = sb("block_on", [P, NBLK])
        same_block = sb("same_block_sb", [P, P])
        nat_a = sb("nat_a", [P, D])
        nat_router = sb("nat_router", [E, D])
        nat_b = sb("nat_b", [P, KC, E, RANK])
        wscale = sb("wscale", [P, KC])
        neg_wscale = sb("neg_wscale", [P, KC])
        wbias = sb("wbias", [P, KC])
        positive = sb("positive", [P, KC, D])
        bank = [ctx.enter_context(nc.psum_tensor(f"wbank{i}", [P, D], F32)) for i in range(6)]
        mask_bank = ctx.enter_context(nc.psum_tensor("mask_bank", [P, D], F32))
        small_bank = ctx.enter_context(nc.psum_tensor("small_bank", [P, KC, P], F32))

        s_const, s_base, s_lora, s_mask, s_bin = (sem(n) for n in (
            "const_loaded", "base_loaded", "lora_loaded", "mask_loaded", "bin_loaded"))
        s_x = sem("x_loaded")
        s_sums, s_onmap, s_nat = sem("mask_sums"), sem("mask_map"), sem("nat_ready")
        s_tr, s_hi, s_lo, s_small, s_small_out = (sem(n) for n in (
            "w_transposed", "w_hi", "w_lo", "lora_transposed", "lora_copied"))
        s_own = sem("prep_vector_own")
        block = ctx.enter_context(nc.Block())
        order = (LORA_FFN, SPARSE, BIN_FFN)

        @block.sync
        def _(sp):
            sp.dma_start(g.ident[:], ins["ident"]).then_inc(s_const, 16)
            sp.dma_start(nat[LORA_FFN][:], ins["L0_ffn_W_base"].rearrange("(c p) k -> p c k", p=P)).then_inc(s_base, 16)
            x = ins["L0_attn_data"].rearrange("b (t p) d -> p (b t) d", p=P)
            for t in range(0, TILES, 4):
                sp.dma_start(g.x[:, t:t + 4, :], x[:, t:t + 4, :]).then_inc(s_x, 16)
            sp.dma_start(nat[SPARSE][:], ins["L0_attn_weight"].rearrange("(c p) k -> p c k", p=P)).then_inc(s_mask, 16)
            sp.dma_start(nat[BIN_FFN][:], ins["L1_ffn_weight"].rearrange("(c p) k -> p c k", p=P)).then_inc(s_bin, 16)
            for n, w in enumerate(("L1_attn_wq", "L1_attn_wk", "L1_attn_wv")):
                sp.dma_start(g.vo[:, n * KC:(n + 1) * KC, :], ins[w].rearrange("(c p) n -> p c n", p=P)).then_inc(g.qkv_loaded, 16)
            sp.wait_ge(s_x, 16 * TILES // 4)

        @block.scalar
        def _(act):
            act.dma_start(nat_a[:], ins["L0_ffn_A"].rearrange("e r k -> (e r) k")).then_inc(s_lora, 16)
            act.dma_start(nat_router[:], ins["L0_ffn_W_router"]).then_inc(s_lora, 16)
            for c in range(KC):
                act.dma_start(nat_b[:, c, :, :], ins["L0_ffn_B"][:, c * P:(c + 1) * P, :].rearrange("e o r -> o e r")).then_inc(s_lora, 16)
            act.dma_start(mask[:], ins["L0_attn_mask"].rearrange("(c p) k -> p c k", p=P)).then_inc(s_mask, 16)
            act.dma_start(same_block[:], ins["same_block"]).then_inc(s_const, 16)
            act.dma_start(g.causal_in[:], ins["causal"]).then_inc(s_const, 16)
            act.dma_start(g.iota[:], ins["iota"].partition_broadcast(P)).then_inc(s_const, 16)
            act.dma_start(g.bias[LORA_FFN][:], ins["L0_ffn_b_base"].partition_broadcast(P)).then_inc(s_const, 16)
            act.dma_start(g.bias[SPARSE][:], ins["L0_attn_bias"].partition_broadcast(P)).then_inc(s_const, 16)
            act.dma_start(wscale[:], ins["L1_ffn_wscale"].rearrange("(c p) o -> p (c o)", p=P), allow_slow_non_contiguous=True).then_inc(s_bin, 16)
            act.dma_start(wbias[:], ins["L1_ffn_wbias"].rearrange("(c p) o -> p (c o)", p=P), allow_slow_non_contiguous=True).then_inc(s_bin, 16)
            for n, kind in enumerate(order):
                for c in range(KC):
                    u = n * KC + c
                    act.wait_ge(s_tr, u + 1)
                    nc.scalar.copy(g.w_hi[kind][:, c, :], bank[u % 6][:]).then_inc(s_hi, 1)

        @block.tensor
        def _(pe):
            pe.wait_ge(s_const, 96)

            def transposed(n, kind):
                for c in range(KC):
                    u = n * KC + c
                    if u >= 6:
                        pe.wait_ge(s_lo, u - 5)
                    for i in range(KC):
                        last = nc.tensor.transpose(bank[u % 6][:, i * P:(i + 1) * P],
                                                   nat[kind][:, i, c * P:(c + 1) * P], g.ident[:])
                    last.then_inc(s_tr, 1)

            pe.wait_ge(s_base, 16)
            transposed(0, LORA_FFN)
            pe.wait_ge(s_lora, 96)
            for c in range(KC):
                last = nc.tensor.transpose(small_bank[:, c, :], nat_a[:, c * P:(c + 1) * P], g.ident[:])
            last.then_inc(s_small, 1)
            pe.wait_ge(s_small_out, 1)
            for c in range(KC):
                last = nc.tensor.transpose(small_bank[:, c, 0:E], nat_router[:, c * P:(c + 1) * P], g.ident[0:E, 0:E])
            last.then_inc(s_small, 1)
            pe.wait_ge(s_small_out, 2)
            for c in range(KC):
                last = nc.tensor.transpose(small_bank[:, c, :],
                                           nat_b[:, c, :, :].rearrange("p e r -> p (e r)"), g.ident[:])
            last.then_inc(s_small, 1)
            pe.wait_ge(s_sums, 1)
            nc.tensor.matmul(mask_bank[:, 0:NBLK], same_block[:], block_sum[:], start=True, stop=True).then_inc(s_onmap, 1)
            pe.wait_ge(s_nat, 1)
            transposed(1, SPARSE)
            pe.wait_ge(s_nat, 2)
            transposed(2, BIN_FFN)

        @block.vector
        def _(dve):
            own = Steps(s_own)

            def rest_of(n, kind):
                for c in range(KC):
                    u = n * KC + c
                    dve.wait_ge(s_hi, u + 1)
                    nc.vector.tensor_tensor(g.w_lo[kind][:, c, :], bank[u % 6][:],
                                            g.w_hi[kind][:, c, :].bitcast(F32), ALU.subtract).then_inc(s_lo, 1)

            dve.wait_ge(s_const, 96)
            own.then_wait(dve, nc.vector.tensor_scalar(g.bias[LORA_FFN][:], g.bias[LORA_FFN][:], 0.5, None, ALU.mult))
            rest_of(0, LORA_FFN)
            dve.wait_ge(s_small, 1)
            nc.vector.tensor_copy(g.ra[:, :, E:E + ER], small_bank[:]).then_inc(s_small_out, 1)
            dve.wait_ge(s_small, 2)
            nc.vector.tensor_copy(g.ra[:, :, 0:E], small_bank[:, :, 0:E]).then_inc(s_small_out, 1)
            dve.wait_ge(s_small, 3)
            up = small_bank[:].rearrange("p c n -> p (c n)")
            own.then_wait(dve, nc.vector.tensor_copy(g.up_hi[:], up))
            own.then_wait(dve, nc.vector.tensor_tensor(g.up_lo[:], up, g.up_hi[:].bitcast(F32), ALU.subtract))
            dve.wait_ge(s_mask, 32)
            nc.vector.tensor_reduce(block_sum[:], mask[:].rearrange("p c (b w) -> p (c b) w", w=BLK), AX.X, ALU.add).then_inc(s_sums, 1)
            dve.wait_ge(s_onmap, 1)
            own.then_wait(dve, nc.vector.tensor_scalar(block_on[:], mask_bank[:, 0:NBLK], 0.0, None, ALU.is_gt))
            w = nat[SPARSE][:].rearrange("p c (b w) -> p (c b) w", w=BLK)
            nc.vector.tensor_tensor(w, w, block_on[:].unsqueeze(2).broadcast_to((P, NBLK, BLK)), ALU.mult).then_inc(s_nat, 1)
            dve.wait_ge(s_bin, 48)
            own.then_wait(dve, nc.vector.tensor_scalar(neg_wscale[:], wscale[:], -1.0, None, ALU.mult))
            w = nat[BIN_FFN]
            own.then_wait(dve, nc.vector.tensor_scalar(positive[:], w[:], 0.0, None, ALU.is_gt))
            for c in range(KC):
                own.then_wait(dve, nc.vector.scalar_tensor_tensor(w[:, c, :], w[:, c, :], 0.0, positive[:, c, :], ALU.is_lt, ALU.subtract))
            for c in range(KC):
                ins_ = nc.vector.tensor_scalar(w[:, c, :], w[:, c, :], neg_wscale[:, c:c + 1], wbias[:, c:c + 1], ALU.mult, ALU.add)
            ins_.then_inc(s_nat, 1)
            rest_of(1, SPARSE)
            rest_of(2, BIN_FFN)


def dense_stages(nc, g, kinds, tag, out=None):
    with ExitStack() as ctx:
        def sb(name, shape, dt=F32):
            return ctx.enter_context(nc.sbuf_tensor(f"{tag}_{name}", shape, dt))

        def psum(name, shape):
            return ctx.enter_context(nc.psum_tensor(f"{tag}_{name}", shape, F32))

        def sem(name):
            return ctx.enter_context(nc.semaphore(f"{tag}_{name}"))

        lora = [k == LORA_FFN for k in kinds]
        normed = [k != OUT_PROJ for k in kinds]
        has_lora = any(lora)
        stats = [sb(f"stats{p}", [P, 6]) for p in range(2)]
        mean_var = [sb(f"mean_var{p}", [P, 2]) for p in range(2)]
        var_eps = [sb(f"var_eps{p}", [P, 1]) for p in range(2)]
        rstd = [sb(f"rstd{p}", [P, 1]) for p in range(2)]
        neg_half = sb("neg_half", [P, 1])
        eps = sb("eps", [P, 1])
        xn = [sb(f"xn{p}", [P, D]) for p in range(2)]
        xt_hi = [sb(f"xt_hi{p}", [P, KC, P], F32R) for p in range(2)]
        xt_lo = [sb(f"xt_lo{p}", [P, KC, P], F32R) for p in range(2)]
        xt_bank = [psum(f"xt_bank{p}", [P, KC, P]) for p in range(2)]
        y_bank = [psum(f"y_bank{p}", [P, D]) for p in range(2)]
        if has_lora:
            xt_sum = [sb(f"xt_sum{p}", [P, KC, P]) for p in range(2)]
            ra_bank = [psum(f"ra_bank{p}", [P, E + ER]) for p in range(2)]
            hw_bank = [psum(f"hw_bank{p}", [P, P]) for p in range(2)]
            top = [sb(f"top{p}", [P, 8]) for p in range(2)]
            top_at = [sb(f"top_at{p}", [P, 8], U32) for p in range(2)]
            top_atf = [sb(f"top_atf{p}", [P, 2]) for p in range(2)]
            ratio = [sb(f"ratio{p}", [P, 1]) for p in range(2)]
            gate = [sb(f"gate{p}", [P, 3]) for p in range(2)]
            share = [sb(f"share{p}", [P, 3, E]) for p in range(2)]
            logits = [sb(f"logits{p}", [P, E]) for p in range(2)]
            hw = [sb(f"hw{p}", [P, E, RANK]) for p in range(2)]
            hwt_hi = [sb(f"hwt_hi{p}", [P, P], F32R) for p in range(2)]
            hwt_lo = [sb(f"hwt_lo{p}", [P, P], F32R) for p in range(2)]

        mv_ready, rstd_ready, xn_ready, xt_ready, hi_ready, lo_ready = (sem(n) for n in (
            "mv_ready", "rstd_ready", "xn_ready", "xt_ready", "hi_ready", "lo_ready"))
        bias_in, multiplied, y_ready, x_done = sem("bias_in"), sem("multiplied"), sem("y_ready"), sem("x_done")
        sum_ready, ra_ready, ratio_ready, hw_ready, hwt_ready, hwt_hi_ready, hwt_lo_ready, top_ready = (sem(n) for n in (
            "sum_ready", "ra_ready", "ratio_ready", "hw_ready", "hwt_ready", "hwt_hi_ready", "hwt_lo_ready", "top_ready"))
        own_vector, own_pool = sem("own_vector"), sem("own_pool")
        block = ctx.enter_context(nc.Block())
        last_tile = len(kinds) * TILES

        if out is not None:
            stored = sem("stored")
            rows = out.rearrange("b (t p) d -> p (b t) d", p=P)

            @block.sync
            def _(sp):
                with sp.Fori(0, TILES) as t:
                    sp.wait_ge(x_done, t + (last_tile - TILES + 1))
                    sp.dma_start(rows[:, t, :], g.x[:, t, :]).then_inc(stored, 16)
                sp.wait_ge(stored, 16 * TILES)

        def normed_before(s):
            return sum(TILES for k in range(s) if normed[k]) - s * TILES

        def experts_before(s):
            return sum(TILES for k in range(s) if lora[k]) - s * TILES

        @block.tensor
        def _(pe):
            def transpose_x(s, t, T, p):
                pe.wait_ge(xn_ready, T + 1)
                at_least(pe, lo_ready, T - 1)
                for c in range(KC):
                    last = nc.tensor.transpose(xt_bank[p][:, c, :], xn[p][:, c * P:(c + 1) * P], g.ident[:])
                last.then_inc(xt_ready, 1)

            def experts_down(s, T, p):
                L = T + experts_before(s)
                pe.wait_ge(sum_ready, L + 1)
                at_least(pe, hw_ready, L - 1)
                for c in range(KC):
                    last = nc.tensor.matmul(ra_bank[p][:], xt_sum[p][:, c, :], g.ra[:, c, :],
                                            start=(c == 0), stop=(c == KC - 1))
                last.then_inc(ra_ready, 1)

            def transpose_hw(s, T, p):
                L = T + experts_before(s)
                pe.wait_ge(hw_ready, L + 1)
                at_least(pe, hwt_lo_ready, L - 1)
                nc.tensor.transpose(hw_bank[p][:], hw[p][:].rearrange("p e r -> p (e r)"), g.ident[:]).then_inc(hwt_ready, 1)

            def project(s, T, p):
                pe.wait_ge(lo_ready, T + 1)
                at_least(pe, x_done, T - 1)
                k = kinds[s]
                for c in range(KC):
                    nc.tensor.matmul(y_bank[p][:], xt_lo[p][:, c, :], g.w_hi[k][:, c, :], start=(c == 0), stop=False)
                    nc.tensor.matmul(y_bank[p][:], xt_hi[p][:, c, :], g.w_lo[k][:, c, :], start=False, stop=False)
                    last = nc.tensor.matmul(y_bank[p][:], xt_hi[p][:, c, :], g.w_hi[k][:, c, :],
                                            start=False, stop=(c == KC - 1 and not lora[s]))
                last.then_inc(multiplied, 1)

            def experts_up(s, T, p):
                L = T + experts_before(s)
                pe.wait_ge(hwt_lo_ready, L + 1)
                nc.tensor.matmul(y_bank[p][:], hwt_lo[p][:], g.up_hi[:], start=False, stop=False)
                nc.tensor.matmul(y_bank[p][:], hwt_hi[p][:], g.up_lo[:], start=False, stop=False)
                nc.tensor.matmul(y_bank[p][:], hwt_hi[p][:], g.up_hi[:], start=False, stop=True).then_inc(y_ready, 1)

            def tile(s, t, T, p):
                if lora[s]:
                    experts_down(s, T, p)
                back = neighbour(kinds, s, t, -1)
                back_lora = back is not None and lora[back[0]]
                if back_lora:
                    transpose_hw(back[0], T - 1, 1 - p)
                on = neighbour(kinds, s, t, 2)
                if on is not None:
                    transpose_x(on[0], on[1], T + 2, p)
                project(s, T, p)
                if back_lora:
                    experts_up(back[0], T - 1, 1 - p)

            transpose_x(0, 0, 0, 0)
            transpose_x(0, 1, 1, 1)
            over_tiles(pe, kinds, tile)
            if lora[-1]:
                transpose_hw(len(kinds) - 1, last_tile - 1, 1)
                experts_up(len(kinds) - 1, last_tile - 1, 1)

        @block.scalar
        def _(act):
            def round_x(s, T, p):
                act.wait_ge(xt_ready, T + 1)
                at_least(act, multiplied, T - 1)
                if lora[s]:
                    L = T + experts_before(s)
                    at_least(act, ra_ready, L - 1)
                    nc.scalar.copy(xt_sum[p][:], xt_bank[p][:]).then_inc(sum_ready, 1)
                nc.scalar.copy(xt_hi[p][:], xt_bank[p][:]).then_inc(hi_ready, 1)

            def tile(s, t, T, p):
                on = neighbour(kinds, s, t, 1)
                if on is not None:
                    round_x(on[0], T + 1, 1 - p)
                back = neighbour(kinds, s, t, -1)
                if back is not None and lora[back[0]]:
                    L = T - 1 + experts_before(back[0])
                    act.wait_ge(hwt_ready, L + 1)
                    nc.scalar.copy(hwt_hi[1 - p][:], hw_bank[1 - p][:]).then_inc(hwt_hi_ready, 1)
                if lora[s]:
                    L = T + experts_before(s)
                    act.wait_ge(top_ready, L + 1)
                    nc.scalar.activation(ratio[p][:], top[p][:, 0:1], ACT.Exp, bias=top[p][:, 1:2], scale=-1.0).then_inc(ratio_ready, 1)

            round_x(0, 0, 0)
            over_tiles(act, kinds, tile)

        @block.gpsimd
        def _(pool):
            own = Steps(own_pool)
            nc.gpsimd.memset(eps[:], EPS)
            own.then_wait(pool, nc.gpsimd.memset(neg_half[:], -0.5))

            def inverse_deviation(s, T, p):
                if not normed[s]:
                    return
                pool.wait_ge(mv_ready, T + normed_before(s) + 1)
                at_least(pool, xn_ready, T - 1)
                own.then_wait(pool, nc.gpsimd.tensor_tensor(var_eps[p][:], mean_var[p][:, 1:2], eps[:], ALU.add))
                nc.gpsimd.tensor_tensor(rstd[p][:], var_eps[p][:], neg_half[:], ALU.pow).then_inc(rstd_ready, 1)

            def tile(s, t, T, p):
                on = neighbour(kinds, s, t, LEAD)
                if on is not None:
                    inverse_deviation(on[0], T + LEAD, p)
                if kinds[s] in g.bias:
                    pool.wait_ge(xn_ready, T + 1)
                    nc.gpsimd.tensor_tensor(g.x[:, t, :], g.x[:, t, :], g.bias[kinds[s]][:], ALU.add).then_inc(bias_in, 1)

            for T in range(LEAD):
                inverse_deviation(0, T, T % 2)
            over_tiles(pool, kinds, tile, own, {k: 2 * (k != OUT_PROJ) for k in kinds})

        @block.vector
        def _(dve):
            own = Steps(own_vector)

            def statistics(s, t, T, p):
                if normed[s]:
                    if s:
                        dve.wait_ge(x_done, T - TILES + 1)
                    own.step(nc.vector.bn_stats(stats[p][:], g.x[:, t, :]))

            def mean_and_variance(s, p):
                if normed[s]:
                    nc.vector.bn_aggr(mean_var[p][:], stats[p][:]).then_inc(mv_ready, 1)

            def normalise(s, t, T, p):
                at_least(dve, xt_ready, T - 1)
                if not normed[s]:
                    nc.vector.tensor_copy(xn[p][:], g.vo[:, t, :]).then_inc(xn_ready, 1)
                    return
                dve.wait_ge(rstd_ready, T + normed_before(s) + 1)
                nc.vector.tensor_scalar(xn[p][:], g.x[:, t, :], mean_var[p][:, 0:1], rstd[p][:], ALU.subtract, ALU.mult).then_inc(xn_ready, 1)

            def rest_of_x(T, p):
                dve.wait_ge(hi_ready, T + 1)
                nc.vector.tensor_tensor(xt_lo[p][:], xt_bank[p][:], xt_hi[p][:].bitcast(F32), ALU.subtract).then_inc(lo_ready, 1)

            def rest_of_hw(s, T, p):
                L = T + experts_before(s)
                dve.wait_ge(hwt_hi_ready, L + 1)
                nc.vector.tensor_tensor(hwt_lo[p][:], hw_bank[p][:], hwt_hi[p][:].bitcast(F32), ALU.subtract).then_inc(hwt_lo_ready, 1)

            def copy_logits(s, T, p):
                L = T + experts_before(s)
                dve.wait_ge(ra_ready, L + 1)
                at_least(dve, ratio_ready, L - 1)
                own.then_wait(dve, nc.vector.tensor_copy(logits[p][:], ra_bank[p][:, 0:E]))

            def gates(s, T, p):
                L = T + experts_before(s)
                own.wait(dve)
                own.then_wait(dve, nc.vector.tensor_copy(top_atf[p][:], top_at[p][:, 0:2]))
                dve.wait_ge(ratio_ready, L + 1)
                own.then_wait(dve, nc.vector.tensor_scalar(gate[p][:, 0:1], ratio[p][:], 1.0, None, ALU.add))
                own.then_wait(dve, nc.vector.reciprocal(gate[p][:, 1:2], gate[p][:, 0:1]))
                own.then_wait(dve, nc.vector.tensor_tensor(gate[p][:, 2:3], gate[p][:, 1:2], ratio[p][:], ALU.mult))
                nc.vector.tensor_scalar(share[p][:, 0, :], g.iota[:], top_atf[p][:, 0:1], gate[p][:, 1:2], ALU.is_equal, ALU.mult)
                own.then_wait(dve, nc.vector.tensor_scalar(share[p][:, 1, :], g.iota[:], top_atf[p][:, 1:2], gate[p][:, 2:3], ALU.is_equal, ALU.mult))
                own.then_wait(dve, nc.vector.tensor_tensor(share[p][:, 2, :], share[p][:, 0, :], share[p][:, 1, :], ALU.add))
                at_least(dve, hwt_ready, L - 1)
                nc.vector.scalar_tensor_tensor(hw[p][:], ra_bank[p][:, E:E + ER].rearrange("p (e r) -> p e r", e=E), LORA_SCALE,
                                               share[p][:, 2, :].unsqueeze(2).broadcast_to((P, E, RANK)),
                                               ALU.mult, ALU.mult).then_inc(hw_ready, 1)

            def add_to_x(s, t, T, p):
                if lora[s]:
                    dve.wait_ge(y_ready, T + experts_before(s) + 1)
                else:
                    dve.wait_ge(multiplied, T + 1)
                n = sum(TILES for k in range(s) if kinds[k] in g.bias) - s * TILES
                if kinds[s] in g.bias:
                    dve.wait_ge(bias_in, T + n + 1)
                nc.vector.scalar_tensor_tensor(g.x[:, t, :], y_bank[p][:], RESIDUAL[kinds[s]], g.x[:, t, :], ALU.mult, ALU.add).then_inc(x_done, 1)

            def tile(s, t, T, p):
                on = neighbour(kinds, s, t, 1)
                if on is not None:
                    rest_of_x(T + 1, 1 - p)
                back = neighbour(kinds, s, t, -1)
                if back is not None and lora[back[0]]:
                    rest_of_hw(back[0], T - 1, 1 - p)
                if lora[s]:
                    copy_logits(s, T, p)
                far, near = neighbour(kinds, s, t, 4), neighbour(kinds, s, t, 3)
                if far is not None:
                    statistics(far[0], far[1], T + 4, p)
                if lora[s]:
                    nc.vector.max(top[p][:], logits[p][:]).then_inc(top_ready, 1)
                    dve.wait_ge(top_ready, T + experts_before(s) + 1)
                if lora[s] or (far is not None and normed[far[0]]):
                    own.wait(dve)
                if near is not None:
                    normalise(near[0], near[1], T + 3, 1 - p)
                if lora[s]:
                    own.step(nc.vector.max_index(top_at[p][:], top[p][:], logits[p][:]))
                if far is not None:
                    mean_and_variance(far[0], p)
                if lora[s]:
                    gates(s, T, p)
                if back is not None:
                    add_to_x(back[0], back[1], T - 1, 1 - p)

            def both(T):
                statistics(0, T, T, T % 2)
                if normed[0]:
                    own.wait(dve)
                mean_and_variance(0, T % 2)

            both(0)
            both(1)
            for T in range(3):
                normalise(0, T, T, T % 2)
                if T < 2:
                    both(T + 2)
            rest_of_x(0, 0)
            own_per = {k: 2 * (k != OUT_PROJ) + 16 * (k == LORA_FFN) for k in kinds}
            over_tiles(dve, kinds, tile, own, own_per)
            if lora[-1]:
                rest_of_hw(len(kinds) - 1, last_tile - 1, 1)
            add_to_x(len(kinds) - 1, TILES - 1, last_tile - 1, 1)


def project_qkv(nc, g):
    SUPER = 4
    TOK = SUPER * P
    HALF = S // P // SUPER
    AHEAD = SUPER + 2
    with ExitStack() as ctx:
        def sb(name, shape, dt=F32):
            return ctx.enter_context(nc.sbuf_tensor(f"qkv_{name}", shape, dt))

        def psum(name, shape):
            return ctx.enter_context(nc.psum_tensor(f"qkv_{name}", shape, F32))

        def sem(name):
            return ctx.enter_context(nc.semaphore(f"qkv_{name}"))

        w_hi = {w: sb(f"w_hi_{w}", [P, KC, D], F32R) for w in "qkv"}
        w_lo = {w: sb(f"w_lo_{w}", [P, KC, D], F32R) for w in "qkv"}
        cos = sb("cos", [P, S])
        sin = sb("sin", [P, S])
        stats = [sb(f"stats{i}", [P, 6]) for i in range(4)]
        mean_var = [sb(f"mean_var{i}", [P, 2]) for i in range(4)]
        var_eps = [sb(f"var_eps{p}", [P, 1]) for p in range(2)]
        rstd = [sb(f"rstd{p}", [P, 1]) for p in range(2)]
        neg_half = sb("neg_half", [P, 1])
        eps = sb("eps", [P, 1])
        xn = [sb(f"xn{p}", [P, D]) for p in range(2)]
        xt_hi = [sb(f"xt_hi{u}", [P, KC, TOK], F32R) for u in range(HALF)]
        xt_lo = [sb(f"xt_lo{u}", [P, KC, TOK], F32R) for u in range(HALF)]
        prod = [sb(f"prod{p}", [P, 4, TOK]) for p in range(2)]
        parts = [sb(f"parts{p}", [P, 2, 3, TOK], BF16) for p in range(2)]
        xt_bank = [psum(f"xt_bank{p}", [P, KC, P]) for p in range(2)]
        v_bank = [psum(f"v_bank{p}", [P, D]) for p in range(2)]
        pair_bank = [[psum(f"pair_bank{p}{e}", [P, TOK]) for e in range(2)] for p in range(2)]

        tables_loaded, w_hi_ready, w_lo_ready = sem("tables"), sem("w_hi"), sem("w_lo")
        mv_ready, rstd_ready, xn_ready, xt_ready, hi_ready, lo_ready, v_ready, v_copied = tile_counts = [sem(n) for n in (
            "mv_ready", "rstd_ready", "xn_ready", "xt_ready", "hi_ready", "lo_ready", "v_ready", "v_copied")]
        pair_ready, products, rotated, high, rest, middle, low = pair_counts = [sem(n) for n in (
            "pair_ready", "products", "rotated", "high", "rest", "middle", "low")]
        stored = [sem(f"stored{p}") for p in range(2)]
        own_vector, own_pool = sem("own_vector"), sem("own_pool")
        START = 2
        block = ctx.enter_context(nc.Block())
        SLOTS = SUPER * HALF
        PAIRS = [("q", 0), ("q", 1), ("k", 0), ("k", 1)]
        STORES = 6 * 16

        def batches(eng, body, steps=None, per=0):
            with eng.Fori(0, B) as b:
                if steps:
                    steps.enter(b, per)
                body(b)
                if steps:
                    steps.leave(B)

        def tile_of(b, m):
            if isinstance(b, int) or m < SLOTS:
                return b * SLOTS + m
            return (1 - b) * SLOTS + (m - SLOTS)

        def xt_place(m):
            return (m // SUPER) % 2, slice(m % SUPER * P, (m % SUPER + 1) * P)

        @block.sync
        def _(sp):
            for count in tile_counts + pair_counts + stored:
                sp.sem_inc(count, START)
            sp.dma_start(cos[:], g.cos_in).then_inc(tables_loaded, 16)
            sp.dma_start(sin[:], g.sin_in).then_inc(tables_loaded, 16)

            def body(b):
                for n in range(SLOTS):
                    N, p = b * SLOTS + n, n % 2
                    u, (which, half) = n // SUPER, PAIRS[n % SUPER]
                    sp.wait_ge(low, N + (START + 1))
                    rows = g.scratch[which].rearrange("c (h e f) t -> e c h f t", e=2, f=8)
                    for e in range(2):
                        for c in range(3):
                            dst = rows[e, c, half * 16:(half + 1) * 16, :, bass.ds(b * S + u * TOK, TOK)]
                            sp.dma_start(dst, parts[p][:, e, c, :]).then_inc(stored[p], 16)

            batches(sp, body)
            for p in range(2):
                sp.wait_ge(stored[p], B * SLOTS // 2 * STORES + START)

        @block.scalar
        def _(act):
            act.wait_ge(g.qkv_loaded, 48)
            for n, w in enumerate("qkv"):
                for c in range(KC):
                    nc.scalar.copy(split_view(w_hi[w], w, c), raw_view(g, n, w, c)).then_inc(w_hi_ready, 1)

            def round_x(N, m):
                act.wait_ge(xt_ready, N + (START + 1))
                if m % SUPER == 0 and m >= SUPER:
                    act.wait_ge(pair_ready, N + (START - SUPER))
                u, t = xt_place(m)
                nc.scalar.copy(xt_hi[u][:, :, t], xt_bank[m % 2][:]).then_inc(hi_ready, 1)

            def high_and_middle(N, n):
                p = n % 2
                act.wait_ge(rotated, N + (START + 1))
                act.wait_ge(stored[p], (N - n) * (STORES // 2) + (n // 2 * STORES + START))
                nc.scalar.copy(parts[p][:, :, 0, :], prod[p][:, 0:2, :]).then_inc(high, 1)
                act.wait_ge(rest, N + (START + 1))
                nc.scalar.copy(parts[p][:, :, 1, :], prod[p][:, 2:4, :]).then_inc(middle, 1)

            def body(b):
                for n in range(SLOTS):
                    N, p = b * SLOTS + n, n % 2
                    act.wait_ge(v_ready, N + (START + 1))
                    nc.scalar.copy(g.vo[:, N, :], v_bank[p][:]).then_inc(v_copied, 1)
                    if n:
                        high_and_middle(N - 1, n - 1)
                    round_x(N + SUPER, n + SUPER)
                high_and_middle(N, SLOTS - 1)

            for m in range(SUPER):
                round_x(m, m)
            batches(act, body)

        @block.tensor
        def _(pe):
            def turn(N, m):
                pe.wait_ge(xn_ready, N + (START + 1))
                pe.wait_ge(lo_ready, N + (START - 1))
                for c in range(KC):
                    last = nc.tensor.transpose(xt_bank[m % 2][:, c, :], xn[m % 2][:, c * P:(c + 1) * P], g.ident[:])
                last.then_inc(xt_ready, 1)

            def body(b):
                for n in range(SLOTS):
                    N, p = b * SLOTS + n, n % 2
                    u, t = xt_place(n)
                    turn(N + SUPER, n + SUPER)
                    pe.wait_ge(lo_ready, N + (START + 1))
                    pe.wait_ge(v_copied, N + (START - 1))
                    for c in range(KC):
                        nc.tensor.matmul(v_bank[p][:], xt_lo[u][:, c, t], w_hi["v"][:, c, :], start=(c == 0), stop=False)
                        nc.tensor.matmul(v_bank[p][:], xt_hi[u][:, c, t], w_lo["v"][:, c, :], start=False, stop=False)
                        last = nc.tensor.matmul(v_bank[p][:], xt_hi[u][:, c, t], w_hi["v"][:, c, :], start=False, stop=(c == KC - 1))
                    last.then_inc(v_ready, 1)
                    if n % SUPER == 0:
                        pe.wait_ge(lo_ready, N + (START + SUPER))
                    pe.wait_ge(products, N + (START - 1))
                    which, half = PAIRS[n % SUPER]
                    for e in range(2):
                        f = slice((half * 2 + e) * P, (half * 2 + e + 1) * P)
                        for c in range(KC):
                            nc.tensor.matmul(pair_bank[p][e][:], w_lo[which][:, c, f], xt_hi[u][:, c, :], start=(c == 0), stop=False)
                            nc.tensor.matmul(pair_bank[p][e][:], w_hi[which][:, c, f], xt_lo[u][:, c, :], start=False, stop=False)
                            last = nc.tensor.matmul(pair_bank[p][e][:], w_hi[which][:, c, f], xt_hi[u][:, c, :], start=False, stop=(c == KC - 1))
                    last.then_inc(pair_ready, 1)

            for m in range(SUPER):
                turn(m, m)
            pe.wait_ge(w_lo_ready, 3 * KC)
            batches(pe, body)

        @block.gpsimd
        def _(pool):
            own = Steps(own_pool)
            nc.gpsimd.memset(eps[:], EPS)
            own.then_wait(pool, nc.gpsimd.memset(neg_half[:], -0.5))

            def inverse_deviation(N, m):
                p = m % 2
                pool.wait_ge(mv_ready, N + (START + 1))
                pool.wait_ge(xn_ready, N + (START - 1))
                own.then_wait(pool, nc.gpsimd.tensor_tensor(var_eps[p][:], mean_var[m % 4][:, 1:2], eps[:], ALU.add))
                nc.gpsimd.tensor_tensor(rstd[p][:], var_eps[p][:], neg_half[:], ALU.pow).then_inc(rstd_ready, 1)

            def low_part(N, n):
                p = n % 2
                pool.wait_ge(middle, N + (START + 1))
                nc.gpsimd.tensor_tensor(parts[p][:, :, 2, :], prod[p][:, 2:4, :], parts[p][:, :, 1, :], ALU.subtract).then_inc(low, 1)

            def body(b):
                for n in range(SLOTS):
                    N, p = b * SLOTS + n, n % 2
                    inverse_deviation(N + AHEAD, n + AHEAD)
                    if n:
                        low_part(N - 1, n - 1)
                    pool.wait_ge(products, N + (START + 1))
                    nc.gpsimd.tensor_tensor(prod[p][:, 0, :], prod[p][:, 0, :], prod[p][:, 2, :], ALU.subtract)
                    nc.gpsimd.tensor_tensor(prod[p][:, 1, :], prod[p][:, 1, :], prod[p][:, 3, :], ALU.add).then_inc(rotated, 1)
                low_part(N, SLOTS - 1)

            for m in range(AHEAD):
                inverse_deviation(m, m)
            batches(pool, body, own, SLOTS)

        @block.vector
        def _(dve):
            own = Steps(own_vector)
            for n, w in enumerate("qkv"):
                for c in range(KC):
                    dve.wait_ge(w_hi_ready, n * KC + c + 1)
                    nc.vector.tensor_tensor(split_view(w_lo[w], w, c), raw_view(g, n, w, c), split_view(w_hi[w], w, c).bitcast(F32), ALU.subtract).then_inc(w_lo_ready, 1)
            dve.wait_ge(tables_loaded, 32)

            def statistics(N, n):
                own.step(nc.vector.bn_stats(stats[n % 4][:], g.x[:, N, :]))

            def mean_and_variance(n):
                nc.vector.bn_aggr(mean_var[n % 4][:], stats[n % 4][:]).then_inc(mv_ready, 1)

            def normalise(N, xi, m):
                dve.wait_ge(rstd_ready, N + (START + 1))
                dve.wait_ge(xt_ready, N + (START - 1))
                nc.vector.tensor_scalar(xn[m % 2][:], g.x[:, xi, :], mean_var[m % 4][:, 0:1], rstd[m % 2][:], ALU.subtract, ALU.mult).then_inc(xn_ready, 1)

            def split(N, m):
                u, t = xt_place(m)
                dve.wait_ge(hi_ready, N + (START + 1))
                nc.vector.tensor_tensor(xt_lo[u][:, :, t], xt_bank[m % 2][:], xt_hi[u][:, :, t].bitcast(F32), ALU.subtract).then_inc(lo_ready, 1)

            def rest_of(N, n):
                p = n % 2
                dve.wait_ge(high, N + (START + 1))
                nc.vector.tensor_tensor(prod[p][:, 2:4, :], prod[p][:, 0:2, :], parts[p][:, :, 0, :], ALU.subtract).then_inc(rest, 1)

            def body(b):
                for n in range(SLOTS):
                    N, p = b * SLOTS + n, n % 2
                    statistics(tile_of(b, n + AHEAD), n + AHEAD)
                    own.wait(dve)
                    m = n + AHEAD - 1
                    normalise(N + (AHEAD - 1), tile_of(b, m), m)
                    mean_and_variance(n + AHEAD)
                    if n:
                        rest_of(N - 1, n - 1)
                    split(N + SUPER, n + SUPER)
                    u = n // SUPER
                    tok = slice(u * TOK, (u + 1) * TOK)
                    dve.wait_ge(pair_ready, N + (START + 1))
                    dve.wait_ge(low, N + (START - 1))
                    even, odd = pair_bank[p]
                    nc.vector.tensor_tensor(prod[p][:, 0, :], even[:], cos[:, tok], ALU.mult)
                    nc.vector.tensor_tensor(prod[p][:, 1, :], even[:], sin[:, tok], ALU.mult)
                    nc.vector.tensor_tensor(prod[p][:, 2, :], odd[:], sin[:, tok], ALU.mult)
                    nc.vector.tensor_tensor(prod[p][:, 3, :], odd[:], cos[:, tok], ALU.mult).then_inc(products, 1)
                rest_of(N, SLOTS - 1)

            for m in range(AHEAD + 1):
                if m < AHEAD:
                    statistics(m, m)
                    own.wait(dve)
                if m:
                    normalise(m - 1, m - 1, m - 1) if m - 1 < AHEAD - 1 else None
                if m < AHEAD:
                    mean_and_variance(m)
                if 2 <= m < SUPER + 2:
                    split(m - 2, m - 2)
            batches(dve, body, own, SLOTS)


def raw_view(g, n, w, c):
    raw = g.vo[:, n * KC + c, :]
    return raw if w == "v" else raw.rearrange("p (a m e) -> p a e m", a=2, e=2)


def split_view(weight, w, c):
    part = weight[:, c, :]
    return part if w == "v" else part.rearrange("p (a e m) -> p a e m", a=2, e=2)


HEADS, HD = 32, 16
GH = 4
GROUPS = B * HEADS // GH
QT = S // P
ROWS = 6 * HD
NEG = -3.0e38


def attention(nc, g):
    NBUF = 3
    NBANK = 3
    with ExitStack() as ctx:
        def sb(name, shape, dt=F32):
            return ctx.enter_context(nc.sbuf_tensor(f"att_{name}", shape, dt))

        def sem(name):
            return ctx.enter_context(nc.semaphore(f"att_{name}"))

        q_rows = [sb(f"q_rows{i}", [P, GH, S], BF16) for i in range(NBUF)]
        k_rows = [sb(f"k_rows{i}", [P, GH, S], BF16) for i in range(NBUF)]
        v_rows = [sb(f"v_rows{i}", [P, QT, GH, 32]) for i in range(NBUF)]
        probs = [sb(f"probs{i}", [P, GH, S]) for i in range(2)]
        o_t = sb("o_t", [P, S])
        part_max = sb("part_max", [P, GH, QT, 2])
        row_max = sb("row_max", [P, GH * QT])
        neg_rest = sb("neg_rest", [P, 2, GH * QT])
        neg_parts = sb("neg_parts", [P, 3, GH * QT], BF16)
        neg_turned = sb("neg_turned", [3 * GH * QT, P], BF16)
        inv_sum = sb("inv_sum", [P, 2, QT // 2 * GH])
        ident_b = sb("ident_b", [P, P], BF16)
        causal = sb("causal", [P, P], BF16)
        scores = [ctx.enter_context(nc.psum_tensor(f"att_scores{i}", [P, D], F32)) for i in range(NBANK)]
        ring = [ctx.enter_context(nc.psum_tensor(f"att_ring{i}", [P, D], F32)) for i in range(NBANK)]
        o_bank = [ctx.enter_context(nc.psum_tensor(f"att_o{i}", [P, D], F32)) for i in range(2)]

        ready = sem("constants")
        rows_loaded = [sem(f"rows_loaded{i}") for i in range(NBUF)]
        max_loaded = [sem(f"max_loaded{i}") for i in range(NBUF)]
        scored, exped, valued, v_ready = (sem(n) for n in ("scored", "exped", "valued", "v_ready"))
        o_copied, ring_ready, ring_done, neg_ready = (sem(n) for n in ("o_copied", "ring_ready", "ring_done", "neg_ready"))
        own_vector, own_pool = sem("own_vector"), sem("own_pool")
        block = ctx.enter_context(nc.Block())

        UNITS = [(h, i, half) for h in range(GH) for i in range(QT) for half in range(1 + (i >= QT // 2))]
        NU = len(UNITS)
        HU = NU // 2
        KEYED = [(j, h, half) for j in range(QT) for h in range(GH) for half in range(j // (QT // 2), 2)]
        NK = len(KEYED)
        ROUND = NU + 3
        assert NK % NBANK == 0 and ROUND % NBANK == 0 and HU % NBANK == 0
        LOADS = 12 * 16

        def keyed_until(j):
            return sum(1 for u in KEYED if u[0] <= j)

        def queries(j, half):
            return max(j * P, half * D), (half + 1) * D

        def keys(i, half):
            return min((i + 1) * P - half * D, D)

        def ring_base(G):
            ahead_of_all = NU + 1 + HU
            if isinstance(G, int) and G == 0:
                return ahead_of_all
            return G * ROUND + (ahead_of_all - 2 - (HU if is_last(G) else 0))

        def ring_plan(G):
            last = GROUPS - 1
            plan = [("o", 0), ("o", 1)] if not is_first(G) else []
            if not is_last(G):
                plan += [("max", u, 1) for u in UNITS[HU:]] + [("turn",)]
                if not isinstance(G, int) or G + 2 <= last:
                    plan += [("max", u, 2) for u in UNITS[:HU]]
            return plan

        def ring_bank(G, n):
            return ring[((ring_base(0) if is_first(G) else ring_base(1)) + n) % NBANK]

        def woven(G):
            main = []
            for n, (j, h, half) in enumerate(KEYED):
                a, z = queries(j, half)
                main.append((("score", n), (z - a) + P * (a == j * P)))
                if j >= 1 and half == 1:
                    if h == 1 and j - 1 < QT // 2:
                        main.append((("value", j - 1, 0), 4 * (D - (j - 1) * P)))
                    if h == GH - 1:
                        a, z = queries(j - 1, 1)
                        main.append((("value", j - 1, 1), 4 * (z - a)))
            main.append((("value", QT - 1, 1), 4 * P))
            out, clock, pending = [], 0.0, []
            plan = list(enumerate(ring_plan(G)))
            free_at = 2.0 * D if not is_first(G) else 0.0
            while main or plan:
                pending = [x for x in pending if x > clock]
                room = plan and len(pending) < NBANK
                if room and plan[0][1][0] == "o" and clock < 3 * D and main:
                    room = False
                if room and plan[0][1][0] == "turn" and clock < free_at + 3 * D and main:
                    room = False
                if room or not main:
                    n, what = plan.pop(0)
                    out.append(("ring", n, what))
                    if what[0] == "max":
                        w = keys(what[1][1], what[1][2])
                        clock, cost = clock + w + P, 2.5 * w + 200
                    elif what[0] == "o":
                        clock, cost = clock + D, 1200
                    else:
                        clock, cost = clock + P, 600
                    free_at = max(free_at, clock + 300) + cost
                    pending.append(free_at)
                else:
                    what, cost = main.pop(0)
                    out.append(what)
                    clock += cost
            return out

        def turns(eng, turn, steps=None, per=0):
            turn(0, 0, 0)
            rounds = (GROUPS - 4) // NBUF
            with eng.Fori(0, rounds) as i:
                if steps:
                    steps.enter(i, per * NBUF)
                for k in range(NBUF):
                    turn(i * NBUF + (1 + k), (1 + k) % NBUF, i + (1 + k) // NBUF)
                if steps:
                    steps.leave(rounds)
            for G in range(1 + rounds * NBUF, GROUPS):
                turn(G, G % NBUF, G // NBUF)

        def is_last(G):
            return isinstance(G, int) and G == GROUPS - 1

        def is_first(G):
            return isinstance(G, int) and G == 0

        def after(buf, cycle):
            return (buf + 1) % NBUF, cycle + (buf + 1) // NBUF

        @block.sync
        def _(sp):
            def load(G, buf):
                head = (G % 8) * (GH * HD)
                tok = (G // 8) * S
                for rows, which, parts in ((q_rows, "q", (0, 1, 2, 0, 1, 0)), (k_rows, "k", (0, 0, 0, 1, 1, 2))):
                    for r, part in enumerate(parts):
                        src = g.scratch[which][part, bass.ds(head, GH * HD), bass.ds(tok, S)]
                        sp.dma_start(rows[buf][r * HD:(r + 1) * HD, :, :], src.rearrange("(h r) t -> r h t", h=GH)).then_inc(rows_loaded[buf], 16)

            def load_max(buf):
                sp.dma_start(q_rows[buf][ROWS:ROWS + 3, :, :].rearrange("c h (i t) -> c (h i) t", t=P), neg_turned[:]).then_inc(max_loaded[buf], 16)

            def turn(G, buf, cycle):
                if not isinstance(G, int) or G + 2 < GROUPS:
                    at_least(sp, scored, G * NK)
                    load(G + 2, (buf + 2) % NBUF)
                if not is_last(G):
                    sp.wait_ge(ring_done, ring_base(G) + HU + (1 if is_first(G) else 3))
                    load_max(after(buf, cycle)[0])

            load(0, 0)
            load(1, 1)
            sp.wait_ge(ring_done, NU + 1)
            load_max(0)
            turns(sp, turn)
            sp.wait_ge(max_loaded[(GROUPS - 1) % NBUF], 16 * (GROUPS // NBUF + 1))

        @block.tensor
        def _(pe):
            def max_unit(u, base, n, bank, buf):
                h, i, half = u
                w = keys(i, half)
                at_least(pe, ring_done, base + n - NBANK + 1)
                diagonal = (i * P) // D == half
                last = nc.tensor.matmul(bank[:, 0:w], q_rows[buf][0:ROWS, h, i * P:(i + 1) * P],
                                        k_rows[buf][0:ROWS, h, half * D:half * D + w], start=True, stop=not diagonal)
                if diagonal:
                    last = nc.tensor.matmul(bank[:, w - P:w], ident_b[:], causal[:], start=False, stop=True)
                last.then_inc(ring_ready, 1)

            def turn_max(base, n, bank, count):
                pe.wait_ge(neg_ready, count)
                at_least(pe, ring_done, base + n - NBANK + 1)
                out = bank[0:3 * GH * QT, 0:P // 2].bitcast(BF16)
                nc.tensor.transpose(out, neg_parts[:].rearrange("p c n -> p (c n)"), ident_b[:]).then_inc(ring_ready, 1)

            def turn_o(base, n, bank, half, G1):
                pe.wait_ge(o_copied, G1 * 2 + 2)
                at_least(pe, ring_done, base + n - NBANK + 1)
                for i in range(QT // 2):
                    c = (half * (QT // 2) + i) * P
                    last = nc.tensor.transpose(bank[:, i * P:(i + 1) * P], o_t[:, c:c + P], g.ident[:])
                last.then_inc(ring_ready, 1)

            def score(G, buf, n):
                j, h, half = KEYED[n]
                a, z = queries(j, half)
                bank = scores[n % NBANK]
                at_least(pe, exped, G * NK + n - NBANK + 1)
                last = nc.tensor.matmul(bank[:, 0:z - a], k_rows[buf][0:ROWS + 3, h, j * P:(j + 1) * P],
                                        q_rows[buf][0:ROWS + 3, h, a:z], start=True, stop=a != j * P)
                if a == j * P:
                    last = nc.tensor.matmul(bank[:, 0:P], causal[:], ident_b[:], start=False, stop=True)
                last.then_inc(scored, 1)

            def value(G, buf, j, half):
                pe.wait_ge(exped, G * NK + keyed_until(j))
                if j == 0:
                    pe.wait_ge(v_ready, G + 1)
                    at_least(pe, o_copied, G * 2)
                a, z = queries(j, half)
                for h in range(GH):
                    last = nc.tensor.matmul(o_bank[half][32 * h:32 * h + 32, a - half * D:z - half * D],
                                            v_rows[buf][:, j, h, :], probs[j % 2][:, h, a:z],
                                            start=(j == 0), stop=(j == (QT // 2 - 1 if half == 0 else QT - 1)),
                                            skip_group_check=True)
                if half == 1:
                    last.then_inc(valued, 1)

            def turn(G, buf, cycle):
                base = ring_base(G)
                pe.wait_ge(max_loaded[buf], cycle * 16 + 16)
                for what in woven(G):
                    if what[0] == "score":
                        score(G, buf, what[1])
                    elif what[0] == "value":
                        value(G, buf, what[1], what[2])
                    else:
                        n, unit = what[1:]
                        bank = ring_bank(G, n)
                        if unit[0] == "o":
                            turn_o(base, n, bank, unit[1], G - 1)
                        elif unit[0] == "turn":
                            turn_max(base, n, bank, G + 2)
                        else:
                            k = unit[2]
                            if unit[1] == UNITS[0]:
                                pe.wait_ge(rows_loaded[(buf + k) % NBUF], (cycle + (buf + k) // NBUF) * LOADS + LOADS)
                            max_unit(unit[1], base, n, bank, (buf + k) % NBUF)

            pe.wait_ge(ready, 4)
            pe.wait_ge(rows_loaded[0], LOADS)
            for n, u in enumerate(UNITS):
                max_unit(u, 0, n, ring[n % NBANK], 0)
            turn_max(0, NU, ring[NU % NBANK], 1)
            pe.wait_ge(rows_loaded[1], LOADS)
            for n, u in enumerate(UNITS[:HU]):
                max_unit(u, NU + 1, n, ring[(NU + 1 + n) % NBANK], 1)
            turns(pe, turn)
            for n in (2, 3):
                turn_o(ring_base(GROUPS - 1), n, ring_bank(1, n), n - 2, GROUPS - 1)

        @block.scalar
        def _(act):
            def copy_o(G1):
                act.wait_ge(valued, G1 * QT + QT)
                if not is_first(G1):
                    act.wait_ge(ring_ready, ring_base(G1) + 2)
                for half in range(2):
                    nc.scalar.copy(o_t[:, half * D:(half + 1) * D], o_bank[half][:]).then_inc(o_copied, 1)

            def turn(G, buf, cycle):
                if not is_first(G):
                    copy_o(G - 1)
                for n, (j, h, half) in enumerate(KEYED):
                    a, z = queries(j, half)
                    act.wait_ge(scored, G * NK + n + 1)
                    at_least(act, valued, G * QT + j - 1)
                    nc.scalar.activation(probs[j % 2][:, h, a:z], scores[n % NBANK][:, 0:z - a], ACT.Exp,
                                         scale=float(HD) ** -0.5).then_inc(exped, 1)

            turns(act, turn)
            copy_o(GROUPS - 1)

        @block.gpsimd
        def _(pool):
            for i in range(NBUF):
                nc.gpsimd.memset(v_rows[i][:], 0.0).then_inc(own_pool, 1)
            pool.wait_ge(own_pool, NBUF)
            for i in range(NBUF):
                nc.gpsimd.memset(v_rows[i][:, :, :, HD:HD + 1], 1.0).then_inc(own_pool, 1)
            pool.wait_ge(own_pool, 2 * NBUF)

            def take_v(G, buf):
                src = g.vo[:, bass.ds((G // 8) * QT, QT), bass.ds((G % 8) * (GH * HD), GH * HD)]
                nc.gpsimd.tensor_copy(v_rows[buf][:, :, :, 0:HD], src.rearrange("p t (h d) -> p t h d", h=GH)).then_inc(v_ready, 1)

            def turn(G, buf, cycle):
                if not is_last(G):
                    at_least(pool, valued, G * QT)
                    take_v(G + 1, (buf + 1) % NBUF)

            take_v(0, 0)
            turns(pool, turn)

        @block.vector
        def _(dve):
            own = Steps(own_vector)
            own.then_wait(dve, nc.vector.tensor_copy(ident_b[:], g.ident[:]))
            nc.vector.tensor_copy(causal[:], g.causal_in[:]).then_inc(ready, 1)
            for i in range(NBUF):
                nc.vector.memset(k_rows[i][ROWS:ROWS + 3, :, :], 1.0).then_inc(ready, 1)
            own.then_wait(dve, nc.vector.memset(part_max[:], NEG))

            def maximum(u, base, n, bank):
                h, i, half = u
                dve.wait_ge(ring_ready, base + n + 1)
                nc.vector.tensor_reduce(part_max[:, h, i, half:half + 1], bank[:, 0:keys(i, half)], AX.X, ALU.max).then_inc(ring_done, 1)

            def negated(base, n, bank):
                dve.wait_ge(ring_done, base + n)
                own.then_wait(dve, nc.vector.tensor_reduce(row_max[:], part_max[:].rearrange("p h i a -> p (h i) a"), AX.X, ALU.max))
                own.then_wait(dve, nc.vector.tensor_scalar(neg_parts[:, 0, :], row_max[:], -1.0, None, ALU.mult))
                own.then_wait(dve, nc.vector.scalar_tensor_tensor(neg_rest[:, 0, :], row_max[:], -1.0, neg_parts[:, 0, :], ALU.mult, ALU.subtract))
                own.then_wait(dve, nc.vector.tensor_copy(neg_parts[:, 1, :], neg_rest[:, 0, :]))
                nc.vector.tensor_tensor(neg_parts[:, 2, :], neg_rest[:, 0, :], neg_parts[:, 1, :], ALU.subtract).then_inc(neg_ready, 1)
                dve.wait_ge(ring_ready, base + n + 1)
                nc.vector.tensor_copy(neg_turned[:], bank[0:3 * GH * QT, 0:P // 2].bitcast(BF16)).then_inc(ring_done, 1)

            def outputs(base, n, bank, half, G1):
                dve.wait_ge(ring_ready, base + n + 1)
                o = bank[:].rearrange("p (i h d) -> p i h d", h=GH, d=32)
                inv = inv_sum[:, half, :].rearrange("p (i h) -> p i h", h=GH)
                own.then_wait(dve, nc.vector.reciprocal(inv, o[:, :, :, HD]))
                dst = g.vo[:, bass.ds((G1 // 8) * QT + half * (QT // 2), QT // 2), bass.ds((G1 % 8) * (GH * HD), GH * HD)]
                nc.vector.tensor_tensor(dst.rearrange("p t (h d) -> p t h d", h=GH), o[:, :, :, 0:HD],
                                        inv.unsqueeze(3).broadcast_to((P, QT // 2, GH, HD)), ALU.mult).then_inc(ring_done, 1)

            def turn(G, buf, cycle):
                base = ring_base(G)
                dve.wait_ge(max_loaded[buf], cycle * 16 + 16)
                for n, what in enumerate(ring_plan(G)):
                    if what[0] == "max":
                        maximum(what[1], base, n, ring_bank(G, n))
                    elif what[0] == "turn":
                        negated(base, n, ring_bank(G, n))
                    else:
                        outputs(base, n, ring_bank(G, n), what[1], G - 1)

            for n, u in enumerate(UNITS):
                maximum(u, 0, n, ring[n % NBANK])
            negated(0, NU, ring[NU % NBANK])
            for n, u in enumerate(UNITS[:HU]):
                maximum(u, NU + 1, n, ring[(NU + 1 + n) % NBANK])
            turns(dve, turn, own, 6)
            for n in (2, 3):
                outputs(ring_base(GROUPS - 1), n, ring_bank(1, n), n - 2, GROUPS - 1)


class Shared:
    pass


def program(nc, ins, out):
    with ExitStack() as ctx:
        def sb(name, shape, dt=F32, at=ctx):
            return at.enter_context(nc.sbuf_tensor(name, shape, dt))

        g = Shared()
        g.x = sb("x", [P, TILES, D])
        g.vo = sb("v_then_o", [P, TILES, D])
        g.ident = sb("identity", [P, P])
        g.causal_in = sb("causal_in", [P, P])
        g.w_hi = {BIN_FFN: sb("w_hi_bin", [P, KC, D], F32R)}
        g.w_lo = {BIN_FFN: sb("w_lo_bin", [P, KC, D], F32R)}
        g.scratch = {w: nc.dram_tensor(f"{w}_parts", (3, D, B * S), BF16, kind="Internal").ap() for w in "qk"}
        g.qkv_loaded = ctx.enter_context(nc.semaphore("qkv_loaded"))
        g.cos_in, g.sin_in = ins["cos"], ins["sin"]
        with ExitStack() as first:
            g.iota = sb("expert_numbers", [P, E], at=first)
            g.bias = {LORA_FFN: sb("bias_ffn", [P, D], at=first), SPARSE: sb("bias_sparse", [P, D], at=first)}
            for k in (LORA_FFN, SPARSE):
                g.w_hi[k] = sb(f"w_hi{k}", [P, KC, D], F32R, at=first)
                g.w_lo[k] = sb(f"w_lo{k}", [P, KC, D], F32R, at=first)
            g.ra = sb("router_and_down", [P, KC, E + ER], at=first)
            g.up_hi = sb("up_hi", [P, D], F32R, at=first)
            g.up_lo = sb("up_lo", [P, D], F32R, at=first)
            prepare_weights(nc, ins, g)
            dense_stages(nc, g, BEFORE, "ffn")
        project_qkv(nc, g)
        attention(nc, g)
        g.w_hi[OUT_PROJ] = sb("w_hi_out", [P, KC, D], F32R)
        g.w_lo[OUT_PROJ] = sb("w_lo_out", [P, KC, D], F32R)
        split_out_projection(nc, ins, g)
        dense_stages(nc, g, (OUT_PROJ, BIN_FFN), "end", out)


def split_out_projection(nc, ins, g):
    with (nc.sbuf_tensor("wo_raw", [P, KC, D], F32) as raw, nc.semaphore("wo_loaded") as loaded,
          nc.semaphore("wo_hi") as hi, nc.Block() as block):
        @block.sync
        def _(sp):
            sp.dma_start(raw[:], ins["L1_attn_wo"].rearrange("(c p) n -> p c n", p=P)).then_inc(loaded, 16)

        @block.scalar
        def _(act):
            act.wait_ge(loaded, 16)
            nc.scalar.copy(g.w_hi[OUT_PROJ][:], raw[:]).then_inc(hi, 1)

        @block.vector
        def _(dve):
            dve.wait_ge(hi, 1)
            nc.vector.tensor_tensor(g.w_lo[OUT_PROJ][:], raw[:], g.w_hi[OUT_PROJ][:].bitcast(F32), ALU.subtract)


def rotation_tables():
    inv = 1.0 / 10000.0 ** (np.arange(0, HD, 2)[:HD // 2].astype(np.float32) / HD)
    f = np.outer(np.arange(S), inv).astype(np.float32)
    return (np.ascontiguousarray(np.tile(t.T, (P // (HD // 2), 1))) for t in (np.cos(f), np.sin(f)))


def shape_constants():
    cos, sin = rotation_tables()
    return {
        "ident": np.eye(P, dtype=np.float32),
        "same_block": np.kron(np.eye(P // BLK, dtype=np.float32), np.ones((BLK, BLK), np.float32)),
        "iota": np.arange(E, dtype=np.float32),
        "causal": np.triu(np.full((P, P), NEG, np.float32), 1),
        "cos": cos,
        "sin": sin,
    }


_INS = ["L0_attn_data", "L0_attn_mask", "L0_attn_weight", "L0_attn_bias", "L0_ffn_W_base", "L0_ffn_b_base",
        "L0_ffn_W_router", "L0_ffn_A", "L0_ffn_B", "L1_attn_wq", "L1_attn_wk", "L1_attn_wv", "L1_attn_wo",
        "L1_ffn_weight", "L1_ffn_wscale", "L1_ffn_wbias"]


def kernel(**inputs):
    import concourse.bacc as bacc
    from concourse.bass_utils import run_bass_kernel_spmd

    nc = bacc.Bacc("TRN2", target_bir_lowering=False, num_devices=1)
    arrays = {name: np.ascontiguousarray(inputs[name]) for name in _INS}
    arrays.update(shape_constants())
    ins = {name: nc.dram_tensor(f"in_{name}", a.shape, mybir.dt.from_np(a.dtype), kind="ExternalInput").ap()
           for name, a in arrays.items()}
    out = nc.dram_tensor("out", (B, S, D), F32, kind="ExternalOutput").ap()
    program(nc, ins, out)
    result = run_bass_kernel_spmd(nc, [{f"in_{name}": a for name, a in arrays.items()}], core_ids=[0])
    return result.results[0]["out"]
```

```python
from contextlib import ExitStack

import numpy as np

import concourse.bass as bass
from concourse import mybir

F32 = mybir.dt.float32
F32R = mybir.dt.float32r
BF16 = mybir.dt.bfloat16
I32 = mybir.dt.int32
U32 = mybir.dt.uint32
ALU = mybir.AluOpType
ACT = mybir.ActivationFunctionType
AX = mybir.AxisListType

P = 128
D = 512
KC = D // P
B, S = 2, 1024
TILES = B * S // P
E, RANK = 8, 16
ER = E * RANK
BLK = 32
NBLK = KC * D // BLK
EPS = 1e-5
LORA_SCALE = 2.0

LORA_FFN, SPARSE, BIN_FFN, OUT_PROJ = range(4)
BEFORE = (LORA_FFN, SPARSE, LORA_FFN, BIN_FFN)
RESIDUAL = {LORA_FFN: 0.5, SPARSE: 1.0, BIN_FFN: 0.5, OUT_PROJ: 1.0}
LEAD = 4


class Steps:

    def __init__(self, sem):
        self.sem, self.base, self.off = sem, 0, 0

    def step(self, ins):
        self.off += 1
        ins.then_inc(self.sem, 1)

    def wait(self, eng):
        at_least(eng, self.sem, self.base + self.off)

    def then_wait(self, eng, ins):
        self.step(ins)
        self.wait(eng)

    def enter(self, i, per):
        self.start = self.base + self.off
        self.per = per
        self.base, self.off = i * per + self.start, 0

    def leave(self, rounds):
        assert self.off == self.per, (self.off, self.per)
        self.base, self.off = self.start + rounds * self.per, 0


def over_tiles(eng, kinds, tile, steps=None, per=None):
    rounds = (TILES - LEAD) // 2 - 1
    for s in range(len(kinds)):
        for t in (0, 1):
            tile(s, t, s * TILES + t, t % 2)
        with eng.Fori(0, rounds) as i:
            if steps:
                steps.enter(i, per[kinds[s]])
            for p in (0, 1):
                tile(s, i * 2 + (2 + p), i * 2 + (s * TILES + 2 + p), p)
            if steps:
                steps.leave(rounds)
        for t in range(TILES - LEAD, TILES):
            tile(s, t, s * TILES + t, t % 2)


def neighbour(kinds, s, t, k):
    if not isinstance(t, int):
        return s, t + k
    n = s * TILES + t + k
    return (n // TILES, n % TILES) if 0 <= n < len(kinds) * TILES else None


def at_least(eng, sem, value):
    if not isinstance(value, int) or value > 0:
        eng.wait_ge(sem, value)


def prepare_weights(nc, ins, g):
    with ExitStack() as ctx:
        def sb(name, shape, dt=F32):
            return ctx.enter_context(nc.sbuf_tensor(name, shape, dt))

        def sem(name):
            return ctx.enter_context(nc.semaphore(name))

        nat = {k: g.vo[:, n * KC:(n + 1) * KC, :] for n, k in enumerate((LORA_FFN, SPARSE, BIN_FFN))}
        signs = g.vo[:, 3 * KC:4 * KC, :]
        mask = sb("mask_in", [P, KC, D], I32)
        block_sum = sb("block_sum", [P, NBLK])
        block_on = sb("block_on", [P, NBLK])
        same_block = sb("same_block_sb", [P, P])
        nat_a = sb("nat_a", [P, D])
        nat_router = sb("nat_router", [E, D])
        nat_b = sb("nat_b", [P, KC, E, RANK])
        wscale = sb("wscale", [P, KC])
        wbias = sb("wbias", [P, KC])
        bank = [ctx.enter_context(nc.psum_tensor(f"wbank{i}", [P, D], F32)) for i in range(6)]
        mask_bank = ctx.enter_context(nc.psum_tensor("mask_bank", [P, D], F32))
        small_bank = ctx.enter_context(nc.psum_tensor("small_bank", [P, KC, P], F32))

        s_const, s_base, s_lora, s_mask, s_bin = (sem(n) for n in (
            "const_loaded", "base_loaded", "lora_loaded", "mask_loaded", "bin_loaded"))
        s_ident, s_sparse_in, s_signs = sem("squares_loaded"), sem("sparse_loaded"), sem("signs_ready")
        s_sums, s_onmap, s_sparse, s_scaled = sem("mask_sums"), sem("mask_map"), sem("sparse_ready"), sem("bin_ready")
        s_tr, s_hi, s_lo, s_small, s_small_out = (sem(n) for n in (
            "w_transposed", "w_hi", "w_lo", "lora_transposed", "lora_copied"))
        s_own = sem("prep_vector_own")
        block = ctx.enter_context(nc.Block())
        order = (LORA_FFN, SPARSE, BIN_FFN)

        @block.sync
        def _(sp):
            def chunked(name):
                return ins[name].rearrange("(c p) k -> p c k", p=P)

            sp.dma_start(g.ident[:], ins["ident"]).then_inc(s_ident, 16)
            sp.dma_start(nat[LORA_FFN], chunked("L0_ffn_W_base")).then_inc(s_base, 16)
            sp.dma_start(mask[:], chunked("L0_attn_mask")).then_inc(s_mask, 16)
            sp.dma_start(nat[SPARSE], chunked("L0_attn_weight")).then_inc(s_sparse_in, 16)
            sp.dma_start(nat[BIN_FFN], chunked("L1_ffn_weight")).then_inc(s_bin, 16)
            sp.wait_ge(s_lora, 96)
            x = ins["L0_attn_data"].rearrange("b (t p) d -> p (b t) d", p=P)
            for t in range(0, TILES, 4):
                sp.dma_start(g.x[:, t:t + 4, :], x[:, t:t + 4, :]).then_inc(g.x_loaded[t // 4], 16)

        @block.scalar
        def _(act):
            act.dma_start(same_block[:], ins["same_block"]).then_inc(s_ident, 16)
            act.dma_start(nat_a[:], ins["L0_ffn_A"].rearrange("e r k -> (e r) k")).then_inc(s_lora, 16)
            act.dma_start(nat_router[:], ins["L0_ffn_W_router"]).then_inc(s_lora, 16)
            for c in range(KC):
                act.dma_start(nat_b[:, c, :, :], ins["L0_ffn_B"][:, c * P:(c + 1) * P, :].rearrange("e o r -> o e r")).then_inc(s_lora, 16)
            act.dma_start(wscale[:], ins["L1_ffn_wscale"].rearrange("(c p) o -> p (c o)", p=P), allow_slow_non_contiguous=True).then_inc(s_bin, 16)
            act.dma_start(wbias[:], ins["L1_ffn_wbias"].rearrange("(c p) o -> p (c o)", p=P), allow_slow_non_contiguous=True).then_inc(s_bin, 16)
            act.dma_start(g.causal_in[:], ins["causal"]).then_inc(s_const, 16)
            act.dma_start(g.iota[:], ins["iota"].partition_broadcast(P)).then_inc(s_const, 16)
            act.dma_start(g.bias[LORA_FFN][:], ins["L0_ffn_b_base"].partition_broadcast(P)).then_inc(s_const, 16)
            act.dma_start(g.bias[SPARSE][:], ins["L0_attn_bias"].partition_broadcast(P)).then_inc(s_const, 16)
            for n, kind in enumerate(order):
                for c in range(KC):
                    u = n * KC + c
                    act.wait_ge(s_tr, u + 1)
                    nc.scalar.copy(g.w_hi[kind][:, c, :], bank[u % 6][:]).then_inc(s_hi, 1)
                if n == 0:
                    act.wait_ge(s_bin, 48)
                    for c in range(KC):
                        nc.scalar.activation(signs[:, c, :], nat[BIN_FFN][:, c, :], ACT.Sign).then_inc(s_signs, 1)

        @block.gpsimd
        def _(pool):
            for c in range(KC):
                pool.wait_ge(s_signs, c + 1)
                nc.gpsimd.tensor_scalar(nat[BIN_FFN][:, c, :], signs[:, c, :], wscale[:, c:c + 1], wbias[:, c:c + 1],
                                        ALU.mult, ALU.add).then_inc(s_scaled, 1)

        @block.tensor
        def _(pe):
            pe.wait_ge(s_ident, 32)

            def transposed(n, kind):
                for c in range(KC):
                    u = n * KC + c
                    if u >= 6:
                        pe.wait_ge(s_lo, u - 5)
                    for i in range(KC):
                        last = nc.tensor.transpose(bank[u % 6][:, i * P:(i + 1) * P],
                                                   nat[kind][:, i, c * P:(c + 1) * P], g.ident[:])
                    last.then_inc(s_tr, 1)

            pe.wait_ge(s_base, 16)
            transposed(0, LORA_FFN)
            pe.wait_ge(s_sums, 1)
            nc.tensor.matmul(mask_bank[:, 0:NBLK], same_block[:], block_sum[:], start=True, stop=True).then_inc(s_onmap, 1)
            pe.wait_ge(s_sparse, 1)
            transposed(1, SPARSE)
            pe.wait_ge(s_lora, 96)
            for c in range(KC):
                last = nc.tensor.transpose(small_bank[:, c, :], nat_a[:, c * P:(c + 1) * P], g.ident[:])
            last.then_inc(s_small, 1)
            pe.wait_ge(s_small_out, 1)
            for c in range(KC):
                last = nc.tensor.transpose(small_bank[:, c, 0:E], nat_router[:, c * P:(c + 1) * P], g.ident[0:E, 0:E])
            last.then_inc(s_small, 1)
            pe.wait_ge(s_small_out, 2)
            for c in range(KC):
                last = nc.tensor.transpose(small_bank[:, c, :],
                                           nat_b[:, c, :, :].rearrange("p e r -> p (e r)"), g.ident[:])
            last.then_inc(s_small, 1)
            pe.wait_ge(s_scaled, KC)
            transposed(2, BIN_FFN)

        @block.vector
        def _(dve):
            own = Steps(s_own)

            def rest_of(n, kind):
                for c in range(KC):
                    u = n * KC + c
                    dve.wait_ge(s_hi, u + 1)
                    nc.vector.tensor_tensor(g.w_lo[kind][:, c, :], bank[u % 6][:],
                                            g.w_hi[kind][:, c, :].bitcast(F32), ALU.subtract).then_inc(s_lo, 1)

            rest_of(0, LORA_FFN)
            dve.wait_ge(s_mask, 16)
            nc.vector.tensor_reduce(block_sum[:], mask[:].rearrange("p c (b w) -> p (c b) w", w=BLK), AX.X, ALU.add).then_inc(s_sums, 1)
            dve.wait_ge(s_onmap, 1)
            own.then_wait(dve, nc.vector.tensor_scalar(block_on[:], mask_bank[:, 0:NBLK], 0.0, None, ALU.is_gt))
            dve.wait_ge(s_sparse_in, 16)
            w = nat[SPARSE].rearrange("p c (b w) -> p (c b) w", w=BLK)
            nc.vector.tensor_tensor(w, w, block_on[:].unsqueeze(2).broadcast_to((P, NBLK, BLK)), ALU.mult).then_inc(s_sparse, 1)
            rest_of(1, SPARSE)
            dve.wait_ge(s_small, 1)
            nc.vector.tensor_copy(g.ra[:, :, E:E + ER], small_bank[:]).then_inc(s_small_out, 1)
            dve.wait_ge(s_small, 2)
            nc.vector.tensor_copy(g.ra[:, :, 0:E], small_bank[:, :, 0:E]).then_inc(s_small_out, 1)
            dve.wait_ge(s_small, 3)
            up = small_bank[:].rearrange("p c n -> p (c n)")
            own.then_wait(dve, nc.vector.tensor_copy(g.up_hi[:], up))
            own.then_wait(dve, nc.vector.tensor_tensor(g.up_lo[:], up, g.up_hi[:].bitcast(F32), ALU.subtract))
            rest_of(2, BIN_FFN)
            dve.wait_ge(s_const, 64)
            nc.vector.tensor_scalar(g.bias[LORA_FFN][:], g.bias[LORA_FFN][:], 0.5, None, ALU.mult)


def dense_stages(nc, g, kinds, tag, out=None):
    with ExitStack() as ctx:
        def sb(name, shape, dt=F32):
            return ctx.enter_context(nc.sbuf_tensor(f"{tag}_{name}", shape, dt))

        def psum(name, shape):
            return ctx.enter_context(nc.psum_tensor(f"{tag}_{name}", shape, F32))

        def sem(name):
            return ctx.enter_context(nc.semaphore(f"{tag}_{name}"))

        lora = [k == LORA_FFN for k in kinds]
        normed = [k != OUT_PROJ for k in kinds]
        has_lora = any(lora)
        stats = [sb(f"stats{p}", [P, 6]) for p in range(2)]
        mean_var = [sb(f"mean_var{p}", [P, 2]) for p in range(2)]
        var_eps = [sb(f"var_eps{p}", [P, 1]) for p in range(2)]
        rstd = [sb(f"rstd{p}", [P, 1]) for p in range(2)]
        neg_half = sb("neg_half", [P, 1])
        eps = sb("eps", [P, 1])
        xn = [sb(f"xn{p}", [P, D]) for p in range(2)]
        xt_hi = [sb(f"xt_hi{p}", [P, KC, P], F32R) for p in range(2)]
        xt_lo = [sb(f"xt_lo{p}", [P, KC, P], F32R) for p in range(2)]
        xt_bank = [psum(f"xt_bank{p}", [P, KC, P]) for p in range(2)]
        y_bank = [psum(f"y_bank{p}", [P, D]) for p in range(2)]
        if has_lora:
            xt_sum = [sb(f"xt_sum{p}", [P, KC, P]) for p in range(2)]
            ra_bank = [psum(f"ra_bank{p}", [P, E + ER]) for p in range(2)]
            hw_bank = [psum(f"hw_bank{p}", [P, P]) for p in range(2)]
            top = [sb(f"top{p}", [P, 8]) for p in range(2)]
            top_at = [sb(f"top_at{p}", [P, 8], U32) for p in range(2)]
            top_atf = [sb(f"top_atf{p}", [P, 2]) for p in range(2)]
            ratio = [sb(f"ratio{p}", [P, 1]) for p in range(2)]
            gate = [sb(f"gate{p}", [P, 3]) for p in range(2)]
            share = [sb(f"share{p}", [P, 3, E]) for p in range(2)]
            logits = [sb(f"logits{p}", [P, E]) for p in range(2)]
            hw = [sb(f"hw{p}", [P, E, RANK]) for p in range(2)]
            hwt_hi = [sb(f"hwt_hi{p}", [P, P], F32R) for p in range(2)]
            hwt_lo = [sb(f"hwt_lo{p}", [P, P], F32R) for p in range(2)]

        mv_ready, rstd_ready, xn_ready, xt_ready, hi_ready, lo_ready = (sem(n) for n in (
            "mv_ready", "rstd_ready", "xn_ready", "xt_ready", "hi_ready", "lo_ready"))
        bias_in, multiplied, y_ready, x_done = sem("bias_in"), sem("multiplied"), sem("y_ready"), sem("x_done")
        sum_ready, ra_ready, ratio_ready, hw_ready, hwt_ready, hwt_hi_ready, hwt_lo_ready, top_ready = (sem(n) for n in (
            "sum_ready", "ra_ready", "ratio_ready", "hw_ready", "hwt_ready", "hwt_hi_ready", "hwt_lo_ready", "top_ready"))
        own_vector, own_pool = sem("own_vector"), sem("own_pool")
        block = ctx.enter_context(nc.Block())
        last_tile = len(kinds) * TILES

        if out is None:
            @block.sync
            def _(sp):
                for n, w in enumerate(g.qkv_in):
                    sp.dma_start(g.vo[:, n * KC:(n + 1) * KC, :], w).then_inc(g.qkv_loaded, 16)

        if out is not None:
            stored = sem("stored")
            rows = out.rearrange("b (t p) d -> p (b t) d", p=P)

            @block.sync
            def _(sp):
                with sp.Fori(0, TILES) as t:
                    sp.wait_ge(x_done, t + (last_tile - TILES + 1))
                    sp.dma_start(rows[:, t, :], g.x[:, t, :]).then_inc(stored, 16)
                sp.wait_ge(stored, 16 * TILES)

        def normed_before(s):
            return sum(TILES for k in range(s) if normed[k]) - s * TILES

        def experts_before(s):
            return sum(TILES for k in range(s) if lora[k]) - s * TILES

        def side_chunks(s, t):
            if out is not None or s != 1 or not isinstance(t, int):
                return ()
            slot = t if t < 2 else t - (TILES - LEAD) + 2
            return 2 * slot, 2 * slot + 1

        @block.tensor
        def _(pe):
            def transpose_x(s, t, T, p):
                pe.wait_ge(xn_ready, T + 1)
                at_least(pe, lo_ready, T - 1)
                for c in range(KC):
                    last = nc.tensor.transpose(xt_bank[p][:, c, :], xn[p][:, c * P:(c + 1) * P], g.ident[:])
                last.then_inc(xt_ready, 1)

            def experts_down(s, T, p):
                L = T + experts_before(s)
                pe.wait_ge(sum_ready, L + 1)
                at_least(pe, hw_ready, L - 1)
                for c in range(KC):
                    last = nc.tensor.matmul(ra_bank[p][:], xt_sum[p][:, c, :], g.ra[:, c, :],
                                            start=(c == 0), stop=(c == KC - 1))
                last.then_inc(ra_ready, 1)

            def transpose_hw(s, T, p):
                L = T + experts_before(s)
                pe.wait_ge(hw_ready, L + 1)
                at_least(pe, hwt_lo_ready, L - 1)
                nc.tensor.transpose(hw_bank[p][:], hw[p][:].rearrange("p e r -> p (e r)"), g.ident[:]).then_inc(hwt_ready, 1)

            def project(s, T, p):
                pe.wait_ge(lo_ready, T + 1)
                at_least(pe, x_done, T - 1)
                k = kinds[s]
                for c in range(KC):
                    nc.tensor.matmul(y_bank[p][:], xt_lo[p][:, c, :], g.w_hi[k][:, c, :], start=(c == 0), stop=False)
                    nc.tensor.matmul(y_bank[p][:], xt_hi[p][:, c, :], g.w_lo[k][:, c, :], start=False, stop=False)
                    last = nc.tensor.matmul(y_bank[p][:], xt_hi[p][:, c, :], g.w_hi[k][:, c, :],
                                            start=False, stop=(c == KC - 1 and not lora[s]))
                last.then_inc(multiplied, 1)

            def experts_up(s, T, p):
                L = T + experts_before(s)
                pe.wait_ge(hwt_lo_ready, L + 1)
                nc.tensor.matmul(y_bank[p][:], hwt_lo[p][:], g.up_hi[:], start=False, stop=False)
                nc.tensor.matmul(y_bank[p][:], hwt_hi[p][:], g.up_lo[:], start=False, stop=False)
                nc.tensor.matmul(y_bank[p][:], hwt_hi[p][:], g.up_hi[:], start=False, stop=True).then_inc(y_ready, 1)

            def tile(s, t, T, p):
                if lora[s]:
                    experts_down(s, T, p)
                back = neighbour(kinds, s, t, -1)
                back_lora = back is not None and lora[back[0]]
                if back_lora:
                    transpose_hw(back[0], T - 1, 1 - p)
                on = neighbour(kinds, s, t, 2)
                if on is not None:
                    transpose_x(on[0], on[1], T + 2, p)
                project(s, T, p)
                if back_lora:
                    experts_up(back[0], T - 1, 1 - p)

            transpose_x(0, 0, 0, 0)
            transpose_x(0, 1, 1, 1)
            over_tiles(pe, kinds, tile)
            if lora[-1]:
                transpose_hw(len(kinds) - 1, last_tile - 1, 1)
                experts_up(len(kinds) - 1, last_tile - 1, 1)

        @block.scalar
        def _(act):
            def round_x(s, T, p):
                act.wait_ge(xt_ready, T + 1)
                at_least(act, multiplied, T - 1)
                if lora[s]:
                    L = T + experts_before(s)
                    at_least(act, ra_ready, L - 1)
                    nc.scalar.copy(xt_sum[p][:], xt_bank[p][:]).then_inc(sum_ready, 1)
                nc.scalar.copy(xt_hi[p][:], xt_bank[p][:]).then_inc(hi_ready, 1)

            def tile(s, t, T, p):
                on = neighbour(kinds, s, t, 1)
                if on is not None:
                    round_x(on[0], T + 1, 1 - p)
                back = neighbour(kinds, s, t, -1)
                if back is not None and lora[back[0]]:
                    L = T - 1 + experts_before(back[0])
                    act.wait_ge(hwt_ready, L + 1)
                    nc.scalar.copy(hwt_hi[1 - p][:], hw_bank[1 - p][:]).then_inc(hwt_hi_ready, 1)
                if lora[s]:
                    L = T + experts_before(s)
                    act.wait_ge(top_ready, L + 1)
                    nc.scalar.activation(ratio[p][:], top[p][:, 0:1], ACT.Exp, bias=top[p][:, 1:2], scale=-1.0).then_inc(ratio_ready, 1)

            def tile_and_side(s, t, T, p):
                tile(s, t, T, p)
                for u in side_chunks(s, t):
                    n, c = divmod(u, KC)
                    w = "qkv"[n]
                    if u == 0:
                        act.wait_ge(g.qkv_loaded, 48)
                    nc.scalar.copy(split_view(g.qkv_hi[w], w, c), raw_view(g, n, w, c)).then_inc(g.qkv_hi_ready, 1)

            round_x(0, 0, 0)
            over_tiles(act, kinds, tile_and_side)

        @block.gpsimd
        def _(pool):
            own = Steps(own_pool)
            nc.gpsimd.memset(eps[:], EPS)
            own.then_wait(pool, nc.gpsimd.memset(neg_half[:], -0.5))

            def inverse_deviation(s, T, p):
                if not normed[s]:
                    return
                pool.wait_ge(mv_ready, T + normed_before(s) + 1)
                at_least(pool, xn_ready, T - 1)
                own.then_wait(pool, nc.gpsimd.tensor_tensor(var_eps[p][:], mean_var[p][:, 1:2], eps[:], ALU.add))
                nc.gpsimd.tensor_tensor(rstd[p][:], var_eps[p][:], neg_half[:], ALU.pow).then_inc(rstd_ready, 1)

            def tile(s, t, T, p):
                on = neighbour(kinds, s, t, LEAD)
                if on is not None:
                    inverse_deviation(on[0], T + LEAD, p)
                if kinds[s] in g.bias:
                    pool.wait_ge(xn_ready, T + 1)
                    nc.gpsimd.tensor_tensor(g.x[:, t, :], g.x[:, t, :], g.bias[kinds[s]][:], ALU.add).then_inc(bias_in, 1)

            def tile_and_side(s, t, T, p):
                tile(s, t, T, p)
                for u in side_chunks(s, t):
                    n, c = divmod(u, KC)
                    w = "qkv"[n]
                    pool.wait_ge(g.qkv_hi_ready, u + 1)
                    nc.gpsimd.tensor_tensor(split_view(g.qkv_lo[w], w, c), raw_view(g, n, w, c), split_view(g.qkv_hi[w], w, c).bitcast(F32), ALU.subtract)

            for T in range(LEAD):
                inverse_deviation(0, T, T % 2)
            over_tiles(pool, kinds, tile_and_side, own, {k: 2 * (k != OUT_PROJ) for k in kinds})

        @block.vector
        def _(dve):
            own = Steps(own_vector)

            def statistics(s, t, T, p):
                if normed[s]:
                    if s:
                        dve.wait_ge(x_done, T - TILES + 1)
                    elif out is None and isinstance(t, int):
                        for quarter in {0: (0,), LEAD: (1,), LEAD + 1: (2, 3)}.get(t, ()):
                            dve.wait_ge(g.x_loaded[quarter], 16)
                    own.step(nc.vector.bn_stats(stats[p][:], g.x[:, t, :]))

            def mean_and_variance(s, p):
                if normed[s]:
                    nc.vector.bn_aggr(mean_var[p][:], stats[p][:]).then_inc(mv_ready, 1)

            def normalise(s, t, T, p):
                at_least(dve, xt_ready, T - 1)
                if not normed[s]:
                    nc.vector.tensor_copy(xn[p][:], g.vo[:, t, :]).then_inc(xn_ready, 1)
                    return
                dve.wait_ge(rstd_ready, T + normed_before(s) + 1)
                nc.vector.tensor_scalar(xn[p][:], g.x[:, t, :], mean_var[p][:, 0:1], rstd[p][:], ALU.subtract, ALU.mult).then_inc(xn_ready, 1)

            def rest_of_x(T, p):
                dve.wait_ge(hi_ready, T + 1)
                nc.vector.tensor_tensor(xt_lo[p][:], xt_bank[p][:], xt_hi[p][:].bitcast(F32), ALU.subtract).then_inc(lo_ready, 1)

            def rest_of_hw(s, T, p):
                L = T + experts_before(s)
                dve.wait_ge(hwt_hi_ready, L + 1)
                nc.vector.tensor_tensor(hwt_lo[p][:], hw_bank[p][:], hwt_hi[p][:].bitcast(F32), ALU.subtract).then_inc(hwt_lo_ready, 1)

            def copy_logits(s, T, p):
                L = T + experts_before(s)
                dve.wait_ge(ra_ready, L + 1)
                at_least(dve, ratio_ready, L - 1)
                own.then_wait(dve, nc.vector.tensor_copy(logits[p][:], ra_bank[p][:, 0:E]))

            def gates(s, T, p):
                L = T + experts_before(s)
                own.wait(dve)
                own.then_wait(dve, nc.vector.tensor_copy(top_atf[p][:], top_at[p][:, 0:2]))
                dve.wait_ge(ratio_ready, L + 1)
                own.then_wait(dve, nc.vector.tensor_scalar(gate[p][:, 0:1], ratio[p][:], 1.0, None, ALU.add))
                own.then_wait(dve, nc.vector.reciprocal(gate[p][:, 1:2], gate[p][:, 0:1]))
                own.then_wait(dve, nc.vector.tensor_tensor(gate[p][:, 2:3], gate[p][:, 1:2], ratio[p][:], ALU.mult))
                nc.vector.tensor_scalar(share[p][:, 0, :], g.iota[:], top_atf[p][:, 0:1], gate[p][:, 1:2], ALU.is_equal, ALU.mult)
                own.then_wait(dve, nc.vector.tensor_scalar(share[p][:, 1, :], g.iota[:], top_atf[p][:, 1:2], gate[p][:, 2:3], ALU.is_equal, ALU.mult))
                own.then_wait(dve, nc.vector.tensor_tensor(share[p][:, 2, :], share[p][:, 0, :], share[p][:, 1, :], ALU.add))
                at_least(dve, hwt_ready, L - 1)
                nc.vector.scalar_tensor_tensor(hw[p][:], ra_bank[p][:, E:E + ER].rearrange("p (e r) -> p e r", e=E), LORA_SCALE,
                                               share[p][:, 2, :].unsqueeze(2).broadcast_to((P, E, RANK)),
                                               ALU.mult, ALU.mult).then_inc(hw_ready, 1)

            def add_to_x(s, t, T, p):
                if lora[s]:
                    dve.wait_ge(y_ready, T + experts_before(s) + 1)
                else:
                    dve.wait_ge(multiplied, T + 1)
                n = sum(TILES for k in range(s) if kinds[k] in g.bias) - s * TILES
                if kinds[s] in g.bias:
                    dve.wait_ge(bias_in, T + n + 1)
                nc.vector.scalar_tensor_tensor(g.x[:, t, :], y_bank[p][:], RESIDUAL[kinds[s]], g.x[:, t, :], ALU.mult, ALU.add).then_inc(x_done, 1)

            def tile(s, t, T, p):
                on = neighbour(kinds, s, t, 1)
                if on is not None:
                    rest_of_x(T + 1, 1 - p)
                back = neighbour(kinds, s, t, -1)
                if back is not None and lora[back[0]]:
                    rest_of_hw(back[0], T - 1, 1 - p)
                if lora[s]:
                    copy_logits(s, T, p)
                far, near = neighbour(kinds, s, t, 4), neighbour(kinds, s, t, 3)
                if far is not None:
                    statistics(far[0], far[1], T + 4, p)
                if lora[s]:
                    nc.vector.max(top[p][:], logits[p][:]).then_inc(top_ready, 1)
                    dve.wait_ge(top_ready, T + experts_before(s) + 1)
                if lora[s] or (far is not None and normed[far[0]]):
                    own.wait(dve)
                if near is not None:
                    normalise(near[0], near[1], T + 3, 1 - p)
                if lora[s]:
                    own.step(nc.vector.max_index(top_at[p][:], top[p][:], logits[p][:]))
                if far is not None:
                    mean_and_variance(far[0], p)
                if lora[s]:
                    gates(s, T, p)
                if back is not None:
                    add_to_x(back[0], back[1], T - 1, 1 - p)

            def both(T):
                statistics(0, T, T, T % 2)
                if normed[0]:
                    own.wait(dve)
                mean_and_variance(0, T % 2)

            both(0)
            both(1)
            for T in range(3):
                normalise(0, T, T, T % 2)
                if T < 2:
                    both(T + 2)
            rest_of_x(0, 0)
            own_per = {k: 2 * (k != OUT_PROJ) + 16 * (k == LORA_FFN) for k in kinds}
            over_tiles(dve, kinds, tile, own, own_per)
            if lora[-1]:
                rest_of_hw(len(kinds) - 1, last_tile - 1, 1)
            add_to_x(len(kinds) - 1, TILES - 1, last_tile - 1, 1)


def project_qkv(nc, g):
    SUPER = 4
    TOK = SUPER * P
    HALF = S // P // SUPER
    AHEAD = SUPER + 2
    with ExitStack() as ctx:
        def sb(name, shape, dt=F32):
            return ctx.enter_context(nc.sbuf_tensor(f"qkv_{name}", shape, dt))

        def psum(name, shape):
            return ctx.enter_context(nc.psum_tensor(f"qkv_{name}", shape, F32))

        def sem(name):
            return ctx.enter_context(nc.semaphore(f"qkv_{name}"))

        w_hi, w_lo = g.qkv_hi, g.qkv_lo
        cos = sb("cos", [P, S])
        sin = sb("sin", [P, S])
        stats = [sb(f"stats{i}", [P, 6]) for i in range(4)]
        mean_var = [sb(f"mean_var{i}", [P, 2]) for i in range(4)]
        var_eps = [sb(f"var_eps{p}", [P, 1]) for p in range(2)]
        rstd = [sb(f"rstd{p}", [P, 1]) for p in range(2)]
        neg_half = sb("neg_half", [P, 1])
        eps = sb("eps", [P, 1])
        xn = [sb(f"xn{p}", [P, D]) for p in range(2)]
        xt_hi = [sb(f"xt_hi{u}", [P, KC, TOK], F32R) for u in range(HALF)]
        xt_lo = [sb(f"xt_lo{u}", [P, KC, TOK], F32R) for u in range(HALF)]
        prod = [sb(f"prod{p}", [P, 4, TOK]) for p in range(2)]
        parts = [sb(f"parts{p}", [P, 2, 3, TOK], BF16) for p in range(2)]
        xt_bank = [psum(f"xt_bank{p}", [P, KC, P]) for p in range(2)]
        v_bank = [psum(f"v_bank{p}", [P, D]) for p in range(2)]
        pair_bank = [[psum(f"pair_bank{p}{e}", [P, TOK]) for e in range(2)] for p in range(2)]

        tables_loaded = sem("tables")
        mv_ready, rstd_ready, xn_ready, xt_ready, hi_ready, lo_ready, v_ready, v_copied = tile_counts = [sem(n) for n in (
            "mv_ready", "rstd_ready", "xn_ready", "xt_ready", "hi_ready", "lo_ready", "v_ready", "v_copied")]
        pair_ready, products, rotated, high, rest, middle, low = pair_counts = [sem(n) for n in (
            "pair_ready", "products", "rotated", "high", "rest", "middle", "low")]
        stored = [sem(f"stored{p}") for p in range(2)]
        own_vector, own_pool = sem("own_vector"), sem("own_pool")
        START = 2
        block = ctx.enter_context(nc.Block())
        SLOTS = SUPER * HALF
        PAIRS = [("q", 0), ("q", 1), ("k", 0), ("k", 1)]
        STORES = 6 * 16

        def batches(eng, body, steps=None, per=0):
            with eng.Fori(0, B) as b:
                if steps:
                    steps.enter(b, per)
                body(b)
                if steps:
                    steps.leave(B)

        def tile_of(b, m):
            if isinstance(b, int) or m < SLOTS:
                return b * SLOTS + m
            return (1 - b) * SLOTS + (m - SLOTS)

        def xt_place(m):
            return (m // SUPER) % 2, slice(m % SUPER * P, (m % SUPER + 1) * P)

        @block.sync
        def _(sp):
            for count in tile_counts + pair_counts + stored:
                sp.sem_inc(count, START)
            sp.dma_start(cos[:], g.cos_in).then_inc(tables_loaded, 16)
            sp.dma_start(sin[:], g.sin_in).then_inc(tables_loaded, 16)

            def body(b):
                for n in range(SLOTS):
                    N, p = b * SLOTS + n, n % 2
                    u, (which, half) = n // SUPER, PAIRS[n % SUPER]
                    sp.wait_ge(low, N + (START + 1))
                    rows = g.scratch[which].rearrange("c (h e f) t -> e c h f t", e=2, f=8)
                    for e in range(2):
                        for c in range(3):
                            dst = rows[e, c, half * 16:(half + 1) * 16, :, bass.ds(b * S + u * TOK, TOK)]
                            sp.dma_start(dst, parts[p][:, e, c, :]).then_inc(stored[p], 16)

            batches(sp, body)
            for p in range(2):
                sp.wait_ge(stored[p], B * SLOTS // 2 * STORES + START)

        @block.scalar
        def _(act):
            def round_x(N, m):
                act.wait_ge(xt_ready, N + (START + 1))
                if m % SUPER == 0 and m >= SUPER:
                    act.wait_ge(pair_ready, N + (START - SUPER))
                u, t = xt_place(m)
                nc.scalar.copy(xt_hi[u][:, :, t], xt_bank[m % 2][:]).then_inc(hi_ready, 1)

            def high_and_middle(N, n):
                p = n % 2
                act.wait_ge(rotated, N + (START + 1))
                act.wait_ge(stored[p], (N - n) * (STORES // 2) + (n // 2 * STORES + START))
                nc.scalar.copy(parts[p][:, :, 0, :], prod[p][:, 0:2, :]).then_inc(high, 1)
                act.wait_ge(rest, N + (START + 1))
                nc.scalar.copy(parts[p][:, :, 1, :], prod[p][:, 2:4, :]).then_inc(middle, 1)

            def body(b):
                for n in range(SLOTS):
                    N, p = b * SLOTS + n, n % 2
                    round_x(N + SUPER, n + SUPER)
                    act.wait_ge(v_ready, N + (START + 1))
                    nc.scalar.copy(g.vo[:, N, :], v_bank[p][:]).then_inc(v_copied, 1)
                    if n:
                        high_and_middle(N - 1, n - 1)
                high_and_middle(N, SLOTS - 1)

            for m in range(SUPER):
                round_x(m, m)
            batches(act, body)

        @block.tensor
        def _(pe):
            def turn(N, m):
                pe.wait_ge(xn_ready, N + (START + 1))
                pe.wait_ge(lo_ready, N + (START - 1))
                for c in range(KC):
                    last = nc.tensor.transpose(xt_bank[m % 2][:, c, :], xn[m % 2][:, c * P:(c + 1) * P], g.ident[:])
                last.then_inc(xt_ready, 1)

            def body(b):
                for n in range(SLOTS):
                    N, p = b * SLOTS + n, n % 2
                    u, t = xt_place(n)
                    turn(N + SUPER, n + SUPER)
                    pe.wait_ge(lo_ready, N + (START + 1))
                    pe.wait_ge(v_copied, N + (START - 1))
                    for c in range(KC):
                        nc.tensor.matmul(v_bank[p][:], xt_lo[u][:, c, t], w_hi["v"][:, c, :], start=(c == 0), stop=False)
                        nc.tensor.matmul(v_bank[p][:], xt_hi[u][:, c, t], w_lo["v"][:, c, :], start=False, stop=False)
                        last = nc.tensor.matmul(v_bank[p][:], xt_hi[u][:, c, t], w_hi["v"][:, c, :], start=False, stop=(c == KC - 1))
                    last.then_inc(v_ready, 1)
                    if n % SUPER == 0:
                        pe.wait_ge(lo_ready, N + (START + SUPER))
                    pe.wait_ge(products, N + (START - 1))
                    which, half = PAIRS[n % SUPER]
                    for e in range(2):
                        f = slice((half * 2 + e) * P, (half * 2 + e + 1) * P)
                        for c in range(KC):
                            nc.tensor.matmul(pair_bank[p][e][:], w_lo[which][:, c, f], xt_hi[u][:, c, :], start=(c == 0), stop=False)
                            nc.tensor.matmul(pair_bank[p][e][:], w_hi[which][:, c, f], xt_lo[u][:, c, :], start=False, stop=False)
                            last = nc.tensor.matmul(pair_bank[p][e][:], w_hi[which][:, c, f], xt_hi[u][:, c, :], start=False, stop=(c == KC - 1))
                    last.then_inc(pair_ready, 1)

            for m in range(SUPER):
                turn(m, m)
            batches(pe, body)

        @block.gpsimd
        def _(pool):
            own = Steps(own_pool)
            nc.gpsimd.memset(eps[:], EPS)
            own.then_wait(pool, nc.gpsimd.memset(neg_half[:], -0.5))

            def inverse_deviation(N, m):
                p = m % 2
                pool.wait_ge(mv_ready, N + (START + 1))
                pool.wait_ge(xn_ready, N + (START - 1))
                own.then_wait(pool, nc.gpsimd.tensor_tensor(var_eps[p][:], mean_var[m % 4][:, 1:2], eps[:], ALU.add))
                nc.gpsimd.tensor_tensor(rstd[p][:], var_eps[p][:], neg_half[:], ALU.pow).then_inc(rstd_ready, 1)

            def low_part(N, n):
                p = n % 2
                pool.wait_ge(middle, N + (START + 1))
                nc.gpsimd.tensor_tensor(parts[p][:, :, 2, :], prod[p][:, 2:4, :], parts[p][:, :, 1, :], ALU.subtract).then_inc(low, 1)

            def body(b):
                for n in range(SLOTS):
                    N, p = b * SLOTS + n, n % 2
                    inverse_deviation(N + AHEAD, n + AHEAD)
                    if n:
                        low_part(N - 1, n - 1)
                    pool.wait_ge(products, N + (START + 1))
                    nc.gpsimd.tensor_tensor(prod[p][:, 0, :], prod[p][:, 0, :], prod[p][:, 2, :], ALU.subtract)
                    nc.gpsimd.tensor_tensor(prod[p][:, 1, :], prod[p][:, 1, :], prod[p][:, 3, :], ALU.add).then_inc(rotated, 1)
                low_part(N, SLOTS - 1)

            for m in range(AHEAD):
                inverse_deviation(m, m)
            batches(pool, body, own, SLOTS)

        @block.vector
        def _(dve):
            own = Steps(own_vector)
            def statistics(N, n):
                own.step(nc.vector.bn_stats(stats[n % 4][:], g.x[:, N, :]))

            def mean_and_variance(n):
                nc.vector.bn_aggr(mean_var[n % 4][:], stats[n % 4][:]).then_inc(mv_ready, 1)

            def normalise(N, xi, m):
                dve.wait_ge(rstd_ready, N + (START + 1))
                dve.wait_ge(xt_ready, N + (START - 1))
                nc.vector.tensor_scalar(xn[m % 2][:], g.x[:, xi, :], mean_var[m % 4][:, 0:1], rstd[m % 2][:], ALU.subtract, ALU.mult).then_inc(xn_ready, 1)

            def split(N, m):
                u, t = xt_place(m)
                dve.wait_ge(hi_ready, N + (START + 1))
                nc.vector.tensor_tensor(xt_lo[u][:, :, t], xt_bank[m % 2][:], xt_hi[u][:, :, t].bitcast(F32), ALU.subtract).then_inc(lo_ready, 1)

            def rest_of(N, n):
                p = n % 2
                dve.wait_ge(high, N + (START + 1))
                nc.vector.tensor_tensor(prod[p][:, 2:4, :], prod[p][:, 0:2, :], parts[p][:, :, 0, :], ALU.subtract).then_inc(rest, 1)

            def body(b):
                for n in range(SLOTS):
                    N, p = b * SLOTS + n, n % 2
                    statistics(tile_of(b, n + AHEAD), n + AHEAD)
                    own.wait(dve)
                    m = n + AHEAD - 1
                    normalise(N + (AHEAD - 1), tile_of(b, m), m)
                    mean_and_variance(n + AHEAD)
                    split(N + SUPER, n + SUPER)
                    if n:
                        rest_of(N - 1, n - 1)
                    u = n // SUPER
                    tok = slice(u * TOK, (u + 1) * TOK)
                    dve.wait_ge(pair_ready, N + (START + 1))
                    dve.wait_ge(low, N + (START - 1))
                    even, odd = pair_bank[p]
                    nc.vector.tensor_tensor(prod[p][:, 0, :], even[:], cos[:, tok], ALU.mult)
                    nc.vector.tensor_tensor(prod[p][:, 1, :], even[:], sin[:, tok], ALU.mult)
                    nc.vector.tensor_tensor(prod[p][:, 2, :], odd[:], sin[:, tok], ALU.mult)
                    nc.vector.tensor_tensor(prod[p][:, 3, :], odd[:], cos[:, tok], ALU.mult).then_inc(products, 1)
                rest_of(N, SLOTS - 1)

            for m in range(AHEAD + 1):
                if m < AHEAD:
                    statistics(m, m)
                    own.wait(dve)
                if m:
                    normalise(m - 1, m - 1, m - 1) if m - 1 < AHEAD - 1 else None
                if m < AHEAD:
                    mean_and_variance(m)
                if 2 <= m < SUPER + 2:
                    split(m - 2, m - 2)
            dve.wait_ge(tables_loaded, 32)
            batches(dve, body, own, SLOTS)


def raw_view(g, n, w, c):
    raw = g.vo[:, n * KC + c, :]
    return raw if w == "v" else raw.rearrange("p (a m e) -> p a e m", a=2, e=2)


def split_view(weight, w, c):
    part = weight[:, c, :]
    return part if w == "v" else part.rearrange("p (a e m) -> p a e m", a=2, e=2)


HEADS, HD = 32, 16
GH = 4
GROUPS = B * HEADS // GH
QT = S // P
ROWS = 6 * HD
NEG = -3.0e38


def attention(nc, g):
    NBUF = 3
    NBANK = 3
    with ExitStack() as ctx:
        def sb(name, shape, dt=F32):
            return ctx.enter_context(nc.sbuf_tensor(f"att_{name}", shape, dt))

        def sem(name):
            return ctx.enter_context(nc.semaphore(f"att_{name}"))

        q_rows = [sb(f"q_rows{i}", [P, GH, S], BF16) for i in range(NBUF)]
        k_rows = [sb(f"k_rows{i}", [P, GH, S], BF16) for i in range(NBUF)]
        v_rows = [sb(f"v_rows{i}", [P, QT, GH, 32]) for i in range(NBUF)]
        probs = [sb(f"probs{i}", [P, GH, S]) for i in range(2)]
        o_t = sb("o_t", [P, S])
        part_max = sb("part_max", [P, GH, QT, 2])
        row_max = sb("row_max", [P, GH * QT])
        neg_rest = sb("neg_rest", [P, 2, GH * QT])
        neg_parts = sb("neg_parts", [P, 3, GH * QT], BF16)
        neg_turned = sb("neg_turned", [3 * GH * QT, P], BF16)
        inv_sum = sb("inv_sum", [P, 2, QT // 2 * GH])
        ident_b = sb("ident_b", [P, P], BF16)
        causal = sb("causal", [P, P], BF16)
        behind = sb("behind", [P, D])
        scores = [ctx.enter_context(nc.psum_tensor(f"att_scores{i}", [P, D], F32)) for i in range(NBANK)]
        ring = [ctx.enter_context(nc.psum_tensor(f"att_ring{i}", [P, D], F32)) for i in range(NBANK)]
        o_bank = [ctx.enter_context(nc.psum_tensor(f"att_o{i}", [P, D], F32)) for i in range(2)]

        ready, wo_loaded, wo_hi_ready, wo_split = (sem(n) for n in ("constants", "wo_loaded", "wo_hi_ready", "wo_split"))
        rows_loaded = [sem(f"rows_loaded{i}") for i in range(NBUF)]
        max_loaded = [sem(f"max_loaded{i}") for i in range(NBUF)]
        scored, exped, valued, v_ready = (sem(n) for n in ("scored", "exped", "valued", "v_ready"))
        o_copied, ring_ready, ring_done, neg_ready = (sem(n) for n in ("o_copied", "ring_ready", "ring_done", "neg_ready"))
        own_vector, pool_ready, diagonals = sem("own_vector"), sem("pool_ready"), sem("diagonals")
        block = ctx.enter_context(nc.Block())

        UNITS = [(h, i, half) for h in range(GH) for i in range(QT) for half in range(1 + (i >= QT // 2))]
        NU = len(UNITS)
        HU = NU // 2
        KEYED = [(j, h, half) for j in range(QT) for h in range(GH) for half in range(j // (QT // 2), 2)]
        NK = len(KEYED)
        TURN_LATE = 3
        MAX_FIRST = 3
        ROUND = NU + 3
        assert NK % NBANK == 0 and ROUND % NBANK == 0 and HU % NBANK == 0
        LOADS = 12 * 16

        def keyed_until(j):
            return sum(1 for u in KEYED if u[0] <= j)

        def queries(j, half):
            return max(j * P, half * D), (half + 1) * D

        def keys(i, half):
            return min((i + 1) * P - half * D, D)

        def ring_base(G):
            if is_first(G):
                return NU + 1
            return G * ROUND + (NU - 1 + HU - (HU if is_last(G) else 0))

        def ring_plan(G):
            last = GROUPS - 1
            outputs = [("o", 0), ("o", 1)] if not is_first(G) else []
            plan = []
            if not is_last(G):
                plan += [("max", u, 1) for u in UNITS[0 if is_first(G) else HU:]]
                after_next = UNITS[:HU] if not isinstance(G, int) or G + 2 <= last else []
                plan += [("max", u, 2) for u in after_next[:TURN_LATE]] + [("turn",)]
                plan += [("max", u, 2) for u in after_next[TURN_LATE:]]
            return plan[:MAX_FIRST] + outputs + plan[MAX_FIRST:]

        def turned(G):
            return ring_base(G) + ring_plan(G).index(("turn",)) + 1

        def outputs_turned(G):
            return ring_base(G) + (0 if is_last(G) else MAX_FIRST) + 2

        def ring_bank(G, n):
            return ring[((ring_base(0) if is_first(G) else ring_base(1)) + n) % NBANK]

        LATENCY, PER_UNIT, O_WORK, O_AFTER, TURN_AFTER = 160, 70, 700, 1000, 800

        def woven(G):
            columns = 1 / 2.4
            main = []
            for n, (j, h, half) in enumerate(KEYED):
                a, z = queries(j, half)
                main.append((("score", n), ((z - a) + P * (a == j * P)) * columns))
                if j >= 1 and half == 1:
                    if h == 1 and j - 1 < QT // 2:
                        main.append((("value", j - 1, 0), 4 * (D - (j - 1) * P) * columns))
                    if h == GH - 1:
                        a, z = queries(j - 1, 1)
                        main.append((("value", j - 1, 1), 4 * (z - a) * columns))
            main.append((("value", QT - 1, 1), 4 * P * columns))
            plan = list(enumerate(ring_plan(G)))
            out, clock = [], 0.0
            exp_done, ring_free, vector_free = [], [0.0] * NBANK, 0.0
            scalar_free = 800.0 if not is_first(G) else 0.0
            while main or plan:
                main_at = ring_at = float("inf")
                if main:
                    what, cost = main[0]
                    if what[0] == "score":
                        main_at = exp_done[what[1] - NBANK] + LATENCY if what[1] >= NBANK else 0.0
                    else:
                        main_at = exp_done[keyed_until(what[1]) - 1] + LATENCY
                if plan:
                    n, unit = plan[0]
                    ring_at = ring_free[n % NBANK] + LATENCY
                    if unit[0] == "o":
                        ring_at = max(ring_at, O_AFTER)
                    elif unit[0] == "turn":
                        ring_at = max(ring_at, vector_free + TURN_AFTER)
                if ring_at <= max(clock, main_at):
                    plan.pop(0)
                    out.append(("ring", n, unit))
                    if unit[0] == "max":
                        w = keys(unit[1][1], unit[1][2])
                        taken, work = w * columns, 1.04 * w + PER_UNIT
                    elif unit[0] == "o":
                        taken, work = D * columns, O_WORK
                    else:
                        taken, work = P * columns, 300
                    clock = max(clock, ring_at) + taken
                    vector_free = max(vector_free, clock + LATENCY) + work
                    ring_free[n % NBANK] = vector_free
                else:
                    main.pop(0)
                    out.append(what)
                    clock = max(clock, main_at) + cost
                    if what[0] == "score":
                        j, h, half = KEYED[what[1]]
                        a, z = queries(j, half)
                        scalar_free = max(scalar_free, clock + LATENCY) + 0.83 * (z - a) + 52
                        exp_done.append(scalar_free)
            return out

        def turns(eng, turn, steps=None, per=0):
            turn(0, 0, 0)
            rounds = (GROUPS - 4) // NBUF
            with eng.Fori(0, rounds) as i:
                if steps:
                    steps.enter(i, per * NBUF)
                for k in range(NBUF):
                    turn(i * NBUF + (1 + k), (1 + k) % NBUF, i + (1 + k) // NBUF)
                if steps:
                    steps.leave(rounds)
            for G in range(1 + rounds * NBUF, GROUPS):
                turn(G, G % NBUF, G // NBUF)

        def is_last(G):
            return isinstance(G, int) and G == GROUPS - 1

        def is_first(G):
            return isinstance(G, int) and G == 0

        def after(buf, cycle):
            return (buf + 1) % NBUF, cycle + (buf + 1) // NBUF

        def load_rows(eng, which, G, buf):
            head, tok = (G % 8) * (GH * HD), (G // 8) * S
            rows, parts = {"q": (q_rows, (0, 1, 2, 0, 1, 0)), "k": (k_rows, (0, 0, 0, 1, 1, 2))}[which]
            for r, part in enumerate(parts):
                src = g.scratch[which][part, bass.ds(head, GH * HD), bass.ds(tok, S)]
                eng.dma_start(rows[buf][r * HD:(r + 1) * HD, :, :], src.rearrange("(h r) t -> r h t", h=GH)).then_inc(rows_loaded[buf], 16)

        wo = probs[1][:, 0:KC, 0:D]

        @block.sync
        def _(sp):
            def load(G, buf):
                load_rows(sp, "q", G, buf)
                load_rows(sp, "k", G, buf)

            def load_max(buf):
                sp.dma_start(q_rows[buf][ROWS:ROWS + 3, :, :].rearrange("c h (i t) -> c (h i) t", t=P), neg_turned[:]).then_inc(max_loaded[buf], 16)

            def turn(G, buf, cycle):
                if not isinstance(G, int) or G + 2 < GROUPS:
                    at_least(sp, scored, G * NK)
                    load(G + 2, (buf + 2) % NBUF)
                if not is_last(G):
                    sp.wait_ge(ring_done, turned(G))
                    load_max(after(buf, cycle)[0])

            load_rows(sp, "q", 0, 0)
            sp.wait_ge(rows_loaded[0], LOADS)
            sp.dma_start(wo, g.wo_in).then_inc(wo_loaded, 16)
            load(1, 1)
            sp.wait_ge(ring_done, NU + 1)
            load_max(0)
            turns(sp, turn)
            sp.wait_ge(max_loaded[(GROUPS - 1) % NBUF], 16 * (GROUPS // NBUF + 1))

        @block.tensor
        def _(pe):
            def max_unit(u, base, n, bank, buf):
                h, i, half = u
                w = keys(i, half)
                at_least(pe, ring_done, base + n - NBANK + 1)
                nc.tensor.matmul(bank[:, 0:w], q_rows[buf][0:ROWS, h, i * P:(i + 1) * P],
                                 k_rows[buf][0:ROWS, h, half * D:half * D + w], start=True, stop=True).then_inc(ring_ready, 1)

            def turn_max(base, n, bank, count):
                pe.wait_ge(neg_ready, count)
                at_least(pe, ring_done, base + n - NBANK + 1)
                out = bank[0:3 * GH * QT, 0:P // 2].bitcast(BF16)
                nc.tensor.transpose(out, neg_parts[:].rearrange("p c n -> p (c n)"), ident_b[:]).then_inc(ring_ready, 1)

            def turn_o(base, n, bank, half, G1):
                pe.wait_ge(o_copied, G1 * 2 + half + 1)
                at_least(pe, ring_done, base + n - NBANK + 1)
                for i in range(QT // 2):
                    c = (half * (QT // 2) + i) * P
                    last = nc.tensor.transpose(bank[:, i * P:(i + 1) * P], o_t[:, c:c + P], g.ident[:])
                last.then_inc(ring_ready, 1)

            def score(G, buf, n):
                j, h, half = KEYED[n]
                a, z = queries(j, half)
                bank = scores[n % NBANK]
                at_least(pe, exped, G * NK + n - NBANK + 1)
                last = nc.tensor.matmul(bank[:, 0:z - a], k_rows[buf][0:ROWS + 3, h, j * P:(j + 1) * P],
                                        q_rows[buf][0:ROWS + 3, h, a:z], start=True, stop=a != j * P)
                if a == j * P:
                    last = nc.tensor.matmul(bank[:, 0:P], causal[:], ident_b[:], start=False, stop=True)
                last.then_inc(scored, 1)

            def value(G, buf, j, half):
                pe.wait_ge(exped, G * NK + keyed_until(j))
                if j == 0:
                    pe.wait_ge(v_ready, G + 1)
                    at_least(pe, o_copied, G * 2)
                a, z = queries(j, half)
                for h in range(GH):
                    last = nc.tensor.matmul(o_bank[half][32 * h:32 * h + 32, a - half * D:z - half * D],
                                            v_rows[buf][:, j, h, :], probs[j % 2][:, h, a:z],
                                            start=(j == 0), stop=(j == (QT // 2 - 1 if half == 0 else QT - 1)),
                                            skip_group_check=True)
                if half == 1:
                    last.then_inc(valued, 1)

            def turn(G, buf, cycle):
                base = ring_base(G)
                pe.wait_ge(max_loaded[buf], cycle * 16 + 16)
                for what in woven(G):
                    if what[0] == "score":
                        score(G, buf, what[1])
                    elif what[0] == "value":
                        value(G, buf, what[1], what[2])
                    else:
                        n, unit = what[1:]
                        bank = ring_bank(G, n)
                        if unit[0] == "o":
                            turn_o(base, n, bank, unit[1], G - 1)
                        elif unit[0] == "turn":
                            turn_max(base, n, bank, G + 2)
                        else:
                            k = unit[2]
                            if unit[1] == UNITS[0]:
                                pe.wait_ge(rows_loaded[(buf + k) % NBUF], (cycle + (buf + k) // NBUF) * LOADS + LOADS)
                            max_unit(unit[1], base, n, bank, (buf + k) % NBUF)

            pe.wait_ge(ready, 1)
            pe.wait_ge(rows_loaded[0], LOADS)
            for n, u in enumerate(UNITS):
                max_unit(u, 0, n, ring[n % NBANK], 0)
            turn_max(0, NU, ring[NU % NBANK], 1)
            pe.wait_ge(pool_ready, 3 * NBUF)
            turns(pe, turn)
            for n in (2, 3):
                turn_o(ring_base(GROUPS - 1), n, ring_bank(1, n), n - 2, GROUPS - 1)

        @block.scalar
        def _(act):
            def copy_o(G1, half):
                act.wait_ge(valued, G1 * QT + (half + 1) * (QT // 2))
                if half == 0 and not is_first(G1):
                    act.wait_ge(ring_ready, outputs_turned(G1))
                nc.scalar.copy(o_t[:, half * D:(half + 1) * D], o_bank[half][:]).then_inc(o_copied, 1)

            def turn(G, buf, cycle):
                for n, (j, h, half) in enumerate(KEYED):
                    if n == 0 and not is_first(G):
                        copy_o(G - 1, 1)
                    if (j, h) == (QT - 2, 0):
                        copy_o(G, 0)
                    a, z = queries(j, half)
                    act.wait_ge(scored, G * NK + n + 1)
                    at_least(act, valued, G * QT + j - 1)
                    nc.scalar.activation(probs[j % 2][:, h, a:z], scores[n % NBANK][:, 0:z - a], ACT.Exp,
                                         scale=float(HD) ** -0.5).then_inc(exped, 1)

            load_rows(act, "k", 0, 0)
            act.wait_ge(wo_loaded, 16)
            nc.scalar.copy(g.w_hi[OUT_PROJ][:], wo).then_inc(wo_hi_ready, 1)
            act.wait_ge(wo_split, 1)
            turns(act, turn)
            copy_o(GROUPS - 1, 1)

        @block.gpsimd
        def _(pool):
            for i in range(NBUF):
                nc.gpsimd.memset(v_rows[i][:, :, :, HD:32], 0.0).then_inc(pool_ready, 1)
            pool.wait_ge(pool_ready, NBUF)
            for i in range(NBUF):
                nc.gpsimd.memset(v_rows[i][:, :, :, HD:HD + 1], 1.0).then_inc(pool_ready, 1)
            for i in range(NBUF):
                pool.wait_ge(pool_ready, 2 * NBUF + i)
                nc.gpsimd.memset(k_rows[i][ROWS:ROWS + 3, :, :], 1.0).then_inc(pool_ready, 1)

            def take_v(G, buf):
                src = g.vo[:, bass.ds((G // 8) * QT, QT), bass.ds((G % 8) * (GH * HD), GH * HD)]
                nc.gpsimd.tensor_copy(v_rows[buf][:, :, :, 0:HD], src.rearrange("p t (h d) -> p t h d", h=GH)).then_inc(v_ready, 1)

            def turn(G, buf, cycle):
                if not is_last(G):
                    at_least(pool, valued, G * QT)
                    take_v(G + 1, (buf + 1) % NBUF)

            pool.wait_ge(pool_ready, 3 * NBUF)
            take_v(0, 0)
            pool.wait_ge(wo_hi_ready, 1)
            nc.gpsimd.tensor_tensor(g.w_lo[OUT_PROJ][:], wo, g.w_hi[OUT_PROJ][:].bitcast(F32), ALU.subtract).then_inc(wo_split, 1)
            turns(pool, turn)

        @block.vector
        def _(dve):
            own = Steps(own_vector)
            own.then_wait(dve, nc.vector.tensor_copy(ident_b[:], g.ident[:]))
            nc.vector.tensor_copy(causal[:], g.causal_in[:]).then_inc(ready, 1)
            own.step(nc.vector.memset(behind[:, 0:D - P], 0.0))
            own.then_wait(dve, nc.vector.tensor_copy(behind[:, D - P:D], g.causal_in[:]))
            own.then_wait(dve, nc.vector.memset(part_max[:], NEG))

            def maximum(u, base, n, bank):
                h, i, half = u
                w = keys(i, half)
                dve.wait_ge(ring_ready, base + n + 1)
                if (i * P) // D == half:
                    dve.sem_inc(diagonals, 1)
                    nc.vector.tensor_tensor_reduce(out=bank[:, 0:w], in0=bank[:, 0:w], in1=behind[:, D - w:D], scale=1.0,
                                                   scalar=NEG, op0=ALU.add, op1=ALU.max,
                                                   accum_out=part_max[:, h, i, half:half + 1]).then_inc(ring_done, 1)
                else:
                    nc.vector.tensor_reduce(part_max[:, h, i, half:half + 1], bank[:, 0:w], AX.X, ALU.max).then_inc(ring_done, 1)

            def negate_step(k, base, n):
                if k == 0:
                    dve.wait_ge(ring_done, base + n)
                    own.then_wait(dve, nc.vector.tensor_reduce(row_max[:], part_max[:].rearrange("p h i a -> p (h i) a"), AX.X, ALU.max))
                    own.step(nc.vector.tensor_scalar(neg_parts[:, 0, :], row_max[:], -1.0, None, ALU.mult))
                elif k == 1:
                    own.wait(dve)
                    own.step(nc.vector.scalar_tensor_tensor(neg_rest[:, 0, :], row_max[:], -1.0, neg_parts[:, 0, :], ALU.mult, ALU.subtract))
                elif k == 2:
                    own.wait(dve)
                    own.step(nc.vector.tensor_copy(neg_parts[:, 1, :], neg_rest[:, 0, :]))
                else:
                    own.wait(dve)
                    nc.vector.tensor_tensor(neg_parts[:, 2, :], neg_rest[:, 0, :], neg_parts[:, 1, :], ALU.subtract).then_inc(neg_ready, 1)

            def take_turned(base, n, bank):
                dve.wait_ge(ring_ready, base + n + 1)
                nc.vector.tensor_copy(neg_turned[:], bank[0:3 * GH * QT, 0:P // 2].bitcast(BF16)).then_inc(ring_done, 1)

            def outputs(base, n, bank, half, G1):
                dve.wait_ge(ring_ready, base + n + 1)
                o = bank[:].rearrange("p (i h d) -> p i h d", h=GH, d=32)
                inv = inv_sum[:, half, :].rearrange("p (i h) -> p i h", h=GH)
                own.then_wait(dve, nc.vector.reciprocal(inv, o[:, :, :, HD]))
                dst = g.vo[:, bass.ds((G1 // 8) * QT + half * (QT // 2), QT // 2), bass.ds((G1 % 8) * (GH * HD), GH * HD)]
                nc.vector.tensor_tensor(dst.rearrange("p t (h d) -> p t h d", h=GH), o[:, :, :, 0:HD],
                                        inv.unsqueeze(3).broadcast_to((P, QT // 2, GH, HD)), ALU.mult).then_inc(ring_done, 1)

            def turn(G, buf, cycle):
                base = ring_base(G)
                dve.wait_ge(max_loaded[buf], cycle * 16 + 16)
                plan = ring_plan(G)
                complete = sum(1 for what in plan if what[0] == "o" or what[0] == "max" and what[2] == 1)
                for n, what in enumerate(plan):
                    if what[0] == "max":
                        if 0 <= n - complete < TURN_LATE:
                            negate_step(n - complete, base, n)
                        maximum(what[1], base, n, ring_bank(G, n))
                    elif what[0] == "turn":
                        for k in range(n - complete, 4):
                            negate_step(k, base, n)
                        take_turned(base, n, ring_bank(G, n))
                    else:
                        outputs(base, n, ring_bank(G, n), what[1], G - 1)

            for n, u in enumerate(UNITS):
                maximum(u, 0, n, ring[n % NBANK])
            for k in range(4):
                negate_step(k, 0, NU)
            take_turned(0, NU, ring[NU % NBANK])
            turns(dve, turn, own, 6)
            for n in (2, 3):
                outputs(ring_base(GROUPS - 1), n, ring_bank(1, n), n - 2, GROUPS - 1)


class Shared:
    pass


def program(nc, ins, out):
    with ExitStack() as ctx:
        def sb(name, shape, dt=F32, at=ctx):
            return at.enter_context(nc.sbuf_tensor(name, shape, dt))

        g = Shared()
        g.x = sb("x", [P, TILES, D])
        g.vo = sb("v_then_o", [P, TILES, D])
        g.ident = sb("identity", [P, P])
        g.causal_in = sb("causal_in", [P, P])
        g.w_hi = {BIN_FFN: sb("w_hi_bin", [P, KC, D], F32R)}
        g.w_lo = {BIN_FFN: sb("w_lo_bin", [P, KC, D], F32R)}
        g.scratch = {w: nc.dram_tensor(f"{w}_parts", (3, D, B * S), BF16, kind="Internal").ap() for w in "qk"}
        g.qkv_loaded = ctx.enter_context(nc.semaphore("qkv_loaded"))
        g.x_loaded = [ctx.enter_context(nc.semaphore(f"x_loaded{i}")) for i in range(TILES // 4)]
        g.cos_in, g.sin_in = ins["cos"], ins["sin"]
        g.qkv_in = [ins[w].rearrange("(c p) n -> p c n", p=P) for w in ("L1_attn_wq", "L1_attn_wk", "L1_attn_wv")]
        g.qkv_hi_ready = ctx.enter_context(nc.semaphore("qkv_weights_hi"))
        with ExitStack() as until_attention:
            g.qkv_hi = {w: sb(f"w_hi_{w}", [P, KC, D], F32R, at=until_attention) for w in "qkv"}
            g.qkv_lo = {w: sb(f"w_lo_{w}", [P, KC, D], F32R, at=until_attention) for w in "qkv"}
            with ExitStack() as first:
                g.iota = sb("expert_numbers", [P, E], at=first)
                g.bias = {LORA_FFN: sb("bias_ffn", [P, D], at=first), SPARSE: sb("bias_sparse", [P, D], at=first)}
                for k in (LORA_FFN, SPARSE):
                    g.w_hi[k] = sb(f"w_hi{k}", [P, KC, D], F32R, at=first)
                    g.w_lo[k] = sb(f"w_lo{k}", [P, KC, D], F32R, at=first)
                g.ra = sb("router_and_down", [P, KC, E + ER], at=first)
                g.up_hi = sb("up_hi", [P, D], F32R, at=first)
                g.up_lo = sb("up_lo", [P, D], F32R, at=first)
                prepare_weights(nc, ins, g)
                dense_stages(nc, g, BEFORE, "ffn")
            project_qkv(nc, g)
        g.w_hi[OUT_PROJ] = sb("w_hi_out", [P, KC, D], F32R)
        g.w_lo[OUT_PROJ] = sb("w_lo_out", [P, KC, D], F32R)
        g.wo_in = ins["L1_attn_wo"].rearrange("(c p) n -> p c n", p=P)
        attention(nc, g)
        dense_stages(nc, g, (OUT_PROJ, BIN_FFN), "end", out)


def rotation_tables():
    inv = 1.0 / 10000.0 ** (np.arange(0, HD, 2)[:HD // 2].astype(np.float32) / HD)
    f = np.outer(np.arange(S), inv).astype(np.float32)
    return (np.ascontiguousarray(np.tile(t.T, (P // (HD // 2), 1))) for t in (np.cos(f), np.sin(f)))


def shape_constants():
    cos, sin = rotation_tables()
    return {
        "ident": np.eye(P, dtype=np.float32),
        "same_block": np.kron(np.eye(P // BLK, dtype=np.float32), np.ones((BLK, BLK), np.float32)),
        "iota": np.arange(E, dtype=np.float32),
        "causal": np.triu(np.full((P, P), NEG, np.float32), 1),
        "cos": cos,
        "sin": sin,
    }


_INS = ["L0_attn_data", "L0_attn_mask", "L0_attn_weight", "L0_attn_bias", "L0_ffn_W_base", "L0_ffn_b_base",
        "L0_ffn_W_router", "L0_ffn_A", "L0_ffn_B", "L1_attn_wq", "L1_attn_wk", "L1_attn_wv", "L1_attn_wo",
        "L1_ffn_weight", "L1_ffn_wscale", "L1_ffn_wbias"]


def kernel(**inputs):
    import concourse.bacc as bacc
    from concourse.bass_utils import run_bass_kernel_spmd

    nc = bacc.Bacc("TRN2", target_bir_lowering=False, num_devices=1)
    arrays = {name: np.ascontiguousarray(inputs[name]) for name in _INS}
    arrays.update(shape_constants())
    ins = {name: nc.dram_tensor(f"in_{name}", a.shape, mybir.dt.from_np(a.dtype), kind="ExternalInput").ap()
           for name, a in arrays.items()}
    out = nc.dram_tensor("out", (B, S, D), F32, kind="ExternalOutput").ap()
    program(nc, ins, out)
    result = run_bass_kernel_spmd(nc, [{f"in_{name}": a for name, a in arrays.items()}], core_ids=[0])
    return result.results[0]["out"]
```
